# Optimizing a Trainium2 kernel written in Bass

```python
import numpy as np
import jax
import jax.numpy as jnp

def _softmax(x, axis=-1):
    return jax.nn.softmax(x, axis=axis)

def _gelu(x):
    return jax.nn.gelu(x, approximate=True)

def _silu(x):
    return jax.nn.silu(x)

def _sigmoid(x):
    return jax.nn.sigmoid(x)

def _layernorm(x, axis=-1, eps=1e-05):
    m = jnp.mean(x, axis=axis, keepdims=True)
    v = jnp.var(x, axis=axis, keepdims=True)
    return (x - m) / jnp.sqrt(v + eps)

def _scatter_add(tgt, idx, src, axis=0):
    return tgt.at[idx].add(src)

def _segment_sum(src, seg, n):
    return jax.ops.segment_sum(src, seg, n)
kernel_name = 'mk_flamingo_gated_d1_seqx_r4_251a6f'

def setup_inputs(seed: int=0):
    np.random.seed(seed)
    _w = jnp.asarray

    def _rec_inputs():
        import jax
        import jax.numpy as jnp
        _rk = jax.random.key(seed)
        x = -0.0002928 + 1 * jax.random.normal(jax.random.fold_in(_rk, 1), (8, 512, 256), jnp.float32)
        _lenS = 512 - jax.random.randint(jax.random.fold_in(_rk, 7), (8,), 0, max(1, 512 // 4) + 1, jnp.int32)
        _lenS2 = 512 - jax.random.randint(jax.random.fold_in(_rk, 8), (8,), 0, max(1, 512 // 4) + 1, jnp.int32)
        _ctx_1024P = jax.random.normal(jax.random.fold_in(_rk, 11), (8, 16, 256), jnp.float32)
        _ctx_1024c = jax.random.dirichlet(jax.random.fold_in(_rk, 511), 0.3 * jnp.ones((16,), jnp.float32), (8, 512))
        _ctx_1024t = jnp.einsum('bsk,bkd->bsd', _ctx_1024c, _ctx_1024P)
        _ctx_1024t = _ctx_1024t * jax.lax.rsqrt(jnp.mean(jnp.square(_ctx_1024t)) + 1e-12) * 0.953939
        ctx_1024 = -1.39393e-06 + 0.999914 * (_ctx_1024t + 0.3 * jax.random.normal(jax.random.fold_in(_rk, 611), (8, 512, 256), jnp.float32))
        _validS = jnp.arange(512)[None, :] < _lenS[:, None]
        _validS2 = jnp.arange(512)[None, :] < _lenS2[:, None]
        _causal = jnp.tril(jnp.ones((512, 512), dtype=bool))
        mask_Bx1x1x4096_ff0 = jnp.where(jnp.ones((8, 1, 1, 1024), dtype=bool), 0.0, -1000000000.0).astype(jnp.float32)
        _g = jax.random.normal(jax.random.fold_in(_rk, 9001), (2, 1), jnp.float32)
        _g = jnp.sign(_g) * jnp.maximum(jnp.abs(_g), 1.0) + (_g == 0) * 1.0
        g_xattn = _g[0]
        g_ffn = _g[1]
        return (x, ctx_1024, mask_Bx1x1x4096_ff0, g_xattn, g_ffn)
    x, ctx_1024, mask_Bx1x1x4096_ff0, g_xattn, g_ffn = _rec_inputs()

    def _L0_xattn_setup():
        import jax, jax.numpy as jnp
        import numpy as np
        B, SQ, SE, H, NH = (2, 512, 512, 256, 16)
        HD = H // NH

        def _split_heads(x):
            b, s, _ = x.shape
            return x.reshape(b, s, NH, HD).transpose(0, 2, 1, 3)
        key = jax.random.key(seed)
        ks = jax.random.split(key, 8)
        s = 1.0 / np.sqrt(H)
        return {'hidden_states': jax.random.normal(ks[0], (B, SQ, H), jnp.float32), 'encoder_hidden_states': jax.random.normal(ks[1], (B, SE, H), jnp.float32), 'attention_mask': jnp.zeros((B, 1, 1, SQ + SE), jnp.float32), 'Wq': jax.random.normal(ks[2], (H, H), jnp.float32) * s, 'bq': jnp.zeros((H,), jnp.float32), 'Wk': jax.random.normal(ks[3], (H, H), jnp.float32) * s, 'bk': jnp.zeros((H,), jnp.float32), 'Wv': jax.random.normal(ks[4], (H, H), jnp.float32) * s, 'bv': jnp.zeros((H,), jnp.float32)}
    _L0_xattn_all = _L0_xattn_setup()
    _L0_xattn_in = {k: v for k, v in _L0_xattn_all.items() if k in ('Wq', 'bq', 'Wk', 'bk', 'Wv', 'bv')}
    del _L0_xattn_all

    def _L0_ffn_setup():
        import jax, jax.numpy as jnp
        import numpy as np
        E = 8
        K = 2
        D = 256
        F = 1024
        EPS = 1e-05

        def _layernorm(h, g, b):
            mu = h.mean(axis=-1, keepdims=True)
            var = ((h - mu) ** 2).mean(axis=-1, keepdims=True)
            return (h - mu) * jax.lax.rsqrt(var + EPS) * g[:, None, :] + b[:, None, :]
        key = jax.random.key(seed)
        ks = jax.random.split(key, 8)
        B, S = (2, 512)
        x = jax.random.normal(ks[0], (B, S, D), dtype=jnp.float32)
        Wr = jax.random.normal(ks[1], (D, E), dtype=jnp.float32) / np.sqrt(D)
        br = jnp.zeros((E,), dtype=jnp.float32)
        W1 = jax.random.normal(ks[2], (E, D, F), dtype=jnp.float32) / np.sqrt(D)
        b1 = jnp.zeros((E, F), dtype=jnp.float32)
        g1 = jnp.ones((E, F), dtype=jnp.float32)
        be1 = jnp.zeros((E, F), dtype=jnp.float32)
        W2 = jax.random.normal(ks[3], (E, F, D), dtype=jnp.float32) / np.sqrt(F)
        b2 = jnp.zeros((E, D), dtype=jnp.float32)
        g2 = jnp.ones((E, D), dtype=jnp.float32)
        be2 = jnp.zeros((E, D), dtype=jnp.float32)
        return {'x': x, 'Wr': Wr, 'br': br, 'W1': W1, 'b1': b1, 'g1': g1, 'be1': be1, 'W2': W2, 'b2': b2, 'g2': g2, 'be2': be2}
    _L0_ffn_all = _L0_ffn_setup()
    _L0_ffn_in = {k: v for k, v in _L0_ffn_all.items() if k in ('Wr', 'br', 'W1', 'b1', 'g1', 'be1', 'W2', 'b2', 'g2', 'be2')}
    del _L0_ffn_all
    return {'x': x, 'ctx_1024': ctx_1024, 'mask_Bx1x1x4096_ff0': mask_Bx1x1x4096_ff0, 'g_xattn': g_xattn, 'g_ffn': g_ffn, 'L0_xattn_Wq': _L0_xattn_in['Wq'], 'L0_xattn_bq': _L0_xattn_in['bq'], 'L0_xattn_Wk': _L0_xattn_in['Wk'], 'L0_xattn_bk': _L0_xattn_in['bk'], 'L0_xattn_Wv': _L0_xattn_in['Wv'], 'L0_xattn_bv': _L0_xattn_in['bv'], 'L0_ffn_Wr': _L0_ffn_in['Wr'], 'L0_ffn_br': _L0_ffn_in['br'], 'L0_ffn_W1': _L0_ffn_in['W1'], 'L0_ffn_b1': _L0_ffn_in['b1'], 'L0_ffn_g1': _L0_ffn_in['g1'], 'L0_ffn_be1': _L0_ffn_in['be1'], 'L0_ffn_W2': _L0_ffn_in['W2'], 'L0_ffn_b2': _L0_ffn_in['b2'], 'L0_ffn_g2': _L0_ffn_in['g2'], 'L0_ffn_be2': _L0_ffn_in['be2']}

def reference(x, ctx_1024, mask_Bx1x1x4096_ff0, g_xattn, g_ffn, L0_xattn_Wq, L0_xattn_bq, L0_xattn_Wk, L0_xattn_bk, L0_xattn_Wv, L0_xattn_bv, L0_ffn_Wr, L0_ffn_br, L0_ffn_W1, L0_ffn_b1, L0_ffn_g1, L0_ffn_be1, L0_ffn_W2, L0_ffn_b2, L0_ffn_g2, L0_ffn_be2):
    import jax
    import jax.numpy as jnp

    def _L0_xattn_ref(hidden_states, encoder_hidden_states, attention_mask, Wq, bq, Wk, bk, Wv, bv):
        import jax, jax.numpy as jnp
        import numpy as np
        B, SQ, SE, H, NH = (2, 512, 512, 256, 16)
        HD = H // NH

        def _split_heads(x):
            b, s, _ = x.shape
            return x.reshape(b, s, NH, HD).transpose(0, 2, 1, 3)
        all_hs = jnp.concatenate([hidden_states, encoder_hidden_states], axis=1)
        q = _split_heads(hidden_states @ Wq + bq)
        k = _split_heads(all_hs @ Wk + bk)
        v = _split_heads(all_hs @ Wv + bv)
        scores = jnp.einsum('bhqd,bhkd->bhqk', q, k) / jnp.sqrt(jnp.float32(HD))
        scores = scores + attention_mask
        probs = jax.nn.softmax(scores, axis=-1)
        ctx = jnp.einsum('bhqk,bhkd->bhqd', probs, v)
        ctx = ctx.transpose(0, 2, 1, 3).reshape(hidden_states.shape[0], hidden_states.shape[1], H)
        return ctx

    def _L0_ffn_ref(x, Wr, br, W1, b1, g1, be1, W2, b2, g2, be2):
        import jax, jax.numpy as jnp
        import numpy as np
        E = 8
        K = 2
        D = 256
        F = 1024
        EPS = 1e-05

        def _layernorm(h, g, b):
            mu = h.mean(axis=-1, keepdims=True)
            var = ((h - mu) ** 2).mean(axis=-1, keepdims=True)
            return (h - mu) * jax.lax.rsqrt(var + EPS) * g[:, None, :] + b[:, None, :]
        B, S, _ = x.shape
        xt = x.reshape(-1, D)
        logits = xt @ Wr + br
        p = jax.nn.softmax(logits, axis=-1)
        probs, idx = jax.lax.top_k(p, K)
        probs = probs / probs.sum(axis=-1, keepdims=True)
        h = jnp.einsum('td,edf->etf', xt, W1) + b1[:, None, :]
        h = _layernorm(jax.nn.relu(h), g1, be1)
        y = jnp.einsum('etf,efd->etd', h, W2) + b2[:, None, :]
        y = _layernorm(jax.nn.relu(y), g2, be2)
        gate = (jax.nn.one_hot(idx, E, dtype=x.dtype) * probs[..., None]).sum(axis=1)
        out = jnp.einsum('te,etd->td', gate, y)
        return out.reshape(B, S, D)
    x = x + jnp.tanh(g_xattn[0]) * _L0_xattn_ref(_layernorm(x, axis=-1), ctx_1024, mask_Bx1x1x4096_ff0, L0_xattn_Wq, L0_xattn_bq, L0_xattn_Wk, L0_xattn_bk, L0_xattn_Wv, L0_xattn_bv)
    x = x + jnp.tanh(g_ffn[0]) * _L0_ffn_ref(_layernorm(x, axis=-1), L0_ffn_Wr, L0_ffn_br, L0_ffn_W1, L0_ffn_b1, L0_ffn_g1, L0_ffn_be1, L0_ffn_W2, L0_ffn_b2, L0_ffn_g2, L0_ffn_be2)
    return x

_drawn_inputs = setup_inputs


def setup_inputs(seed=0):
    import zlib

    import numpy as np

    out = dict(_drawn_inputs(seed))
    spreads = {'L0_xattn_bq': (0.0, 0.1),
     'L0_xattn_bk': (0.0, 0.1),
     'L0_xattn_bv': (0.0, 0.1),
     'L0_ffn_br': (0.0, 0.1),
     'L0_ffn_b1': (0.0, 0.1),
     'L0_ffn_g1': (1.0, 0.2),
     'L0_ffn_be1': (0.0, 0.1),
     'L0_ffn_b2': (0.0, 0.1),
     'L0_ffn_g2': (1.0, 0.2),
     'L0_ffn_be2': (0.0, 0.1)}
    factors = {}
    for name, (base, spread) in spreads.items():
        noise = np.random.default_rng([zlib.crc32(name.encode()), seed]).standard_normal(out[name].shape)
        drawn = base * np.exp(spread * noise) if base else spread * noise
        out[name] = jnp.asarray(drawn.astype(out[name].dtype))
    for name, factor in factors.items():
        out[name] = (out[name] * factor).astype(out[name].dtype)
    return out
```

```python
from contextlib import ExitStack

import concourse.bass as bass
from concourse import mybir

F32 = mybir.dt.float32
BF16 = mybir.dt.bfloat16
I32 = mybir.dt.int32
U32 = mybir.dt.uint32
ALU = mybir.AluOpType
ACT = mybir.ActivationFunctionType
AX = mybir.AxisListType

P = 128
B, S, D = 8, 512, 256
NH, HD = 16, 16
KEYS = 2 * S
GH = 4
G = NH // GH
KT = KEYS // P
QT = S // P
DC = D // P
UNITS = B * G
EPS = 1e-5
Q_PART = (0, 0, 1, 1, 0, 2)
K_PART = (0, 1, 0, 1, 2, 0)
PARTS = 3
PROD = len(Q_PART) * HD
R_MASK = PROD
R_MAX = R_MASK + PARTS
ROWS = R_MAX + PARTS
LOADS = 2 * len(Q_PART) + 1



E, F = 8, 1024
FC = F // P
HC = FC // 2
TOP = 2
TOKENS = B * S
TT = TOKENS // P
CONSTS = 4
SLOT_TILES = TOP * TOKENS // P + E


def carve(region, at, shape, dt=F32):
    n = 1
    for d in shape[1:]:
        n *= d
    cols = n * (2 if dt == BF16 else 4) // 4
    v = region[0:shape[0], at:at + cols]
    if dt != F32:
        v = v.bitcast(dt)
    if len(shape) == 2:
        return v
    names = "abcd"[:len(shape) - 1]
    return v.rearrange(f"p ({' '.join(names)}) -> p {' '.join(names)}", **dict(zip(names, shape[1:])))


def flamingo_kernel(nc, x, ctx_in, mask, g_xattn, g_ffn, Wq, bq, Wk, bk, Wv, bv,
                    Wr, br, W1, b1, g1, be1, W2, b2, g2, be2, out):
    with ExitStack() as ctx:
        def sb(name, shape, dt=F32):
            return ctx.enter_context(nc.sbuf_tensor(name, shape, dt))

        def sem(name):
            return ctx.enter_context(nc.semaphore(name))

        def dram(name, shape, dt=F32):
            return nc.dram_tensor(name, shape, dt, kind="Internal").ap()

        q_parts = dram("q_parts", (B, PARTS, D, S), BF16)
        k_parts = dram("k_parts", (B, PARTS, D, KEYS), BF16)
        mask_parts = dram("mask_parts", (PARTS, B, KEYS), BF16)

        x1_d = dram("x1_d", (TT, P, D))
        slot_x = dram("slot_x", (SLOT_TILES * P, D))
        slot_y = dram("slot_y", (SLOT_TILES * P, D))

        big = sb("big", [P, E * (DC * F + FC * D)])
        mid = sb("mid", [P, E * F])
        small = sb("small", [P, 4864])
        q_stack = carve(big, 0, [P, G, GH, S], BF16)
        k_stack = carve(big, 4096, [P, G, GH, KEYS], BF16)
        probs = carve(big, 12288, [P, 2, GH, S])
        v_ring = carve(big, 16384, [P, G, KT, GH, 32])
        v_all = carve(big, 20480, [P, KT, D])
        all_t = carve(big, 22528, [P, DC, KEYS])
        x_in = carve(big, 24576, [P, QT, D])
        c_in = carve(big, 25600, [P, QT, D])
        proj = carve(big, 26624, [P, 2, S])
        rest = carve(big, 27648, [P, 2, S])
        proj_parts = carve(big, 28672, [P, 2, PARTS, S], BF16)
        x_res = carve(small, 0, [P, QT, D])
        o_sb = carve(small, 1024, [P, S])
        ctx_n = carve(small, 1536, [P, QT, GH * HD])
        xn2 = carve(small, 1792, [P, QT, D])
        xn2_t = carve(small, 2816, [P, DC, S])
        zero_rows = carve(small, 3840, [P, D])
        wq, wk, wv = (carve(big, 30208 + 512 * i, [P, DC, D]) for i in range(3))
        xn2_all = carve(mid, 0, [P, TT, D])
        wr = sb("wr", [P, DC, E]); b_r = sb("b_r", [P, E])
        logits = carve(small, 4352, [P, TT, E])
        gf_raw = sb("gf_raw", [P, 1]); gf_tanh = sb("gf_tanh", [P, 1])
        b_q = sb("b_q", [P, DC]); b_qs = sb("b_qs", [P, DC]); b_k = sb("b_k", [P, DC])
        b_v = carve(small, 4096, [P, D])
        ident = sb("ident", [P, P])
        g_raw = sb("g_raw", [P, 1]); g_tanh = sb("g_tanh", [P, 1])
        stat1 = sb("stat1", [P, QT, 6]); mv1 = sb("mv1", [P, QT, 2]); rstd1 = sb("rstd1", [P, QT])
        minus_half = sb("minus_half", [P, QT]); zero = sb("zero", [P, 1])
        stat2 = sb("stat2", [P, QT, 6]); mv2 = sb("mv2", [P, QT, 2]); rstd2 = sb("rstd2", [P, QT])
        m_half = carve(big, 31744, [P, 2, GH * QT * 2]); m_row = carve(big, 31808, [P, GH * QT])
        m_neg = carve(big, 31824, [GH * QT, P]); m_rest = carve(big, 31952, [GH * QT, P])
        m_parts = carve(big, 32080, [GH * QT, PARTS, P], BF16)
        r_sum = sb("r_sum", [P, QT, GH]); r_scl = sb("r_scl", [P, QT, GH])
        mk = carve(big, 32272, [64, P]); mk_rest = carve(big, 32400, [64, P]); mk_parts = carve(big, 32528, [64, PARTS, P], BF16)

        ps_t = ctx.enter_context(nc.psum_tensor("ps_t", [P, GH, S], F32))
        ps_s = ctx.enter_context(nc.psum_tensor("ps_s", [P, 2, S], F32))
        ps_o = ctx.enter_context(nc.psum_tensor("ps_o", [P, S], F32))
        ps_m = ctx.enter_context(nc.psum_tensor("ps_m", [P, S], F32))

        x_loaded = sem("x_loaded"); c_loaded = sem("c_loaded"); w_loaded = sem("w_loaded")
        const_ready = sem("const_ready"); ident_zero = sem("ident_zero"); bq_scaled = sem("bq_scaled"); bv_scaled = sem("bv_scaled"); res_biased = sem("res_biased"); g_ready = sem("g_ready")
        mask_loaded = sem("mask_loaded"); mask_step = sem("mask_step"); mask_stored = sem("mask_stored")
        stats1 = sem("stats1"); agg1 = sem("agg1"); rstd1_step = sem("rstd1_step"); x_normed = sem("x_normed")
        t_ready = sem("t_ready"); t_evac = sem("t_evac")
        qk_ready = sem("qk_ready"); qk_evac = sem("qk_evac"); qk_split = sem("qk_split"); parts_stored = [sem(f"parts_stored{h}") for h in range(2)]
        v_ready = sem("v_ready"); v_evac = sem("v_evac"); v_copied = sem("v_copied")
        stack_loaded = [sem(f"stack_loaded{g}") for g in range(G)]
        s_ready = sem("s_ready"); s_used = sem("s_used"); m_reduced = sem("m_reduced")
        m_ready = sem("m_ready"); m_evac = sem("m_evac"); m_split = sem("m_split")
        max_loaded = [sem(f"max_loaded{g}") for g in range(G)]
        st_ready = sem("st_ready"); exp_done = sem("exp_done"); pv_done = sem("pv_done")
        o_copied = sem("o_copied"); o_ready = sem("o_ready"); o_recip = sem("o_recip"); o_scaled = sem("o_scaled"); o_evac = sem("o_evac")
        res_loaded = sem("res_loaded"); x1_added = sem("x1_added")
        stats2 = sem("stats2"); agg2 = sem("agg2"); rstd2_step = sem("rstd2_step"); x1_normed = sem("x1_normed")
        x1_stored = sem("x1_stored"); xn2_stored = sem("xn2_stored")
        l_ready = sem("l_ready"); l_evac = sem("l_evac"); r_ready = sem("r_ready"); r_evac = sem("r_evac")
        ones_ready = sem("ones_ready"); ones_set = sem("ones_set"); zero_ready = sem("zero_ready"); slots_zeroed = sem("slots_zeroed")

        x_v = x.rearrange("b (t p) d -> b p t d", p=P)
        c_v = ctx_in.rearrange("b (t p) d -> b p t d", p=P)
        out_v = out.rearrange("b (t p) d -> (b t) p d", p=P)
        x1_v = x1_d.rearrange("(b t) p d -> b p t d", t=QT)

        PLAN = {0: ["T0"], 1: ["M", "T1"], 2: ["O", "T2"], 3: ["T3"], 4: ["Q0"], 5: ["Q1"], 6: ["Q2"],
                7: ["Q3"], 8: ["Q4"], 9: ["M", "Q5"], 10: ["O"], 11: ["V0"], 12: ["V1"], 13: ["V2"], 14: ["V3"],
                17: ["M"], 18: ["O"], 19: ["L0"], 20: ["L1"], 22: ["R"], 25: ["M"], 26: ["O"]}

        def plan(step, first, last):
            for use in PLAN.get(step, []):
                if use[0] in "TQV" and last:
                    continue
                if use == "M" and last and step >= 24:
                    continue
                if first and (use == "O" and step < 8 or use[0] in "LR"):
                    continue
                yield use

        w1_sb = carve(big, 0, [P, E, DC, F])
        w2_sb = carve(big, E * DC * F, [P, E, FC, D])
        b1_bc = carve(mid, 0, [P, E, F])
        h_sb = carve(small, 0, [P, 2, F])
        ht_sb = carve(small, 2048, [P, FC, P])
        x_sb = carve(small, 3072, [P, 2, D])
        xt_sb = carve(small, 3584, [P, 2, DC, P])
        y_sb = carve(small, 4096, [P, 3, D])
        g2_bc = sb("g2_bc", [P, E, D]); be2_bc = sb("be2_bc", [P, E, D]); b2_bc = sb("b2_bc", [P, E, D])
        gb_rows = carve(small, 4096, [E * FC, 2, P])
        g1_t = sb("g1_t", [P, 2, E * FC])
        h_stat = sb("h_stat", [P, 2, 6]); h_mv = sb("h_mv", [P, 2, 2]); h_rstd = sb("h_rstd", [P, 2])
        y_stat = sb("y_stat", [P, 6]); y_mv = sb("y_mv", [P, 2]); y_rstd = sb("y_rstd", [P, 1])
        ra, rb, rc, one1, one2, base_a, base_b = (carve(small, 256 * i, [P, TT, E]) for i in range(7))
        rank = carve(small, 1792, [P, E]); rank_i = carve(small, 1800, [P, E], I32)
        step_f = carve(small, 1808, [P, TT]); step_i = carve(small, 1840, [P, TT], I32)
        slot_f = carve(small, 1872, [P, SLOT_TILES]); slot_i = carve(small, 1952, [P, SLOT_TILES], I32)
        top1, top2, den, best = (carve(small, 2048 + 32 * i, [P, TT]) for i in range(4))
        tiles_e, start_a, start_b, count_e = (carve(small, 2176 + 8 * i, [P, E]) for i in range(4))
        more = carve(small, 2304, [P, E, TT])
        owner = carve(small, 2560, [P, SLOT_TILES, E])
        pos_f = carve(small, 3200, [P, TOP, TT]); owner_f = carve(small, 3264, [P, SLOT_TILES])
        oh = sb("oh", [P, TT, E], BF16); tri = sb("tri", [P, P], BF16); ones = sb("ones", [P, P], BF16)
        pos = sb("pos", [P, TOP, TT], U32)
        owner_i = sb("owner_i", [1, SLOT_TILES], I32)
        w_top = sb("w_top", [P, TOP, TT])
        y_got = carve(big, 0, [P, TOP, TT, D]); x1_sb = carve(big, TOP * TT * D, [P, TT, D])

        bc_loaded = sem("bc_loaded"); w1_loaded = sem("w1_loaded"); gb_loaded = sem("gb_loaded")
        gb_ready = sem("gb_ready"); gb_evac = sem("gb_evac")
        iota_step = sem("iota_step"); route = sem("route"); route_exp = sem("route_exp")
        counted = sem("counted"); scattered = sem("scattered"); oh_ready = sem("oh_ready"); routed = sem("routed")
        x_got = [sem(f"x_got{h}") for h in range(2)]
        xt_ready = sem("xt_ready"); xt_evac = sem("xt_evac")
        h_ready = sem("h_ready"); h_biased = sem("h_biased"); h_relu = sem("h_relu"); h_stats = sem("h_stats")
        h_agg = sem("h_agg"); h_pow = sem("h_pow"); h_normed = sem("h_normed")
        ht_ready = sem("ht_ready"); ht_scaled = sem("ht_scaled"); ht_done = sem("ht_done")
        y_ready = sem("y_ready"); y_biased = sem("y_biased"); y_relu = sem("y_relu"); y_stats = sem("y_stats")
        y_agg = sem("y_agg"); y_pow = sem("y_pow"); y_normed = sem("y_normed"); y_scaled = sem("y_scaled"); y_done = sem("y_done")
        y_stored = sem("y_stored")
        x1_back = [sem(f"x1_back{i}") for i in range(B)]
        y_back = [sem(f"y_back{i}") for i in range(B)]
        mixed = sem("mixed"); out_ready = sem("out_ready"); out_stored = sem("out_stored")
        ps_h = [ps_t[:, 0:2, :], ps_t[:, 2:4, :]]
        ps_ht = ps_s
        ps_y = ps_o[:, 0:D]
        ps_x = ps_m[:, 0:D]
        LAST = SLOT_TILES

        def tiles(eng, step):
            step(0); step(1)
            with eng.Fori(1, SLOT_TILES // 2 - 2) as i:
                step(2 * i, 0); step(2 * i + 1, 1)
            for j in range(SLOT_TILES - 4, SLOT_TILES):
                step(j)

        def experts_sync(sp):
            sp.wait_ge(pv_done, KT * UNITS)
            sp.wait_ge(o_ready, UNITS)
            for e in range(E):
                sp.dma_start(w1_sb[:, e, :, :], W1[e].rearrange("(c p) f -> p c f", p=P)).then_inc(w1_loaded, 16)
                sp.dma_start(w2_sb[:, e, :, :], W2[e].rearrange("(c p) d -> p c d", p=P)).then_inc(w1_loaded, 16)
            sp.wait_ge(r_ready, B)
            sp.wait_ge(xn2_stored, 16 * B)
            sp.dma_start(gb_rows[:, 0, :], g1.rearrange("e (c p) -> (e c) p", p=P)).then_inc(gb_loaded, 16)
            sp.dma_start(gb_rows[:, 1, :], be1.rearrange("e (c p) -> (e c) p", p=P)).then_inc(gb_loaded, 16)
            sp.wait_ge(scattered, 16 * TOP * TT)
            sp.dma_start(b1_bc[:, :, :], b1.partition_broadcast(P)).then_inc(w1_loaded, 16)

            def load(j, par):
                if isinstance(j, int) and j >= SLOT_TILES:
                    return
                if not (isinstance(j, int) and j < 2):
                    sp.wait_ge(xt_ready, j - 1)
                sp.dma_start(x_sb[:, par, :], slot_x[bass.ds(j * P, P), :]).then_inc(x_got[par], 16)

            def store(j):
                sp.wait_ge(y_done, j + 1)
                sp.dma_start(slot_y[bass.ds(j * P, P), :], y_sb[:, 2, :]).then_inc(y_stored, 16)

            sp.wait_ge(routed, 2)
            sp.wait_ge(gb_evac, 1)
            for j in range(4):
                load(j, j % 2)

            def step(j, par=None):
                par = j % 2 if par is None else par
                load(j + 4, par)
                if not (isinstance(j, int) and j == 0):
                    store(j - 1)

            tiles(sp, step)
            store(SLOT_TILES - 1)
            sp.wait_ge(y_ready, SLOT_TILES)
            for b in range(B):
                sp.dma_start(x1_sb[:, b * QT:(b + 1) * QT, :], x1_v[b]).then_inc(x1_back[b], 16)
            for t in range(TT):
                sp.wait_ge(out_ready, t + 1)
                sp.dma_start(out_v[t], x1_sb[:, t, :]).then_inc(out_stored, 16)
            sp.wait_ge(out_stored, 16 * TT)

        def expert_of(eng, j):
            return eng.value_load(owner_i[0:1, bass.ds(j, 1)], min_val=0, max_val=E - 1)

        def experts_tensor(pe):
            pe.wait_ge(oh_ready, 1)
            pe.wait_ge(r_evac, B)
            pe.matmul(ps_o[:, 0:TT * E], tri[:, :], oh[:, :, :], start=True, stop=True).then_inc(counted, 1)
            pe.matmul(ps_m[:, 0:TT * E], ones[:, :], oh[:, :, :], start=True, stop=True).then_inc(counted, 1)
            pe.wait_ge(gb_loaded, 32)
            for i in range(2):
                mm = pe.transpose(ps_s[:, 0, i * 64:(i + 1) * 64], gb_rows[:, i, :], ident[0:64, 0:64])
            mm.then_inc(gb_ready, 1)
            pe.wait_ge(gb_evac, 1)
            pe.wait_ge(routed, 1)

            def turn_x(j, par):
                if isinstance(j, int) and j >= SLOT_TILES:
                    return
                pe.wait_ge(x_got[par], 16 * (j // 2 + 1) if isinstance(j, int) else 16 * half[0])
                if not (isinstance(j, int) and j == 0):
                    pe.wait_ge(xt_evac, j)
                for k in range(DC):
                    mm = pe.transpose(ps_x[:, k * P:(k + 1) * P], x_sb[:, par, k * P:(k + 1) * P], ident[:, :])
                mm.then_inc(xt_ready, 1)

            half = [None]

            def up(j, par):
                if isinstance(j, int) and j >= SLOT_TILES:
                    return
                e = expert_of(pe, j)
                pe.wait_ge(xt_evac, j + 1)
                if not (isinstance(j, int) and j < 2):
                    pe.wait_ge(h_biased, j - 1)
                for n in range(2):
                    for k in range(DC):
                        mm = pe.matmul(ps_h[par][:, n, :], xt_sb[:, par, k, :], w1_sb[:, e, k, n * 512:(n + 1) * 512],
                                       start=(k == 0), stop=(k == DC - 1))
                mm.then_inc(h_ready, 1)

            def turn_h(j, par):
                pe.wait_ge(h_normed, j + 1)
                if not (isinstance(j, int) and j == 0):
                    pe.wait_ge(ht_scaled, 2 * j)
                for c in range(FC):
                    mm = pe.transpose(ps_ht[:, c // 4, c % 4 * P:(c % 4 + 1) * P], h_sb[:, par, c * P:(c + 1) * P], ident[:, :])
                mm.then_inc(ht_ready, 1)

            def down(j):
                e = expert_of(pe, j)
                if not (isinstance(j, int) and j == 0):
                    pe.wait_ge(y_biased, j)
                for c in range(FC):
                    if c % HC == 0:
                        pe.wait_ge(ht_done, 2 * j + c // HC + 1)
                    mm = pe.matmul(ps_y, ht_sb[:, c, :], w2_sb[:, e, c, :], start=(c == 0), stop=(c == FC - 1))
                mm.then_inc(y_ready, 1)

            pe.wait_ge(w1_loaded, 16 * (2 * E + 1))
            turn_x(0, 0)
            turn_x(1, 1)
            up(0, 0)
            turn_x(2, 0)
            up(1, 1)

            def plain(j, par_):
                turn_h(j, par_)
                up(j + 2, par_)
                turn_x(j + 3, 1 - par_)
                down(j)

            plain(0, 0)
            plain(1, 1)
            with pe.Fori(1, SLOT_TILES // 2 - 2) as i:
                half[0] = i + 2
                plain(2 * i, 0)
                half[0] = i + 3
                plain(2 * i + 1, 1)
            for j in range(SLOT_TILES - 4, SLOT_TILES):
                plain(j, j % 2)

        def experts_scalar(act):
            act.wait_ge(route, 3)
            act.activation(rb[:, :, :], ra[:, :, :], ACT.Exp).then_inc(route_exp, 1)

            def evac_x(j, par):
                if isinstance(j, int) and j >= SLOT_TILES:
                    return
                act.wait_ge(xt_ready, j + 1)
                if not (isinstance(j, int) and j < 2):
                    act.wait_ge(h_ready, j - 1)
                act.activation(xt_sb[:, par, :, :], ps_x.rearrange("p (k t) -> p k t", k=DC), ACT.Copy).then_inc(xt_evac, 1)

            def relu_h(j, par):
                if isinstance(j, int) and j >= SLOT_TILES:
                    return
                act.wait_ge(h_biased, j + 1)
                act.activation(h_sb[:, par, :], h_sb[:, par, :], ACT.Relu).then_inc(h_relu, 1)

            def relu_y(j):
                act.wait_ge(y_biased, j + 1)
                act.activation(y_sb[:, 0, :], y_sb[:, 0, :], ACT.Relu).then_inc(y_relu, 1)

            evac_x(0, 0)
            evac_x(1, 1)
            evac_x(2, 0)
            relu_h(0, 0)
            relu_h(1, 1)

            def step(j, par=None):
                par = j % 2 if par is None else par
                if not (isinstance(j, int) and j == 0):
                    relu_y(j - 1)
                evac_x(j + 3, 1 - par)
                relu_h(j + 2, par)

            tiles(act, step)
            relu_y(SLOT_TILES - 1)

        def experts_vector(dve):
            n = [0]

            def chain(ins):
                n[0] += 1
                ins.then_inc(route, 1)
                dve.wait_ge(route, n[0])

            def over_e(t):
                return t.unsqueeze(2).to_broadcast((P, TT, E))

            def over_t(t):
                return t.unsqueeze(1).to_broadcast((P, TT, E))

            dve.wait_ge(r_evac, B)
            dve.wait_ge(xn2_stored, 16 * B)
            dve.wait_ge(x1_stored, 16 * B)
            dve.wait_ge(iota_step, 3)
            chain(dve.tensor_tensor(ra[:, :, :], logits[:, :, :], over_t(b_r[:, :]), ALU.add))
            chain(dve.tensor_reduce(best[:, :], ra[:, :, :], AX.X, ALU.max))
            chain(dve.tensor_tensor(ra[:, :, :], ra[:, :, :], over_e(best[:, :]), ALU.subtract))
            dve.tensor_copy(rank[:, :], rank_i[:, :]).then_inc(route, 1)
            dve.tensor_copy(step_f[:, :], step_i[:, :]).then_inc(route, 1)
            n[0] += 2
            chain(dve.tensor_copy(slot_f[:, :], slot_i[:, :]))
            dve.wait_ge(route_exp, 1)
            chain(dve.tensor_reduce(den[:, :], rb[:, :, :], AX.X, ALU.add))
            chain(dve.reciprocal(den[:, :], den[:, :]))
            chain(dve.tensor_tensor(rb[:, :, :], rb[:, :, :], over_e(den[:, :]), ALU.mult))
            for top, one in ((top1, one1), (top2, one2)):
                chain(dve.tensor_reduce(top[:, :], rb[:, :, :], AX.X, ALU.max))
                chain(dve.tensor_tensor(rc[:, :, :], rb[:, :, :], over_e(top[:, :]), ALU.is_equal))
                chain(dve.tensor_tensor(rc[:, :, :], rc[:, :, :], over_t(rank[:, :]), ALU.mult))
                chain(dve.tensor_reduce(best[:, :], rc[:, :, :], AX.X, ALU.max))
                chain(dve.tensor_tensor(one[:, :, :], rc[:, :, :], over_e(best[:, :]), ALU.is_equal))
                if one is one1:
                    chain(dve.scalar_tensor_tensor(rb[:, :, :], one1[:, :, :], -2.0, rb[:, :, :], ALU.mult, ALU.add))
            dve.tensor_tensor(oh[:, :, :], one1[:, :, :], one2[:, :, :], ALU.add).then_inc(oh_ready, 1)
            chain(dve.tensor_tensor(den[:, :], top1[:, :], top2[:, :], ALU.add))
            chain(dve.reciprocal(den[:, :], den[:, :]))
            for k, top in enumerate((top1, top2)):
                chain(dve.tensor_tensor(top[:, :], top[:, :], den[:, :], ALU.mult))
                chain(dve.tensor_scalar(w_top[:, k, :], top[:, :], gf_tanh[:, 0:1], None, ALU.mult))
            dve.wait_ge(counted, 2)
            chain(dve.tensor_copy(base_a[:, :, :], ps_m[:, 0:TT * E].rearrange("p (t e) -> p t e", e=E)))
            chain(dve.tensor_copy(rc[:, :, :], base_a[:, :, :]))
            a, b_, reach = base_a, base_b, 1
            while reach < TT:
                dve.tensor_copy(b_[:, 0:reach, :], a[:, 0:reach, :]).then_inc(route, 1)
                n[0] += 1
                chain(dve.tensor_tensor(b_[:, reach:TT, :], a[:, reach:TT, :], a[:, 0:TT - reach, :], ALU.add))
                a, b_, reach = b_, a, 2 * reach
            chain(dve.tensor_copy(count_e[:, :], a[:, TT - 1, :]))
            chain(dve.tensor_tensor(b_[:, :, :], a[:, :, :], rc[:, :, :], ALU.subtract))
            chain(dve.tensor_tensor(more[:, :, :], count_e[:, :].unsqueeze(2).to_broadcast((P, E, TT)),
                                    step_f[:, :].unsqueeze(1).to_broadcast((P, E, TT)), ALU.is_gt))
            chain(dve.tensor_reduce(tiles_e[:, :], more[:, :, :], AX.X, ALU.add))
            chain(dve.memset(start_a[:, 0:1], 0.0))
            chain(dve.tensor_copy(start_a[:, 1:E], tiles_e[:, 0:E - 1]))
            c, d, reach = start_a, start_b, 1
            while reach < E:
                dve.tensor_copy(d[:, 0:reach], c[:, 0:reach]).then_inc(route, 1)
                n[0] += 1
                chain(dve.tensor_tensor(d[:, reach:E], c[:, reach:E], c[:, 0:E - reach], ALU.add))
                c, d, reach = d, c, 2 * reach
            chain(dve.scalar_tensor_tensor(b_[:, :, :], over_t(c[:, :]), float(P), b_[:, :, :], ALU.mult, ALU.add))
            chain(dve.tensor_tensor(b_[:, :, :], b_[:, :, :], ps_o[:, 0:TT * E].rearrange("p (t e) -> p t e", e=E), ALU.add))
            for k, one in enumerate((one1, one2)):
                chain(dve.tensor_tensor(rc[:, :, :], one[:, :, :], b_[:, :, :], ALU.mult))
                chain(dve.tensor_reduce(pos_f[:, k, :], rc[:, :, :], AX.X, ALU.add))
            dve.tensor_copy(pos[:, :, :], pos_f[:, :, :]).then_inc(routed, 1)
            chain(dve.tensor_tensor(owner[0:1, :, 1:E], slot_f[0:1, :].unsqueeze(2).to_broadcast((1, SLOT_TILES, E - 1)),
                                    c[0:1, 1:E].unsqueeze(1).to_broadcast((1, SLOT_TILES, E - 1)), ALU.is_ge))
            chain(dve.tensor_reduce(owner_f[0:1, :], owner[0:1, :, 1:E], AX.X, ALU.add))
            dve.tensor_copy(owner_i[:, :], owner_f[0:1, :]).then_inc(routed, 1)
            dve.wait_ge(gb_ready, 1)
            dve.tensor_copy(g1_t[:, :, :], ps_s[:, 0, 0:P].rearrange("p (i n) -> p i n", i=2)).then_inc(gb_evac, 1)
            dve.wait_ge(gb_evac, 1)
            dve.wait_ge(routed, 2)
            dve.wait_ge(w1_loaded, 16 * (2 * E + 1))
            dve.wait_ge(bc_loaded, 48)

            def bias_h(j, par):
                if isinstance(j, int) and j >= SLOT_TILES:
                    return
                e = expert_of(dve, j)
                dve.wait_ge(h_ready, j + 1)
                if not (isinstance(j, int) and j < 2):
                    dve.wait_ge(ht_ready, j - 1)
                dve.tensor_tensor(h_sb[:, par, :].rearrange("p (n f) -> p n f", n=2), ps_h[par],
                                  b1_bc[:, e, :].rearrange("p (n f) -> p n f", n=2), ALU.add).then_inc(h_biased, 1)

            def stats_h(j, par):
                if isinstance(j, int) and j >= SLOT_TILES:
                    return
                hold(dve, h_relu, j + 1)
                for i in range(2):
                    dve.bn_stats(h_stat[:, i, :], h_sb[:, par, i * 512:(i + 1) * 512]).then_inc(h_stats, 1)
                hold(dve, h_stats, 2 * (j + 1))
                dve.bn_aggr(h_mv[:, par, :], h_stat[:, :, :]).then_inc(h_agg, 1)

            def norm_h(j, par):
                if isinstance(j, int) and j >= SLOT_TILES:
                    return
                dve.wait_ge(h_pow, 2 * (j + 1))
                dve.tensor_scalar(h_sb[:, par, :], h_sb[:, par, :], h_mv[:, par, 0:1], h_rstd[:, par:par + 1],
                                  ALU.subtract, ALU.mult).then_inc(h_normed, 1)

            def scale_ht(j):
                e = expert_of(dve, j)
                dve.wait_ge(ht_ready, j + 1)
                if not (isinstance(j, int) and j == 0):
                    dve.wait_ge(y_ready, j)
                for i in range(2):
                    dve.tensor_tensor(ht_sb[:, i * HC:(i + 1) * HC, :], ps_ht[:, i, :].rearrange("p (c t) -> p c t", t=P),
                                      g1_t[:, 0, bass.ds(e * FC + i * HC, HC)].unsqueeze(2).to_broadcast((P, HC, P)),
                                      ALU.mult).then_inc(ht_scaled, 1)

            def bias_y(j):
                e = expert_of(dve, j)
                dve.wait_ge(y_ready, j + 1)
                if not (isinstance(j, int) and j == 0):
                    dve.wait_ge(y_normed, j)
                dve.tensor_tensor(y_sb[:, 0, :], ps_y, b2_bc[:, e, :], ALU.add).then_inc(y_biased, 1)

            def stats_y(j):
                hold(dve, y_relu, j + 1)
                dve.bn_stats(y_stat[:, :], y_sb[:, 0, :]).then_inc(y_stats, 1)
                hold(dve, y_stats, j + 1)
                dve.bn_aggr(y_mv[:, :], y_stat[:, :]).then_inc(y_agg, 1)

            def norm_y(j):
                dve.wait_ge(y_pow, 2 * (j + 1))
                if not (isinstance(j, int) and j == 0):
                    dve.wait_ge(y_scaled, j)
                dve.tensor_scalar(y_sb[:, 1, :], y_sb[:, 0, :], y_mv[:, 0:1], y_rstd[:, 0:1],
                                  ALU.subtract, ALU.mult).then_inc(y_normed, 1)

            bias_h(0, 0)
            stats_h(0, 0)
            bias_h(1, 1)
            norm_h(0, 0)
            stats_h(1, 1)

            def step(j, par=None):
                par = j % 2 if par is None else par
                after = not (isinstance(j, int) and j == 0)
                scale_ht(j)
                if after:
                    bias_y(j - 1)
                norm_h(j + 1, 1 - par)
                bias_h(j + 2, par)
                if after:
                    stats_y(j - 1)
                stats_h(j + 2, par)
                if after:
                    norm_y(j - 1)

            tiles(dve, step)
            bias_y(SLOT_TILES - 1)
            stats_y(SLOT_TILES - 1)
            norm_y(SLOT_TILES - 1)
            for t in range(TT):
                if t % QT == 0:
                    dve.wait_ge(x1_back[t // QT], 16)
                    dve.wait_ge(y_back[t // QT], 16 * TOP * QT)
                dve.scalar_tensor_tensor(x1_sb[:, t, :], y_got[:, 0, t, :], w_top[:, 0, t:t + 1], x1_sb[:, t, :],
                                         ALU.mult, ALU.add).then_inc(mixed, 1)
                dve.wait_ge(mixed, t + 1)
                dve.scalar_tensor_tensor(x1_sb[:, t, :], y_got[:, 1, t, :], w_top[:, 1, t:t + 1], x1_sb[:, t, :],
                                         ALU.mult, ALU.add).then_inc(out_ready, 1)

        def experts_gpsimd(pool):
            pool.wait_ge(xn2_stored, 16 * B)
            pool.wait_ge(x1_stored, 16 * B)
            pool.wait_ge(r_ready, B)
            pool.iota(rank_i[:, :], pattern=[[-1, E]], base=E, channel_multiplier=0).then_inc(iota_step, 1)
            pool.iota(step_i[:, :], pattern=[[P, TT]], base=0, channel_multiplier=0).then_inc(iota_step, 1)
            pool.iota(slot_i[:, :], pattern=[[1, SLOT_TILES]], base=0, channel_multiplier=0).then_inc(iota_step, 1)
            pool.wait_ge(routed, 1)
            pool.wait_ge(slots_zeroed, 16)
            for t in range(TT):
                for k in range(TOP):
                    pool.indirect_dma_start(out=slot_x, out_offset=bass.IndirectOffsetOnAxis(ap=pos[:, k, t:t + 1], axis=0),
                                            in_=xn2_all[:, t, :], in_offset=None).then_inc(scattered, 16)
            pool.wait_ge(gb_evac, 1)
            pool.wait_ge(routed, 2)

            def pow_h(j, par):
                if isinstance(j, int) and j >= SLOT_TILES:
                    return
                hold(pool, h_agg, j + 1)
                pool.tensor_scalar(h_rstd[:, par:par + 1], h_mv[:, par, 1:2], EPS, None, ALU.add).then_inc(h_pow, 1)
                pool.wait_ge(h_pow, 2 * j + 1)
                pool.tensor_tensor(h_rstd[:, par:par + 1], h_rstd[:, par:par + 1], minus_half[:, 0:1], ALU.pow).then_inc(h_pow, 1)

            def shift_ht(j):
                e = expert_of(pool, j)
                for i in range(2):
                    pool.wait_ge(ht_scaled, 2 * j + i + 1)
                    h = ht_sb[:, i * HC:(i + 1) * HC, :]
                    pool.tensor_tensor(h, h, g1_t[:, 1, bass.ds(e * FC + i * HC, HC)].unsqueeze(2).to_broadcast((P, HC, P)),
                                       ALU.add).then_inc(ht_done, 1)

            def pow_y(j):
                hold(pool, y_agg, j + 1)
                pool.tensor_scalar(y_rstd[:, :], y_mv[:, 1:2], EPS, None, ALU.add).then_inc(y_pow, 1)
                pool.wait_ge(y_pow, 2 * j + 1)
                pool.tensor_tensor(y_rstd[:, :], y_rstd[:, :], minus_half[:, 0:1], ALU.pow).then_inc(y_pow, 1)

            def scale_y(j):
                e = expert_of(pool, j)
                pool.wait_ge(y_normed, j + 1)
                if not (isinstance(j, int) and j == 0):
                    pool.wait_ge(y_stored, 16 * j)
                pool.tensor_tensor(y_sb[:, 2, :], y_sb[:, 1, :], g2_bc[:, e, :], ALU.mult).then_inc(y_scaled, 1)
                pool.wait_ge(y_scaled, j + 1)
                pool.tensor_tensor(y_sb[:, 2, :], y_sb[:, 2, :], be2_bc[:, e, :], ALU.add).then_inc(y_done, 1)

            pow_h(0, 0)
            pow_h(1, 1)

            def step(j, par=None):
                par = j % 2 if par is None else par
                after = not (isinstance(j, int) and j == 0)
                shift_ht(j)
                if after:
                    pow_y(j - 1)
                pow_h(j + 2, par)
                if after:
                    scale_y(j - 1)

            tiles(pool, step)
            pow_y(SLOT_TILES - 1)
            scale_y(SLOT_TILES - 1)
            pool.wait_ge(y_stored, 16 * SLOT_TILES)
            for t in range(TT):
                for k in range(TOP):
                    pool.indirect_dma_start(out=y_got[:, k, t, :], out_offset=None, in_=slot_y,
                                            in_offset=bass.IndirectOffsetOnAxis(ap=pos[:, k, t:t + 1], axis=0)
                                            ).then_inc(y_back[t // QT], 16)

        hold_reg = {}

        def hold(eng, semaphore, count):
            if isinstance(count, int):
                eng.wait_ge(semaphore, count)
            else:
                if eng.engine not in hold_reg:
                    hold_reg[eng.engine] = eng.alloc_register(f"hold_{len(hold_reg)}")
                eng.reg_mov(hold_reg[eng.engine], count)
                eng.wait_ge(const_ready, CONSTS)
                eng.wait_ge(semaphore, hold_reg[eng.engine])

        def split3(eng, dst, src, tmp, step, at):
            none = zero[0:src.shape[0], 0:1].to_broadcast(src.shape)
            eng.tensor_tensor(dst[0], src, none, ALU.add).then_inc(step, 1)
            hold(eng, step, at + 1)
            eng.tensor_tensor(tmp, src, dst[0], ALU.subtract).then_inc(step, 1)
            hold(eng, step, at + 2)
            eng.tensor_tensor(dst[1], tmp, none, ALU.add).then_inc(step, 1)
            hold(eng, step, at + 3)
            eng.tensor_tensor(dst[2], tmp, dst[1], ALU.subtract).then_inc(step, 1)

        def bank(kind, b, i):
            if not (isinstance(b, int) and b == 0):
                return ps_m[:, :]
            return ps_s[:, i % 2, :] if kind == "V" else ps_t[:, i % 4, :]

        block = ctx.enter_context(nc.Block())

        @block.sync
        def _(sp):
            def load_x(b):
                sp.dma_start(x_in[:, :, :], x_v[b]).then_inc(x_loaded, 16)
                sp.dma_start(c_in[:, :, :], c_v[b]).then_inc(c_loaded, 16)

            def store_parts(b, i):
                sp.wait_ge(qk_split, 4 * (6 * b + i + 1))
                if i < 2:
                    dst = q_parts[b, :, i * P:(i + 1) * P, :]
                else:
                    c, h = divmod(i - 2, 2)
                    dst = k_parts[b, :, c * P:(c + 1) * P, h * S:(h + 1) * S]
                sp.dma_start(dst.rearrange("j p t -> p j t"), proj_parts[:, i % 2, :, :]).then_inc(parts_stored[i % 2], 16)

            def load_stack(b, g):
                for r in range(len(Q_PART)):
                    h0 = g * GH * HD
                    src = q_parts[b, Q_PART[r], h0:h0 + GH * HD, :].rearrange("(h d) t -> d h t", d=HD)
                    sp.dma_start(q_stack[r * HD:(r + 1) * HD, g, :, :], src).then_inc(stack_loaded[g], 16)
                    src = k_parts[b, K_PART[r], h0:h0 + GH * HD, :].rearrange("(h d) t -> d h t", d=HD)
                    sp.dma_start(k_stack[r * HD:(r + 1) * HD, g, :, :], src).then_inc(stack_loaded[g], 16)
                src = mask_parts[:, b, :].unsqueeze(1).to_broadcast((PARTS, GH, KEYS))
                sp.dma_start(k_stack[R_MASK:R_MAX, g, :, :], src).then_inc(stack_loaded[g], 16)

            def load_max(b, g):
                sp.wait_ge(m_split, 4 * (G * b + g + 1))
                for j in range(PARTS):
                    sp.dma_start(q_stack[R_MAX + j:R_MAX + j + 1, g, :, :].rearrange("o h (t q) -> o (h t) q", q=P),
                                 m_parts[:, j, :]).then_inc(max_loaded[g], 16)

            def batch(b, first=False, last=False):
                if not first:
                    sp.wait_ge(st_ready, 2 * KT * (G * b))
                    load_stack(b, 3)
                load_max(b, 1)
                if not last:
                    sp.wait_ge(t_ready, 4 * (b + 2))
                    load_next(b + 2)
                    for i in range(5):
                        store_parts(b + 1, i)
                    sp.wait_ge(parts_stored[0], 16 * (3 * (b + 1) + 2))
                    sp.wait_ge(parts_stored[1], 16 * (3 * (b + 1) + 2))
                    sp.wait_ge(st_ready, 2 * KT * (G * b + 1))
                    load_stack(b + 1, 0)
                load_max(b, 2)
                if not last:
                    store_parts(b + 1, 5)
                if not first:
                    store_x1(b - 1)
                sp.dma_start(x_res[:, :, :], x_v[b]).then_inc(res_loaded, 16)
                if not last:
                    for half in range(2):
                        sp.wait_ge(parts_stored[half], 16 * 3 * (b + 2))
                load_max(b, 3)
                if not last:
                    sp.wait_ge(st_ready, 2 * KT * (G * b + 2))
                    load_stack(b + 1, 1)
                    load_max(b + 1, 0)
                    sp.wait_ge(st_ready, 2 * KT * (G * b + 3))
                    load_stack(b + 1, 2)

            def store_x1(b):
                sp.wait_ge(x1_added, G * (b + 1))
                sp.dma_start(x1_v[b], x_res[:, :, :]).then_inc(x1_stored, 16)
                sp.wait_ge(x1_normed, QT * (b + 1))
                sp.dma_start(xn2_all[:, bass.ds(b * QT, QT), :], xn2[:, :, :]).then_inc(xn2_stored, 16)
                sp.wait_ge(x1_stored, 16 * (b + 1))

            def load_next(b):
                if isinstance(b, int) and b >= B:
                    return
                load_x(b)

            sp.dma_start(mk[:, :], mask.rearrange("b o n (k c) -> (b o n k) c", c=P)).then_inc(mask_loaded, 16)
            load_x(0)
            for w, t in ((Wq, wq), (Wk, wk), (Wv, wv)):
                sp.dma_start(t[:, :, :], w.rearrange("(c p) n -> p c n", p=P)).then_inc(w_loaded, 16)
            sp.dma_start(b_q[:, :], bq.rearrange("(c p) -> p c", p=P), allow_slow_non_contiguous=True).then_inc(w_loaded, 16)
            sp.dma_start(b_k[:, :], bk.rearrange("(c p) -> p c", p=P), allow_slow_non_contiguous=True).then_inc(w_loaded, 16)
            sp.dma_start(b_v[:, :], bv.partition_broadcast(P)).then_inc(w_loaded, 16)
            sp.dma_start(g_raw[:, :], g_xattn.partition_broadcast(P)).then_inc(w_loaded, 16)
            sp.dma_start(wr[:, :, :], Wr.rearrange("(c p) e -> p c e", p=P)).then_inc(w_loaded, 16)
            sp.dma_start(b_r[:, :], br.partition_broadcast(P)).then_inc(w_loaded, 16)
            sp.dma_start(gf_raw[:, :], g_ffn.partition_broadcast(P)).then_inc(w_loaded, 16)
            sp.wait_ge(mask_step, 4)
            sp.dma_start(mask_parts.rearrange("j b (k c) -> (b k) j c", c=P), mk_parts[:, :, :]).then_inc(mask_stored, 16)
            sp.wait_ge(t_ready, 4)
            load_x(1)
            for i in range(6):
                store_parts(0, i)
            for half in range(2):
                sp.wait_ge(parts_stored[half], 16 * 3)
            sp.wait_ge(mask_stored, 16)
            sp.wait_ge(ones_set, 3)
            for g in range(4):
                load_stack(0, g)
            load_max(0, 0)
            sp.wait_ge(zero_ready, 1)
            sp.dma_start(slot_x.rearrange("(j p) d -> p j d", p=P),
                         zero_rows[:, :].unsqueeze(1).to_broadcast((P, SLOT_TILES, D))).then_inc(slots_zeroed, 16)
            sp.dma_start(g2_bc[:, :, :], g2.partition_broadcast(P)).then_inc(bc_loaded, 16)
            sp.dma_start(be2_bc[:, :, :], be2.partition_broadcast(P)).then_inc(bc_loaded, 16)
            sp.dma_start(b2_bc[:, :, :], b2.partition_broadcast(P)).then_inc(bc_loaded, 16)
            batch(0, first=True)
            with sp.Fori(1, B - 2) as b:
                batch(b)
            batch(B - 2)
            batch(B - 1, last=True)
            store_x1(B - 1)
            experts_sync(sp)

        @block.tensor
        def _(pe):
            EVAC = {"T": t_evac, "Q": qk_evac, "V": v_evac, "M": m_evac, "O": o_evac, "L": l_evac, "R": r_evac}
            prev = [None]

            def spare_free():
                if prev[0] is not None:
                    kind, n = prev[0]
                    pe.wait_ge(EVAC[kind], n + 1)

            def use_T(b, i):
                src = x_in if i < 2 else c_in
                if i == 0:
                    pe.wait_ge(x_normed, QT * (b + 1))
                if i == 2:
                    pe.wait_ge(c_loaded, 16 * (b + 1))
                for t in range(QT):
                    mm = pe.transpose(bank("T", b, i)[:, t * P:(t + 1) * P], src[:, t, (i % 2) * P:(i % 2 + 1) * P], ident[:, :])
                mm.then_inc(t_ready, 1)

            def use_Q(b, i):
                pe.wait_ge(t_evac, 4 * b + 4 if i > 1 else 4 * b + 2)
                c, h = (i, 0) if i < 2 else divmod(i - 2, 2)
                w = wq if i < 2 else wk
                if isinstance(b, int) and b == 0 and i >= 4:
                    pe.wait_ge(qk_evac, i - 3)
                for k in range(DC):
                    mm = pe.matmul(bank("Q", b, i), w[:, k, c * P:(c + 1) * P], all_t[:, k, h * S:(h + 1) * S],
                                   start=(k == 0), stop=(k == DC - 1))
                mm.then_inc(qk_ready, 1)

            def use_V(b, i):
                if isinstance(b, int) and b == 0 and i >= 2:
                    pe.wait_ge(v_evac, i - 1)
                for n in range(2):
                    for k in range(DC):
                        kt = 2 * i + n
                        mm = pe.matmul(bank("V", b, i)[:, n * D:(n + 1) * D], all_t[:, k, kt * P:(kt + 1) * P], wv[:, k, :],
                                       start=(k == 0), stop=(k == DC - 1))
                mm.then_inc(v_ready, 1)

            def use_M(u):
                pe.wait_ge(m_reduced, u + 1)
                pe.transpose(ps_m[0:GH * QT, 0:P], m_row[:, :], ident[:, :]).then_inc(m_ready, 1)

            def use_O(u):
                pe.wait_ge(o_copied, u + 1)
                for t in range(QT):
                    mm = pe.transpose(ps_m[:, t * P:(t + 1) * P], o_sb[:, t * P:(t + 1) * P], ident[:, :])
                mm.then_inc(o_ready, 1)

            def use_L(b, i):
                if i == 0:
                    pe.wait_ge(x1_normed, QT * (b + 1))
                for t in range(QT):
                    mm = pe.transpose(ps_m[:, t * P:(t + 1) * P], xn2[:, t, i * P:(i + 1) * P], ident[:, :])
                mm.then_inc(l_ready, 1)

            def use_R(b):
                for t in range(QT):
                    for k in range(DC):
                        mm = pe.matmul(ps_m[:, t * E:(t + 1) * E], xn2_t[:, k, t * P:(t + 1) * P], wr[:, k, :],
                                       start=(k == 0), stop=(k == DC - 1))
                mm.then_inc(r_ready, 1)

            def spare(use, b, u):
                spare_free()
                kind, i = use[0], int(use[1:] or 0)
                if kind == "T":
                    use_T(b + 1, i); n = 4 * (b + 1) + i
                elif kind == "Q":
                    use_Q(b + 1, i); n = 6 * (b + 1) + i
                elif kind == "V":
                    use_V(b + 1, i); n = 4 * (b + 1) + i
                elif kind == "M":
                    use_M(u + 1); n = u + 1
                elif kind == "L":
                    use_L(b - 1, i); n = 2 * (b - 1) + i
                elif kind == "R":
                    use_R(b - 1); n = b - 1
                else:
                    use_O(u - 1); n = u - 1
                prev[0] = (kind, n)

            def scores_max(w, g, i):
                h, t, half = i // 8, i // 2 % QT, i % 2
                n = 32 * w + i
                if not (isinstance(n, int) and n < 2):
                    pe.wait_ge(s_used, n - 1)
                pe.matmul(ps_s[:, i % 2, :], q_stack[0:R_MAX, g, h, t * P:(t + 1) * P],
                          k_stack[0:R_MAX, g, h, half * S:(half + 1) * S], start=True, stop=True).then_inc(s_ready, 1)

            def scores_t(b, g, k, pair):
                n = KT * (G * b + g) + k
                if k == 0 and pair == 0:
                    pe.wait_ge(max_loaded[g], 16 * PARTS * (b + 1))
                if not (isinstance(n, int) and n == 0):
                    pe.wait_ge(exp_done, 2 * n - 1 + pair)
                for h in (2 * pair, 2 * pair + 1):
                    mm = pe.matmul(ps_t[:, h, :], k_stack[0:ROWS, g, h, k * P:(k + 1) * P], q_stack[0:ROWS, g, h, :],
                                   start=True, stop=True)
                mm.then_inc(st_ready, 1)

            def probs_v(b, g, k):
                u = G * b + g
                pe.wait_ge(exp_done, 2 * (KT * u + k) + 2)
                if k == 0:
                    pe.wait_ge(v_copied, u + 1)
                    if not (isinstance(u, int) and u == 0):
                        pe.wait_ge(o_copied, u)
                for h in range(GH):
                    mm = pe.matmul(ps_o[32 * h:32 * h + 32, :], v_ring[:, g, k, h, :], probs[:, k % 2, h, :],
                                   start=(k == 0), stop=(k == KT - 1))
                mm.then_inc(pv_done, 1)

            def batch(b, first=False, last=False):
                for step in range(G * KT):
                    g, k = divmod(step, KT)
                    slot = (g + 2) % G

                    def ahead(i):
                        if last and g >= 2:
                            return
                        if k == 0 and i == 0:
                            pe.wait_ge(stack_loaded[slot], 16 * LOADS * (b + 1 + (g + 2) // G))
                        scores_max(G * b + g + 2, slot, 4 * k + i)

                    ahead(0)
                    scores_t(b, g, k, 0)
                    ahead(1)
                    scores_t(b, g, k, 1)
                    uses = list(plan(step, first, last))
                    for use in uses[0:1]:
                        spare(use, b, G * b + g)
                    ahead(2)
                    ahead(3)
                    if step:
                        probs_v(b, (step - 1) // KT, (step - 1) % KT)
                    elif not first:
                        probs_v(b - 1, G - 1, KT - 1)
                    for use in uses[1:]:
                        spare(use, b, G * b + g)

            pe.wait_ge(const_ready, CONSTS)
            pe.wait_ge(w_loaded, 16 * 10)
            for i in range(4):
                use_T(0, i)
            for i in range(6):
                use_Q(0, i)
            for i in range(4):
                use_V(0, i)
            pe.wait_ge(v_evac, 4)
            for w in range(2):
                pe.wait_ge(stack_loaded[w], 16 * LOADS)
                for i in range(32):
                    scores_max(w, w, i)
                if w == 0:
                    spare("M", 0, -1)
            batch(0, first=True)
            with pe.Fori(1, B - 2) as b:
                prev[0] = ("O", G * b - 2)
                batch(b)
            prev[0] = ("O", G * (B - 2) - 2)
            batch(B - 2)
            batch(B - 1, last=True)
            probs_v(B - 1, G - 1, KT - 1)
            for use in ("O", "L0", "L1", "R"):
                spare(use, B, UNITS)
            experts_tensor(pe)

        @block.scalar
        def _(act):
            def evac_T(b, i):
                act.wait_ge(t_ready, 4 * b + i + 1)
                o = S * (i // 2)
                act.activation(all_t[:, i % 2, o:o + S], bank("T", b, i), ACT.Copy).then_inc(t_evac, 1)

            def evac_Q(b, i):
                act.wait_ge(qk_ready, 6 * b + i + 1)
                if not (isinstance(b, int) and b == 0 and i < 2):
                    act.wait_ge(qk_split, 4 * (6 * b + i - 1))
                bias = b_qs[:, i:i + 1] if i < 2 else b_k[:, (i - 2) // 2:(i - 2) // 2 + 1]
                act.activation(proj[:, i % 2, :], bank("Q", b, i), ACT.Identity, bias=bias,
                               scale=HD ** -0.5 if i < 2 else 1.0).then_inc(qk_evac, 1)

            def evac_V(b, i):
                act.wait_ge(v_ready, 4 * b + i + 1)
                if i == 0 and not (isinstance(b, int) and b == 0):
                    act.wait_ge(v_copied, G * b)
                act.activation(v_all[:, 2 * i:2 * i + 2, :], bank("V", b, i).rearrange("p (n d) -> p n d", d=D),
                               ACT.Copy).then_inc(v_evac, 1)

            def evac_L(b, i):
                act.wait_ge(l_ready, 2 * b + i + 1)
                if i == 0 and not (isinstance(b, int) and b == 0):
                    act.wait_ge(r_ready, b)
                act.activation(xn2_t[:, i, :], ps_m[:, :], ACT.Copy).then_inc(l_evac, 1)

            def copy_O(u):
                act.wait_ge(pv_done, KT * (u + 1))
                if not (isinstance(u, int) and u == 0):
                    act.wait_ge(o_ready, u)
                act.activation(o_sb[:, :], ps_o[:, :], ACT.Copy).then_inc(o_copied, 1)

            def exp(b, g, k, pair):
                n = KT * (G * b + g) + k
                act.wait_ge(st_ready, 2 * n + pair + 1)
                if pair == 0 and not (isinstance(n, int) and n < 2):
                    act.wait_ge(pv_done, n - 1)
                act.activation(probs[:, k % 2, 2 * pair:2 * pair + 2, :], ps_t[:, 2 * pair:2 * pair + 2, :],
                               ACT.Exp).then_inc(exp_done, 1)

            def batch(b, first=False, last=False):
                for step in range(G * KT):
                    g, k = divmod(step, KT)
                    exp(b, g, k, 0)
                    exp(b, g, k, 1)
                    for use in plan(step, first, last):
                        if use[0] == "T":
                            evac_T(b + 1, int(use[1]))
                        if use[0] == "Q":
                            evac_Q(b + 1, int(use[1]))
                        if use[0] == "V":
                            evac_V(b + 1, int(use[1]))
                        if use[0] == "L":
                            evac_L(b - 1, int(use[1]))
                    if k == 0 and not (first and g == 0):
                        copy_O(G * b + g - 1)

            act.wait_ge(w_loaded, 16 * 10)
            act.activation(b_qs[:, :], b_q[:, :], ACT.Copy, scale=HD ** -0.5).then_inc(bq_scaled, 1)
            act.activation(g_tanh[:, :], g_raw[:, :], ACT.Tanh).then_inc(g_ready, 1)
            act.activation(gf_tanh[:, :], gf_raw[:, :], ACT.Tanh).then_inc(g_ready, 1)
            act.wait_ge(bq_scaled, 1)
            for i in range(4):
                evac_T(0, i)
            for i in range(6):
                evac_Q(0, i)
            for i in range(4):
                evac_V(0, i)
            batch(0, first=True)
            with act.Fori(1, B - 2) as b:
                batch(b)
            batch(B - 2)
            batch(B - 1, last=True)
            copy_O(UNITS - 1)
            evac_L(B - 1, 0)
            evac_L(B - 1, 1)
            experts_scalar(act)

        @block.vector
        def _(dve):
            def stats_x(b, tiles=range(QT)):
                dve.wait_ge(x_loaded, 16 * (b + 1))
                for t in tiles:
                    dve.bn_stats(stat1[:, t, :], x_in[:, t, :]).then_inc(stats1, 1)

            def means_x(b):
                hold(dve, stats1, QT * (b + 1))
                if not (isinstance(b, int) and b == 0):
                    hold(dve, x_normed, QT * b)
                for t in range(QT):
                    dve.bn_aggr(mv1[:, t, :], stat1[:, t, :]).then_inc(agg1, 1)

            def norm_x(b, tiles=range(QT)):
                dve.wait_ge(rstd1_step, 2 * b + 2)
                for t in tiles:
                    dve.tensor_scalar(x_in[:, t, :], x_in[:, t, :], mv1[:, t, 0:1], rstd1[:, t:t + 1],
                                      ALU.subtract, ALU.mult).then_inc(x_normed, 1)

            def stats_x1(b, tiles=range(QT)):
                dve.wait_ge(x1_added, G * (b + 1))
                for t in tiles:
                    dve.bn_stats(stat2[:, t, :], x_res[:, t, :]).then_inc(stats2, 1)

            def means_x1(b):
                hold(dve, stats2, QT * (b + 1))
                if not (isinstance(b, int) and b == 0):
                    hold(dve, x1_normed, QT * b)
                for t in range(QT):
                    dve.bn_aggr(mv2[:, t, :], stat2[:, t, :]).then_inc(agg2, 1)

            def norm_x1(b, tiles=range(QT)):
                if tiles[0] == 0:
                    dve.wait_ge(rstd2_step, 2 * b + 2)
                if tiles[0] == 0 and not (isinstance(b, int) and b == 0):
                    hold(dve, xn2_stored, 16 * b)
                    hold(dve, l_ready, 2 * b)
                for t in tiles:
                    dve.tensor_scalar(xn2[:, t, :], x_res[:, t, :], mv2[:, t, 0:1], rstd2[:, t:t + 1],
                                      ALU.subtract, ALU.mult).then_inc(x1_normed, 1)

            def evac_R(b):
                dve.wait_ge(r_ready, b + 1)
                dve.tensor_copy(logits[:, bass.ds(b * QT, QT), :],
                                ps_m[:, 0:QT * E].rearrange("p (t e) -> p t e", e=E)).then_inc(r_evac, 1)

            def reduce_max(w, par, i):
                n = 32 * w + i
                if i == 0 and not (isinstance(w, int) and w < 2):
                    dve.wait_ge(m_reduced, w - 1)
                dve.wait_ge(s_ready, n + 1)
                dve.tensor_reduce(m_half[:, par, i:i + 1], ps_s[:, i % 2, :], AX.X, ALU.max).then_inc(s_used, 1)

            def join_max(u, par):
                dve.wait_ge(s_used, 32 * (u + 1))
                if not (isinstance(u, int) and u == 0):
                    dve.wait_ge(m_ready, u)
                dve.tensor_reduce(m_row[:, :], m_half[:, par, :].rearrange("p (n h) -> p n h", h=2), AX.X,
                                  ALU.max).then_inc(m_reduced, 1)

            def evac_M(u):
                dve.wait_ge(m_ready, u + 1)
                if not (isinstance(u, int) and u == 0):
                    dve.wait_ge(m_split, 4 * u)
                dve.tensor_scalar(m_neg[:, :], ps_m[0:GH * QT, 0:P], -1.0, None, ALU.mult).then_inc(m_evac, 1)

            def evac_O(u):
                dve.wait_ge(o_ready, u + 1)
                o = ps_m[:, :].rearrange("p (t h d) -> p t h d", t=QT, h=GH)
                dve.reciprocal(r_sum[:, :, :], o[:, :, :, HD]).then_inc(o_recip, 1)
                dve.wait_ge(o_recip, u + 1)
                dve.tensor_scalar(r_scl[:, :, :], r_sum[:, :, :], g_tanh[:, 0:1], None, ALU.mult).then_inc(o_scaled, 1)
                dve.wait_ge(o_scaled, u + 1)
                if not (isinstance(u, int) and u == 0):
                    dve.wait_ge(x1_added, u)
                dve.tensor_tensor(ctx_n[:, :, :].rearrange("p t (h d) -> p t h d", d=HD), o[:, :, :, 0:HD],
                                  r_scl[:, :, :].unsqueeze(3).to_broadcast((P, QT, GH, HD)),
                                  ALU.mult).then_inc(o_evac, 1)

            def ahead(u, g, k, i, last):
                if not (last and g >= 2):
                    reduce_max(u + 2, g % 2, 4 * k + i)
                    reduce_max(u + 2, g % 2, 4 * k + i + 1)

            HALF = (range(0, QT // 2), range(QT // 2, QT))

            def batch(b, first=False, last=False, stats=True):
                for step in range(G * KT):
                    g, k = divmod(step, KT)
                    u = G * b + g
                    if k == 0 and not (last and g == 3):
                        join_max(u + 1, (g + 1) % 2)
                    ahead(u, g, k, 0, last)
                    for use in plan(step, first, last):
                        if use == "M":
                            evac_M(u + 1)
                        if use == "O":
                            evac_O(u - 1)
                        if use == "R":
                            evac_R(b - 1)
                    ahead(u, g, k, 2, last)
                    if not first:
                        if step in (5, 6):
                            stats_x1(b - 1, HALF[step - 5])
                        if step == 7:
                            means_x1(b - 1)
                        if step in (11, 12):
                            norm_x1(b - 1, HALF[step - 11])
                    if stats and not last:
                        if step in (20, 21):
                            stats_x(b + 2, HALF[step - 20])
                        if step == 22:
                            means_x(b + 2)
                        if step in (23, 24):
                            norm_x(b + 2, HALF[step - 23])

            stats_x(0)
            means_x(0)
            norm_x(0)
            two_ones = 1 + 0x3F80 / 2.0 ** 23
            for stack in (q_stack, k_stack):
                dve.memset(stack[R_MASK:P, :, :, :].bitcast(F32), two_ones).then_inc(ones_set, 1)
            dve.memset(v_ring[:, :, :, :, HD:32], 1.0).then_inc(ones_set, 1)
            dve.wait_ge(w_loaded, 16 * 10)
            dve.wait_ge(g_ready, 2)
            dve.tensor_scalar(b_v[:, :], b_v[:, :], g_tanh[:, 0:1], None, ALU.mult).then_inc(bv_scaled, 1)
            for i in range(6):
                dve.wait_ge(qk_evac, i + 1)
                if i >= 2:
                    dve.wait_ge(parts_stored[i % 2], 16 * (i // 2))
                split3(dve, [proj_parts[:, i % 2, j, :] for j in range(PARTS)], proj[:, i % 2, :], rest[:, i % 2, :],
                       qk_split, 4 * i)
            for w in range(2):
                for i in range(32):
                    reduce_max(w, w, i)
                if w == 0:
                    join_max(0, 0)
                    evac_M(0)
                    stats_x(1)
                    means_x(1)
                    norm_x(1)
            batch(0, first=True)
            with dve.Fori(1, B - 2) as b:
                batch(b)
            batch(B - 2, stats=False)
            batch(B - 1, last=True)
            evac_O(UNITS - 1)
            stats_x1(B - 1)
            means_x1(B - 1)
            norm_x1(B - 1)
            evac_R(B - 1)
            experts_vector(dve)

        @block.gpsimd
        def _(pool):
            def rstd_x(b):
                hold(pool, agg1, QT * (b + 1))
                pool.tensor_scalar(rstd1[:, :], mv1[:, :, 1], EPS, None, ALU.add).then_inc(rstd1_step, 1)
                hold(pool, rstd1_step, 2 * b + 1)
                pool.tensor_tensor(rstd1[:, :], rstd1[:, :], minus_half[:, :], ALU.pow).then_inc(rstd1_step, 1)

            def split_Q(b, i):
                n = 6 * b + i
                hold(pool, qk_evac, n + 1)
                if not (isinstance(n, int) and n < 2):
                    hold(pool, parts_stored[i % 2], 16 * (3 * b + i // 2))
                split3(pool, [proj_parts[:, i % 2, j, :] for j in range(PARTS)], proj[:, i % 2, :], rest[:, i % 2, :],
                       qk_split, 4 * n)

            def split_M(u, g):
                hold(pool, m_evac, u + 1)
                if not (isinstance(u, int) and u == 0):
                    hold(pool, max_loaded[(g - 1) % G], 16 * PARTS * ((u - 1 - (g - 1) % G) // G + 1) if isinstance(u, int)
                                 else 16 * PARTS * mload[0])
                split3(pool, [m_parts[:, j, :] for j in range(PARTS)], m_neg[:, :], m_rest[:, :], m_split, 4 * u)

            mload = [None]

            def copy_V(b, g):
                hold(pool, v_evac, 4 * (b + 1))
                if not (isinstance(b, int) and b == 0):
                    hold(pool, pv_done, KT * (G * (b - 1) + g + 1))
                v = v_all[:, :, g * GH * HD:(g + 1) * GH * HD].rearrange("p k (h d) -> p k h d", d=HD)
                pool.tensor_tensor(v_ring[:, g, :, :, 0:HD], v,
                                   zero[:, 0:1].unsqueeze(2).unsqueeze(3).to_broadcast((P, KT, GH, HD)), ALU.add).then_inc(v_copied, 1)

            def add_x(b, g):
                if g == 0:
                    pool.wait_ge(res_loaded, 16 * (b + 1))
                    pool.tensor_tensor(x_res[:, :, :], x_res[:, :, :], b_v[:, :].unsqueeze(1).to_broadcast((P, QT, D)),
                                       ALU.add).then_inc(res_biased, 1)
                    pool.wait_ge(res_biased, b + 1)
                pool.wait_ge(o_evac, G * b + g + 1)
                o = g * GH * HD
                pool.tensor_tensor(x_res[:, :, o:o + GH * HD], x_res[:, :, o:o + GH * HD], ctx_n[:, :, :],
                                   ALU.add).then_inc(x1_added, 1)

            def rstd_x1(b):
                hold(pool, agg2, QT * (b + 1))
                pool.tensor_scalar(rstd2[:, :], mv2[:, :, 1], EPS, None, ALU.add).then_inc(rstd2_step, 1)
                pool.wait_ge(rstd2_step, 2 * b + 1)
                pool.tensor_tensor(rstd2[:, :], rstd2[:, :], minus_half[:, :], ALU.pow).then_inc(rstd2_step, 1)

            def batch(b, first=False, last=False, norm=True):
                for step in range(G * KT):
                    g, k = divmod(step, KT)
                    u = G * b + g
                    if step == 4 and not first:
                        copy_V(b, 3)
                    if step == 20 and not last:
                        copy_V(b + 1, 0)
                        copy_V(b + 1, 1)
                    if step == 28 and not last:
                        copy_V(b + 1, 2)
                    for use in plan(step, first, last):
                        if use == "M":
                            mload[0] = b + 1
                            split_M(u + 1, (g + 1) % G)
                        if use == "O":
                            if g == 0:
                                add_x(b - 1, 3)
                            else:
                                add_x(b, g - 1)
                        if use[0] == "Q":
                            split_Q(b + 1, int(use[1]))
                    if step == 7 and not first:
                        rstd_x1(b - 1)
                    if step == 22 and norm and not last:
                        rstd_x(b + 2)

            pool.memset(zero_rows[:, :], 0.0).then_inc(zero_ready, 1)
            pool.memset(ones[:, :], 1.0).then_inc(ones_ready, 1)
            pool.wait_ge(ones_ready, 1)
            pool.affine_select(out=tri[:, :], in_=ones[:, :], compare_op=ALU.is_gt, fill=0.0, base=0,
                               pattern=[[1, P]], channel_multiplier=-1).then_inc(const_ready, 1)
            pool.memset(minus_half[:, :], -0.5).then_inc(const_ready, 1)
            pool.memset(zero[:, :], 0.0).then_inc(const_ready, 1)
            pool.memset(ident[:, :], 0.0).then_inc(ident_zero, 1)
            hold(pool, ident_zero, 1)
            pool.affine_select(out=ident[:, :], in_=ident[:, :], compare_op=ALU.not_equal, fill=1.0, base=0,
                               pattern=[[-1, P]], channel_multiplier=1).then_inc(const_ready, 1)
            pool.wait_ge(const_ready, CONSTS)
            hold(pool, mask_loaded, 16)
            pool.tensor_copy(mk_parts[:, 0, :], mk[:, :]).then_inc(mask_step, 1)
            hold(pool, mask_step, 1)
            pool.tensor_tensor(mk_rest[:, :], mk[:, :], mk_parts[:, 0, :], ALU.subtract).then_inc(mask_step, 1)
            hold(pool, mask_step, 2)
            pool.tensor_copy(mk_parts[:, 1, :], mk_rest[:, :]).then_inc(mask_step, 1)
            pool.wait_ge(mask_step, 3)
            pool.tensor_tensor(mk_parts[:, 2, :], mk_rest[:, :], mk_parts[:, 1, :], ALU.subtract).then_inc(mask_step, 1)
            rstd_x(0)
            pool.wait_ge(bv_scaled, 1)
            for g in range(4):
                copy_V(0, g)
            split_M(0, 0)
            rstd_x(1)
            batch(0, first=True)
            with pool.Fori(1, B - 2) as b:
                batch(b)
            batch(B - 2, norm=False)
            batch(B - 1, last=True)
            add_x(B - 1, 3)
            rstd_x1(B - 1)
            experts_gpsimd(pool)


_INS = ['x', 'ctx_1024', 'mask_Bx1x1x4096_ff0', 'g_xattn', 'g_ffn', 'L0_xattn_Wq', 'L0_xattn_bq', 'L0_xattn_Wk',
        'L0_xattn_bk', 'L0_xattn_Wv', 'L0_xattn_bv', 'L0_ffn_Wr', 'L0_ffn_br', 'L0_ffn_W1', 'L0_ffn_b1', 'L0_ffn_g1',
        'L0_ffn_be1', 'L0_ffn_W2', 'L0_ffn_b2', 'L0_ffn_g2', 'L0_ffn_be2']
_OUTS = [((8, 512, 256), 'float32')]


def kernel(**inputs):
    import numpy as _np
    import concourse.bacc as _bacc
    from concourse import mybir as _mybir
    from concourse.bass_utils import run_bass_kernel_spmd as _run

    nc = _bacc.Bacc("TRN2", target_bir_lowering=False, num_devices=1)
    arrays, args = {}, []
    for name in _INS:
        a = _np.ascontiguousarray(inputs[name])
        arrays[f"in_{name}_dram"] = a
        args.append(nc.dram_tensor(f"in_{name}_dram", a.shape, _mybir.dt.from_np(a.dtype), kind="ExternalInput").ap())
    for i, (shape, dtype) in enumerate(_OUTS):
        dt = _mybir.dt.from_np(_np.dtype(dtype))
        args.append(nc.dram_tensor(f"out_{i}_dram", shape, dt, kind="ExternalOutput").ap())
    flamingo_kernel(nc, *args)
    r = _run(nc, [arrays], core_ids=[0])
    return r.results[0]["out_0_dram"]
```

```python
from contextlib import ExitStack

import concourse.bass as bass
from concourse import mybir

F32 = mybir.dt.float32
BF16 = mybir.dt.bfloat16
I32 = mybir.dt.int32
U32 = mybir.dt.uint32
ALU = mybir.AluOpType
ACT = mybir.ActivationFunctionType
AX = mybir.AxisListType

P = 128
B, S, D = 8, 512, 256
NH, HD = 16, 16
KEYS = 2 * S
GH = 4
G = NH // GH
KT = KEYS // P
QT = S // P
DC = D // P
UNITS = B * G
EPS = 1e-5
Q_PART = (0, 0, 1, 1, 0, 2)
K_PART = (0, 1, 0, 1, 2, 0)
PARTS = 3
PROD = len(Q_PART) * HD
R_MASK = PROD
R_MAX = R_MASK + PARTS
ROWS = R_MAX + PARTS
LOADS = 2 * len(Q_PART) + 1



E, F = 8, 1024
FC = F // P
HC = FC // 2
TOP = 2
TOKENS = B * S
TT = TOKENS // P
CONSTS = 4
SLOT_TILES = TOP * TOKENS // P + E


def carve(region, at, shape, dt=F32):
    n = 1
    for d in shape[1:]:
        n *= d
    cols = n * (2 if dt == BF16 else 4) // 4
    v = region[0:shape[0], at:at + cols]
    if dt != F32:
        v = v.bitcast(dt)
    if len(shape) == 2:
        return v
    names = "abcdefgh"[:len(shape) - 1]
    return v.rearrange(f"p ({' '.join(names)}) -> p {' '.join(names)}", **dict(zip(names, shape[1:])))


def flamingo_kernel(nc, x, ctx_in, mask, g_xattn, g_ffn, Wq, bq, Wk, bk, Wv, bv,
                    Wr, br, W1, b1, g1, be1, W2, b2, g2, be2, out):
    with ExitStack() as ctx:
        def sb(name, shape, dt=F32):
            return ctx.enter_context(nc.sbuf_tensor(name, shape, dt))

        def sem(name):
            return ctx.enter_context(nc.semaphore(name))

        def dram(name, shape, dt=F32):
            return nc.dram_tensor(name, shape, dt, kind="Internal").ap()

        q_parts = dram("q_parts", (B, PARTS, D, S), BF16)
        k_parts = dram("k_parts", (B, PARTS, D, KEYS), BF16)
        mask_parts = dram("mask_parts", (PARTS, B, KEYS), BF16)

        acc_d = dram("acc_d", (TOKENS + P, D))
        xn2_d = dram("xn2_d", (TOKENS, D))

        big = sb("big", [P, E * (DC * F + FC * D)])
        mid = sb("mid", [P, E * F])
        small = sb("small", [P, 4864])
        q_stack = carve(big, 0, [P, G, GH, S], BF16)
        k_stack = carve(big, 4096, [P, G, GH, KEYS], BF16)
        probs = carve(big, 12288, [P, 2, GH, S])
        v_ring = carve(big, 16384, [P, G, KT, GH, 32])
        v_all = carve(big, 20480, [P, KT, D])
        all_t = carve(big, 22528, [P, DC, KEYS])
        x_in = carve(big, 24576, [P, QT, D])
        c_in = carve(big, 25600, [P, QT, D])
        proj = carve(big, 26624, [P, 2, S])
        rest = carve(big, 27648, [P, 2, S])
        proj_parts = carve(big, 28672, [P, 2, PARTS, S], BF16)
        x_res = carve(small, 0, [P, QT, D])
        o_sb = carve(small, 1024, [P, S])
        ctx_n = carve(small, 1536, [P, QT, GH * HD])
        xn2 = carve(small, 1792, [P, QT, D])
        xn2_t = carve(small, 2816, [P, DC, S])
        wq, wk, wv = (carve(big, 30208 + 512 * i, [P, DC, D]) for i in range(3))
        wr = sb("wr", [P, DC, E]); b_r = sb("b_r", [P, E])
        logits = carve(small, 4352, [P, TT, E])
        gf_raw = sb("gf_raw", [P, 1]); gf_tanh = sb("gf_tanh", [P, 1])
        b_q = sb("b_q", [P, DC]); b_qs = sb("b_qs", [P, DC]); b_k = sb("b_k", [P, DC])
        b_v = carve(small, 4096, [P, D])
        ident = sb("ident", [P, P])
        g_raw = sb("g_raw", [P, 1]); g_tanh = sb("g_tanh", [P, 1])
        stat1 = sb("stat1", [P, QT, 6]); mv1 = sb("mv1", [P, QT, 2]); rstd1 = sb("rstd1", [P, QT])
        minus_half = sb("minus_half", [P, QT]); zero = sb("zero", [P, 1])
        stat2 = sb("stat2", [P, QT, 6]); mv2 = sb("mv2", [P, QT, 2]); rstd2 = sb("rstd2", [P, QT])
        m_half = carve(big, 31744, [P, 2, GH * QT * 2]); m_row = carve(big, 31808, [P, GH * QT])
        m_neg = carve(big, 31824, [GH * QT, P]); m_rest = carve(big, 31952, [GH * QT, P])
        m_parts = carve(big, 32080, [GH * QT, PARTS, P], BF16)
        r_sum = sb("r_sum", [P, QT, GH]); r_scl = sb("r_scl", [P, QT, GH])
        mk = carve(big, 32272, [64, P]); mk_rest = carve(big, 32400, [64, P]); mk_parts = carve(big, 32528, [64, PARTS, P], BF16)

        ps_t = ctx.enter_context(nc.psum_tensor("ps_t", [P, GH, S], F32))
        ps_s = ctx.enter_context(nc.psum_tensor("ps_s", [P, 2, S], F32))
        ps_o = ctx.enter_context(nc.psum_tensor("ps_o", [P, S], F32))
        ps_m = ctx.enter_context(nc.psum_tensor("ps_m", [P, S], F32))

        x_loaded = sem("x_loaded"); c_loaded = sem("c_loaded"); w_loaded = sem("w_loaded")
        const_ready = sem("const_ready"); ident_zero = sem("ident_zero"); bq_scaled = sem("bq_scaled"); bv_scaled = sem("bv_scaled"); res_biased = sem("res_biased"); g_ready = sem("g_ready")
        mask_loaded = sem("mask_loaded"); mask_step = sem("mask_step"); mask_stored = sem("mask_stored")
        stats1 = sem("stats1"); agg1 = sem("agg1"); rstd1_step = sem("rstd1_step"); x_normed = sem("x_normed")
        t_ready = sem("t_ready"); t_evac = sem("t_evac")
        qk_ready = sem("qk_ready"); qk_evac = sem("qk_evac"); qk_split = sem("qk_split"); parts_stored = [sem(f"parts_stored{h}") for h in range(2)]
        v_ready = sem("v_ready"); v_evac = sem("v_evac"); v_copied = sem("v_copied")
        stack_loaded = [sem(f"stack_loaded{g}") for g in range(G)]
        s_ready = sem("s_ready"); s_used = sem("s_used"); m_reduced = sem("m_reduced")
        m_ready = sem("m_ready"); m_evac = sem("m_evac"); m_split = sem("m_split")
        max_loaded = [sem(f"max_loaded{g}") for g in range(G)]
        st_ready = sem("st_ready"); exp_done = sem("exp_done"); pv_done = sem("pv_done")
        o_copied = sem("o_copied"); o_ready = sem("o_ready"); o_recip = sem("o_recip"); o_scaled = sem("o_scaled"); o_evac = sem("o_evac")
        res_loaded = sem("res_loaded"); x1_added = sem("x1_added")
        stats2 = sem("stats2"); agg2 = sem("agg2"); rstd2_step = sem("rstd2_step"); x1_normed = sem("x1_normed")
        x1_stored = sem("x1_stored"); xn2_stored = sem("xn2_stored")
        l_ready = sem("l_ready"); l_evac = sem("l_evac"); r_ready = sem("r_ready"); r_evac = sem("r_evac")
        ones_ready = sem("ones_ready"); ones_set = sem("ones_set");

        x_v = x.rearrange("b (t p) d -> b p t d", p=P)
        c_v = ctx_in.rearrange("b (t p) d -> b p t d", p=P)
        xn2_v = xn2_d.rearrange("(b t p) d -> b p t d", t=QT, p=P)
        x1_v = acc_d[0:TOKENS, :].rearrange("(b t p) d -> b p t d", t=QT, p=P)

        PLAN = {0: ["T0"], 1: ["M", "T1"], 2: ["O", "T2"], 3: ["T3"], 4: ["Q0"], 5: ["Q1"], 6: ["Q2"],
                7: ["Q3"], 8: ["Q4"], 9: ["M", "Q5"], 10: ["O"], 11: ["V0"], 12: ["V1"], 13: ["V2"], 14: ["V3"],
                17: ["M"], 18: ["O"], 19: ["L0"], 20: ["L1"], 22: ["R"], 25: ["M"], 26: ["O"]}

        def plan(step, first, last):
            for use in PLAN.get(step, []):
                if use[0] in "TQV" and last:
                    continue
                if use == "M" and last and step >= 24:
                    continue
                if first and (use == "O" and step < 8 or use[0] in "LR"):
                    continue
                yield use

        w1_sb = carve(big, 0, [P, E, DC, F])
        w2_sb = carve(big, E * DC * F, [P, E, FC, D])
        b1_bc = carve(mid, 0, [P, E, F])
        h_sb = carve(small, 0, [P, 2, F])
        ht_sb = carve(small, 2048, [P, FC, P])
        x_sb = carve(small, 3072, [P, 2, D])
        xt_sb = carve(small, 3584, [P, 2, DC, P])
        y_sb = carve(small, 4096, [P, 3, D])
        late = sb("late", [P, 3 * E * D])
        g2_bc, be2_bc, b2_bc = (carve(late, i * E * D, [P, E, D]) for i in range(3))
        is_lane = carve(late, 0, [P, 2, TOP, QT, P])
        in_tile = carve(late, 2048, [P, 2, TOP, QT, SLOT_TILES])
        slot_of = carve(late, 3200, [P, 2, TOP, QT, 2, SLOT_TILES])
        gb_rows = carve(small, 3840, [E * FC, 2, P])
        g1_t = sb("g1_t", [P, 2, E * FC])
        h_stat = sb("h_stat", [P, 2, 6]); h_mv = sb("h_mv", [P, 2, 2]); h_rstd = sb("h_rstd", [P, 2])
        y_stat = sb("y_stat", [P, 6]); y_mv = sb("y_mv", [P, 2]); y_rstd = sb("y_rstd", [P, 1])
        ra, rb, rc, one1, one2, base_a, base_b = (carve(small, 256 * i, [P, TT, E]) for i in range(7))
        rank = carve(small, 1792, [P, E]); rank_i = carve(small, 1800, [P, E], I32)
        step_f = carve(small, 1808, [P, TT]); step_i = carve(small, 1840, [P, TT], I32)
        slot_f = carve(small, 1872, [P, SLOT_TILES]); slot_i = carve(small, 1952, [P, SLOT_TILES], I32)
        top1, top2, den, best = (carve(small, 2048 + 32 * i, [P, TT]) for i in range(4))
        tiles_e, start_a, start_b, count_e = (carve(small, 2176 + 8 * i, [P, E]) for i in range(4))
        more = carve(small, 2304, [P, E, TT])
        owner = carve(small, 2560, [P, SLOT_TILES, E])
        pos_f = carve(small, 3200, [P, TOP, TT]); owner_f = carve(small, 3264, [P, SLOT_TILES])
        lane_i = carve(small, 3336, [P, P], I32); lane_f = carve(small, 3464, [P, P])
        low_i, high_i = (carve(small, 3592 + 64 * i, [P, TOP, TT], U32) for i in range(2))
        low_f, high_f = (carve(small, 3720 + 64 * i, [P, TOP, TT]) for i in range(2))
        token_i = carve(small, 3848, [P, TT], I32); token_f = carve(small, 3880, [P, TT])
        slot_tok = sb("slot_tok", [P, SLOT_TILES]); slot_gate = sb("slot_gate", [P, SLOT_TILES])
        x_idx = sb("x_idx", [P, 2], U32); y_idx = sb("y_idx", [P, 2], U32); slot_dst = sb("slot_dst", [P, SLOT_TILES])
        no_token = carve(small, 3912, [P, SLOT_TILES]); spare_i = carve(small, 3984, [P, 1], I32); spare_f = carve(small, 3985, [P, 1])
        oh = sb("oh", [P, TT, E], BF16); tri = sb("tri", [P, P], BF16); ones = sb("ones", [P, P], BF16)
        pos = sb("pos", [P, TOP, TT], U32)
        owner_i = sb("owner_i", [1, SLOT_TILES], I32)
        w_top = sb("w_top", [P, TOP, TT])

        bc_loaded = sem("bc_loaded"); w1_loaded = sem("w1_loaded"); gb_loaded = sem("gb_loaded")
        gb_ready = sem("gb_ready"); gb_evac = sem("gb_evac")
        iota_step = sem("iota_step"); found = sem("found"); valued = sem("valued"); turned = sem("turned"); slots_ready = sem("slots_ready"); idx_ready = sem("idx_ready"); route = sem("route"); route_exp = sem("route_exp")
        counted = sem("counted"); oh_ready = sem("oh_ready"); routed = sem("routed")
        x_got = [sem(f"x_got{h}") for h in range(2)]
        xt_ready = sem("xt_ready"); xt_evac = sem("xt_evac")
        h_ready = sem("h_ready"); h_biased = sem("h_biased"); h_relu = sem("h_relu"); h_stats = sem("h_stats")
        h_agg = sem("h_agg"); h_pow = sem("h_pow"); h_normed = sem("h_normed")
        ht_ready = sem("ht_ready"); ht_scaled = sem("ht_scaled"); ht_done = sem("ht_done")
        y_ready = sem("y_ready"); y_biased = sem("y_biased"); y_relu = sem("y_relu"); y_stats = sem("y_stats")
        y_agg = sem("y_agg"); y_pow = sem("y_pow"); y_normed = sem("y_normed"); y_scaled = sem("y_scaled"); y_done = sem("y_done")
        y_gated = sem("y_gated"); y_added = sem("y_added")
        spare_stored = sem("spare_stored"); out_stored = sem("out_stored")
        ps_h = [ps_t[:, 0:2, :], ps_t[:, 2:4, :]]
        ps_ht = ps_s
        ps_y = ps_o[:, 0:D]
        ps_x = ps_m[:, 0:D]
        LAST = SLOT_TILES

        def tiles(eng, step):
            for j in range(4):
                step(j)
            with eng.Fori(2, SLOT_TILES // 2 - 2) as i:
                step(2 * i, 0); step(2 * i + 1, 1)
            for j in range(SLOT_TILES - 4, SLOT_TILES):
                step(j)

        def experts_sync(sp):
            sp.wait_ge(pv_done, KT * UNITS)
            load_w1(1); load_w2(1); load_w1(5); load_w1(6); load_w1(7)
            sp.wait_ge(turned, B)
            sp.wait_ge(x_got[1], 16)
            for i, (t, v) in enumerate(((b2_bc, b2), (g2_bc, g2), (be2_bc, be2))):
                sp.dma_start(t[:, :, :], v.partition_broadcast(P)).then_inc(bc_loaded, 16)
                sp.wait_ge(bc_loaded, 16 * (i + 1))

            sp.wait_ge(y_added, 16 * SLOT_TILES)
            sp.dma_start(out.rearrange("b s d -> (b s) d"), acc_d[0:TOKENS, :]).then_inc(out_stored, 16)
            sp.wait_ge(out_stored, 16)

        def load_w1(e):
            nc.sync.dma_start(w1_sb[:, e, :, :], W1[e].rearrange("(c p) f -> p c f", p=P)).then_inc(w1_loaded, 16)

        def load_w2(e):
            nc.sync.dma_start(w2_sb[:, e, :, :], W2[e].rearrange("(c p) d -> p c d", p=P)).then_inc(w1_loaded, 16)

        def expert_of(eng, j):
            return eng.value_load(owner_i[0:1, bass.ds(j, 1)], min_val=0, max_val=E - 1)

        def experts_tensor(pe):
            pe.wait_ge(oh_ready, 1)
            pe.wait_ge(r_evac, B)
            pe.matmul(ps_o[:, 0:TT * E], tri[:, :], oh[:, :, :], start=True, stop=True).then_inc(counted, 1)
            pe.matmul(ps_m[:, 0:TT * E], ones[:, :], oh[:, :, :], start=True, stop=True).then_inc(counted, 1)
            for b in range(B):
                pe.wait_ge(found, 3 * (b + 1))
                pe.wait_ge(valued, b + 1)
                for k in range(TOP):
                    for t in range(QT):
                        mm = pe.matmul(ps_t[:, 0, 0:2 * SLOT_TILES], is_lane[:, b % 2, k, t, :], slot_of[:, b % 2, k, t, :, :],
                                       start=(b + k + t == 0), stop=(b == B - 1 and k == TOP - 1 and t == QT - 1))
                mm.then_inc(turned, 1)

            def turn_x(j, par):
                if isinstance(j, int) and j >= SLOT_TILES:
                    return
                pe.wait_ge(x_got[par], 16 * (j // 2 + 1) if isinstance(j, int) else 16 * half[0])
                if not (isinstance(j, int) and j == 0):
                    pe.wait_ge(xt_evac, j)
                for k in range(DC):
                    mm = pe.transpose(ps_x[:, k * P:(k + 1) * P], x_sb[:, par, k * P:(k + 1) * P], ident[:, :])
                mm.then_inc(xt_ready, 1)

            half = [None]

            def up(j, par):
                if isinstance(j, int) and j >= SLOT_TILES:
                    return
                e = expert_of(pe, j)
                pe.wait_ge(xt_evac, j + 1)
                if not (isinstance(j, int) and j < 2):
                    pe.wait_ge(h_biased, j - 1)
                for n in range(2):
                    for k in range(DC):
                        mm = pe.matmul(ps_h[par][:, n, :], xt_sb[:, par, k, :], w1_sb[:, e, k, n * 512:(n + 1) * 512],
                                       start=(k == 0), stop=(k == DC - 1))
                mm.then_inc(h_ready, 1)

            def turn_h(j, par):
                pe.wait_ge(h_normed, j + 1)
                if not (isinstance(j, int) and j == 0):
                    pe.wait_ge(ht_scaled, 2 * j)
                for c in range(FC):
                    mm = pe.transpose(ps_ht[:, c // 4, c % 4 * P:(c % 4 + 1) * P], h_sb[:, par, c * P:(c + 1) * P], ident[:, :])
                mm.then_inc(ht_ready, 1)

            def down(j):
                e = expert_of(pe, j)
                if not (isinstance(j, int) and j == 0):
                    pe.wait_ge(y_biased, j)
                for c in range(FC):
                    if c % HC == 0:
                        pe.wait_ge(ht_done, 2 * j + c // HC + 1)
                    mm = pe.matmul(ps_y, ht_sb[:, c, :], w2_sb[:, e, c, :], start=(c == 0), stop=(c == FC - 1))
                mm.then_inc(y_ready, 1)

            turn_x(0, 0)
            turn_x(1, 1)
            pe.wait_ge(w1_loaded, 16 * (2 * E + 1))
            pe.wait_ge(slots_ready, 3)
            up(0, 0)
            turn_x(2, 0)
            up(1, 1)

            def plain(j, par_):
                turn_h(j, par_)
                up(j + 2, par_)
                turn_x(j + 3, 1 - par_)
                down(j)

            plain(0, 0)
            plain(1, 1)
            with pe.Fori(1, SLOT_TILES // 2 - 2) as i:
                half[0] = i + 2
                plain(2 * i, 0)
                half[0] = i + 3
                plain(2 * i + 1, 1)
            for j in range(SLOT_TILES - 4, SLOT_TILES):
                plain(j, j % 2)

        def experts_scalar(act):
            act.wait_ge(route, 3)
            act.activation(rb[:, :, :], ra[:, :, :], ACT.Exp).then_inc(route_exp, 1)

            def evac_x(j, par):
                if isinstance(j, int) and j >= SLOT_TILES:
                    return
                act.wait_ge(xt_ready, j + 1)
                if not (isinstance(j, int) and j < 2):
                    act.wait_ge(h_ready, j - 1)
                act.activation(xt_sb[:, par, :, :], ps_x.rearrange("p (k t) -> p k t", k=DC), ACT.Copy).then_inc(xt_evac, 1)

            def relu_h(j, par):
                if isinstance(j, int) and j >= SLOT_TILES:
                    return
                act.wait_ge(h_biased, j + 1)
                act.activation(h_sb[:, par, :], h_sb[:, par, :], ACT.Relu).then_inc(h_relu, 1)

            def relu_y(j):
                act.wait_ge(y_biased, j + 1)
                act.activation(y_sb[:, 0, :], y_sb[:, 0, :], ACT.Relu).then_inc(y_relu, 1)

            def pick_x(j, par):
                if isinstance(j, int) and j >= SLOT_TILES:
                    return
                if not (isinstance(j, int) and j < 2):
                    act.wait_ge(xt_ready, j - 1)
                act.activation(x_idx[:, par:par + 1], slot_tok[:, bass.ds(j, 1)], ACT.Copy).then_inc(idx_ready, 1)

            def gate_y(j, par):
                act.wait_ge(y_done, j + 1)
                act.activation(y_sb[:, 1 + par, :], y_sb[:, 1 + par, :], ACT.Copy,
                               scale=slot_gate[:, bass.ds(j, 1)]).then_inc(y_gated, 1)
                if not (isinstance(j, int) and j < 2):
                    act.wait_ge(y_added, 16 * (j - 1))
                act.activation(y_idx[:, par:par + 1], slot_dst[:, bass.ds(j, 1)], ACT.Copy).then_inc(y_gated, 1)

            act.wait_ge(slots_ready, 3)
            pick_x(0, 0)
            pick_x(1, 1)
            evac_x(0, 0)
            pick_x(2, 0)
            evac_x(1, 1)
            pick_x(3, 1)
            evac_x(2, 0)
            relu_h(0, 0)
            relu_h(1, 1)

            def step(j, par=None):
                par = j % 2 if par is None else par
                if not (isinstance(j, int) and j < 2):
                    gate_y(j - 2, par)
                pick_x(j + 4, par)
                if not (isinstance(j, int) and j == 0):
                    relu_y(j - 1)
                evac_x(j + 3, 1 - par)
                relu_h(j + 2, par)

            tiles(act, step)
            gate_y(SLOT_TILES - 2, 0)
            relu_y(SLOT_TILES - 1)
            gate_y(SLOT_TILES - 1, 1)

        def experts_vector(dve):
            n = [0]

            def chain(ins):
                n[0] += 1
                ins.then_inc(route, 1)
                dve.wait_ge(route, n[0])

            def over_e(t):
                return t.unsqueeze(2).to_broadcast((P, TT, E))

            def over_t(t):
                return t.unsqueeze(1).to_broadcast((P, TT, E))

            dve.wait_ge(r_evac, B)
            dve.wait_ge(xn2_stored, 16 * B)
            dve.wait_ge(x1_stored, 16 * B)
            dve.wait_ge(iota_step, 6)
            chain(dve.tensor_tensor(ra[:, :, :], logits[:, :, :], over_t(b_r[:, :]), ALU.add))
            chain(dve.tensor_reduce(best[:, :], ra[:, :, :], AX.X, ALU.max))
            chain(dve.tensor_tensor(ra[:, :, :], ra[:, :, :], over_e(best[:, :]), ALU.subtract))
            dve.tensor_copy(rank[:, :], rank_i[:, :]).then_inc(route, 1)
            dve.tensor_copy(step_f[:, :], step_i[:, :]).then_inc(route, 1)
            dve.tensor_copy(lane_f[:, :], lane_i[:, :]).then_inc(route, 1)
            dve.tensor_copy(token_f[:, :], token_i[:, :]).then_inc(route, 1)
            dve.tensor_copy(spare_f[:, :], spare_i[:, :]).then_inc(route, 1)
            n[0] += 5
            chain(dve.tensor_copy(slot_f[:, :], slot_i[:, :]))
            dve.wait_ge(route_exp, 1)
            chain(dve.tensor_reduce(den[:, :], rb[:, :, :], AX.X, ALU.add))
            chain(dve.reciprocal(den[:, :], den[:, :]))
            chain(dve.tensor_tensor(rb[:, :, :], rb[:, :, :], over_e(den[:, :]), ALU.mult))
            for top, one in ((top1, one1), (top2, one2)):
                chain(dve.tensor_reduce(top[:, :], rb[:, :, :], AX.X, ALU.max))
                chain(dve.tensor_tensor(rc[:, :, :], rb[:, :, :], over_e(top[:, :]), ALU.is_equal))
                chain(dve.tensor_tensor(rc[:, :, :], rc[:, :, :], over_t(rank[:, :]), ALU.mult))
                chain(dve.tensor_reduce(best[:, :], rc[:, :, :], AX.X, ALU.max))
                chain(dve.tensor_tensor(one[:, :, :], rc[:, :, :], over_e(best[:, :]), ALU.is_equal))
                if one is one1:
                    chain(dve.scalar_tensor_tensor(rb[:, :, :], one1[:, :, :], -2.0, rb[:, :, :], ALU.mult, ALU.add))
            dve.tensor_tensor(oh[:, :, :], one1[:, :, :], one2[:, :, :], ALU.add).then_inc(oh_ready, 1)
            chain(dve.tensor_tensor(den[:, :], top1[:, :], top2[:, :], ALU.add))
            chain(dve.reciprocal(den[:, :], den[:, :]))
            for k, top in enumerate((top1, top2)):
                chain(dve.tensor_tensor(top[:, :], top[:, :], den[:, :], ALU.mult))
                chain(dve.tensor_scalar(w_top[:, k, :], top[:, :], gf_tanh[:, 0:1], None, ALU.mult))
            dve.wait_ge(counted, 2)
            chain(dve.tensor_copy(base_a[:, :, :], ps_m[:, 0:TT * E].rearrange("p (t e) -> p t e", e=E)))
            chain(dve.tensor_copy(rc[:, :, :], base_a[:, :, :]))
            a, b_, reach = base_a, base_b, 1
            while reach < TT:
                dve.tensor_copy(b_[:, 0:reach, :], a[:, 0:reach, :]).then_inc(route, 1)
                n[0] += 1
                chain(dve.tensor_tensor(b_[:, reach:TT, :], a[:, reach:TT, :], a[:, 0:TT - reach, :], ALU.add))
                a, b_, reach = b_, a, 2 * reach
            chain(dve.tensor_copy(count_e[:, :], a[:, TT - 1, :]))
            chain(dve.tensor_tensor(b_[:, :, :], a[:, :, :], rc[:, :, :], ALU.subtract))
            chain(dve.tensor_tensor(more[:, :, :], count_e[:, :].unsqueeze(2).to_broadcast((P, E, TT)),
                                    step_f[:, :].unsqueeze(1).to_broadcast((P, E, TT)), ALU.is_gt))
            chain(dve.tensor_reduce(tiles_e[:, :], more[:, :, :], AX.X, ALU.add))
            chain(dve.memset(start_a[:, 0:1], 0.0))
            chain(dve.tensor_copy(start_a[:, 1:E], tiles_e[:, 0:E - 1]))
            c, d, reach = start_a, start_b, 1
            while reach < E:
                dve.tensor_copy(d[:, 0:reach], c[:, 0:reach]).then_inc(route, 1)
                n[0] += 1
                chain(dve.tensor_tensor(d[:, reach:E], c[:, reach:E], c[:, 0:E - reach], ALU.add))
                c, d, reach = d, c, 2 * reach
            chain(dve.scalar_tensor_tensor(b_[:, :, :], over_t(c[:, :]), float(P), b_[:, :, :], ALU.mult, ALU.add))
            chain(dve.tensor_tensor(b_[:, :, :], b_[:, :, :], ps_o[:, 0:TT * E].rearrange("p (t e) -> p t e", e=E), ALU.add))
            for k, one in enumerate((one1, one2)):
                chain(dve.tensor_tensor(rc[:, :, :], one[:, :, :], b_[:, :, :], ALU.mult))
                chain(dve.tensor_reduce(pos_f[:, k, :], rc[:, :, :], AX.X, ALU.add))
            chain(dve.tensor_copy(pos[:, :, :], pos_f[:, :, :]))
            dve.tensor_scalar(low_i[:, :, :], pos[:, :, :], P - 1, None, ALU.bitwise_and).then_inc(route, 1)
            dve.tensor_scalar(high_i[:, :, :], pos[:, :, :], 7, None, ALU.logical_shift_right).then_inc(route, 1)
            n[0] += 2
            dve.wait_ge(route, n[0])
            dve.tensor_copy(low_f[:, :, :], low_i[:, :, :]).then_inc(route, 1)
            dve.tensor_copy(high_f[:, :, :], high_i[:, :, :]).then_inc(route, 1)
            n[0] += 2
            dve.wait_ge(route, n[0])
            for b in range(B):
                if b >= 2:
                    dve.wait_ge(turned, b - 1)
                t0, par = b * QT, b % 2
                dve.tensor_tensor(in_tile[:, par], slot_f[:, :].unsqueeze(1).unsqueeze(2).to_broadcast((P, TOP, QT, SLOT_TILES)),
                                  high_f[:, :, t0:t0 + QT].unsqueeze(3).to_broadcast((P, TOP, QT, SLOT_TILES)),
                                  ALU.is_equal).then_inc(found, 1)
                dve.tensor_tensor(is_lane[:, par], lane_f[:, :].unsqueeze(1).unsqueeze(2).to_broadcast((P, TOP, QT, P)),
                                  low_f[:, :, t0:t0 + QT].unsqueeze(3).to_broadcast((P, TOP, QT, P)),
                                  ALU.is_equal).then_inc(found, 1)
                dve.wait_ge(found, 3 * b + 1)
                dve.tensor_tensor(slot_of[:, par, :, :, 1, :], in_tile[:, par],
                                  w_top[:, :, t0:t0 + QT].unsqueeze(3).to_broadcast((P, TOP, QT, SLOT_TILES)),
                                  ALU.mult).then_inc(found, 1)
            chain(dve.tensor_tensor(owner[0:1, :, 1:E], slot_f[0:1, :].unsqueeze(2).to_broadcast((1, SLOT_TILES, E - 1)),
                                    c[0:1, 1:E].unsqueeze(1).to_broadcast((1, SLOT_TILES, E - 1)), ALU.is_ge))
            chain(dve.tensor_reduce(owner_f[0:1, :], owner[0:1, :, 1:E], AX.X, ALU.add))
            dve.tensor_copy(owner_i[:, :], owner_f[0:1, :]).then_inc(routed, 1)
            dve.wait_ge(turned, B)
            dve.tensor_scalar(slot_tok[:, :], ps_t[:, 0, 0:SLOT_TILES], 1.0, 0.0, ALU.subtract, ALU.max).then_inc(slots_ready, 1)
            dve.tensor_copy(slot_gate[:, :], ps_t[:, 0, SLOT_TILES:2 * SLOT_TILES]).then_inc(slots_ready, 1)
            chain(dve.tensor_scalar(no_token[:, :], ps_t[:, 0, 0:SLOT_TILES], 0.0, spare_f[:, 0:1], ALU.is_equal, ALU.mult))
            dve.scalar_tensor_tensor(slot_dst[:, :], ps_t[:, 0, 0:SLOT_TILES], -1.0, no_token[:, :],
                                     ALU.add, ALU.add).then_inc(slots_ready, 1)
            dve.wait_ge(routed, 1)
            dve.wait_ge(w1_loaded, 16 * (2 * E + 1))

            def bias_h(j, par):
                if isinstance(j, int) and j >= SLOT_TILES:
                    return
                e = expert_of(dve, j)
                dve.wait_ge(h_ready, j + 1)
                if not (isinstance(j, int) and j < 2):
                    dve.wait_ge(ht_ready, j - 1)
                dve.tensor_tensor(h_sb[:, par, :].rearrange("p (n f) -> p n f", n=2), ps_h[par],
                                  b1_bc[:, e, :].rearrange("p (n f) -> p n f", n=2), ALU.add).then_inc(h_biased, 1)

            def stats_h(j, par):
                if isinstance(j, int) and j >= SLOT_TILES:
                    return
                hold(dve, h_relu, j + 1)
                for i in range(2):
                    dve.bn_stats(h_stat[:, i, :], h_sb[:, par, i * 512:(i + 1) * 512]).then_inc(h_stats, 1)
                hold(dve, h_stats, 2 * (j + 1))
                dve.bn_aggr(h_mv[:, par, :], h_stat[:, :, :]).then_inc(h_agg, 1)

            def norm_h(j, par):
                if isinstance(j, int) and j >= SLOT_TILES:
                    return
                dve.wait_ge(h_pow, 2 * (j + 1))
                dve.tensor_scalar(h_sb[:, par, :], h_sb[:, par, :], h_mv[:, par, 0:1], h_rstd[:, par:par + 1],
                                  ALU.subtract, ALU.mult).then_inc(h_normed, 1)

            def scale_ht(j):
                e = expert_of(dve, j)
                dve.wait_ge(ht_ready, j + 1)
                if not (isinstance(j, int) and j == 0):
                    dve.wait_ge(y_ready, j)
                for i in range(2):
                    dve.tensor_tensor(ht_sb[:, i * HC:(i + 1) * HC, :], ps_ht[:, i, :].rearrange("p (c t) -> p c t", t=P),
                                      g1_t[:, 0, bass.ds(e * FC + i * HC, HC)].unsqueeze(2).to_broadcast((P, HC, P)),
                                      ALU.mult).then_inc(ht_scaled, 1)

            def bias_y(j):
                e = expert_of(dve, j)
                dve.wait_ge(y_ready, j + 1)
                if isinstance(j, int) and j == 0:
                    dve.wait_ge(bc_loaded, 16)
                else:
                    dve.wait_ge(y_scaled, j)
                dve.tensor_tensor(y_sb[:, 0, :], ps_y, b2_bc[:, e, :], ALU.add).then_inc(y_biased, 1)

            def stats_y(j):
                hold(dve, y_relu, j + 1)
                dve.bn_stats(y_stat[:, :], y_sb[:, 0, :]).then_inc(y_stats, 1)
                hold(dve, y_stats, j + 1)
                dve.bn_aggr(y_mv[:, :], y_stat[:, :]).then_inc(y_agg, 1)

            def norm_y(j):
                dve.wait_ge(y_pow, 2 * (j + 1))
                dve.tensor_scalar(y_sb[:, 0, :], y_sb[:, 0, :], y_mv[:, 0:1], y_rstd[:, 0:1],
                                  ALU.subtract, ALU.mult).then_inc(y_normed, 1)

            bias_h(0, 0)
            stats_h(0, 0)
            bias_h(1, 1)
            norm_h(0, 0)
            stats_h(1, 1)

            def step(j, par=None):
                par = j % 2 if par is None else par
                after = not (isinstance(j, int) and j == 0)
                scale_ht(j)
                if after:
                    bias_y(j - 1)
                norm_h(j + 1, 1 - par)
                bias_h(j + 2, par)
                if after:
                    stats_y(j - 1)
                stats_h(j + 2, par)
                if after:
                    norm_y(j - 1)

            tiles(dve, step)
            bias_y(SLOT_TILES - 1)
            stats_y(SLOT_TILES - 1)
            norm_y(SLOT_TILES - 1)

        def experts_gpsimd(pool):
            pool.wait_ge(xn2_stored, 16 * B)
            pool.wait_ge(x1_stored, 16 * B)
            pool.wait_ge(spare_stored, 16)
            pool.wait_ge(r_ready, B)
            pool.iota(rank_i[:, :], pattern=[[-1, E]], base=E, channel_multiplier=0).then_inc(iota_step, 1)
            pool.iota(step_i[:, :], pattern=[[P, TT]], base=0, channel_multiplier=0).then_inc(iota_step, 1)
            pool.iota(slot_i[:, :], pattern=[[1, SLOT_TILES]], base=0, channel_multiplier=0).then_inc(iota_step, 1)
            pool.iota(lane_i[:, :], pattern=[[1, P]], base=0, channel_multiplier=0).then_inc(iota_step, 1)
            pool.iota(spare_i[:, :], pattern=[[1, 1]], base=TOKENS + 1, channel_multiplier=1).then_inc(iota_step, 1)
            pool.iota(token_i[:, :], pattern=[[P, TT]], base=1, channel_multiplier=1).then_inc(iota_step, 1)
            for b in range(B):
                pool.wait_ge(found, 3 * b + 1)
                if b >= 2:
                    pool.wait_ge(turned, b - 1)
                t0, par = b * QT, b % 2
                pool.tensor_tensor(slot_of[:, par, :, :, 0, :], in_tile[:, par],
                                   token_f[:, t0:t0 + QT].unsqueeze(1).unsqueeze(3).to_broadcast((P, TOP, QT, SLOT_TILES)),
                                   ALU.mult).then_inc(valued, 1)

            def gather_x(j, par):
                if isinstance(j, int) and j >= SLOT_TILES:
                    return
                hold(pool, idx_ready, j + 1)
                pool.indirect_dma_start(out=x_sb[:, par, :], out_offset=None, in_=xn2_d,
                                        in_offset=bass.IndirectOffsetOnAxis(ap=x_idx[:, par:par + 1], axis=0)
                                        ).then_inc(x_got[par], 16)

            for j in range(4):
                gather_x(j, j % 2)

            def pow_h(j, par):
                if isinstance(j, int) and j >= SLOT_TILES:
                    return
                hold(pool, h_agg, j + 1)
                pool.tensor_scalar(h_rstd[:, par:par + 1], h_mv[:, par, 1:2], EPS, None, ALU.add).then_inc(h_pow, 1)
                pool.wait_ge(h_pow, 2 * j + 1)
                pool.tensor_tensor(h_rstd[:, par:par + 1], h_rstd[:, par:par + 1], minus_half[:, 0:1], ALU.pow).then_inc(h_pow, 1)

            def shift_ht(j):
                e = expert_of(pool, j)
                for i in range(2):
                    pool.wait_ge(ht_scaled, 2 * j + i + 1)
                    h = ht_sb[:, i * HC:(i + 1) * HC, :]
                    pool.tensor_tensor(h, h, g1_t[:, 1, bass.ds(e * FC + i * HC, HC)].unsqueeze(2).to_broadcast((P, HC, P)),
                                       ALU.add).then_inc(ht_done, 1)

            def pow_y(j):
                hold(pool, y_agg, j + 1)
                pool.tensor_scalar(y_rstd[:, :], y_mv[:, 1:2], EPS, None, ALU.add).then_inc(y_pow, 1)
                pool.wait_ge(y_pow, 2 * j + 1)
                pool.tensor_tensor(y_rstd[:, :], y_rstd[:, :], minus_half[:, 0:1], ALU.pow).then_inc(y_pow, 1)

            def scale_y(j, par):
                e = expert_of(pool, j)
                if isinstance(j, int) and j == 0:
                    pool.wait_ge(bc_loaded, 48)
                pool.wait_ge(y_normed, j + 1)
                if not (isinstance(j, int) and j < 2):
                    pool.wait_ge(y_added, 16 * (j - 1))
                y = y_sb[:, 1 + par, :]
                pool.tensor_tensor(y, y_sb[:, 0, :], g2_bc[:, e, :], ALU.mult).then_inc(y_scaled, 1)
                pool.wait_ge(y_scaled, j + 1)
                pool.tensor_tensor(y, y, be2_bc[:, e, :], ALU.add).then_inc(y_done, 1)

            def add_y(j, par):
                hold(pool, y_gated, 2 * (j + 1))
                if not (isinstance(j, int) and j == 0):
                    hold(pool, y_added, 16 * j)
                pool.indirect_dma_start(out=acc_d, out_offset=bass.IndirectOffsetOnAxis(ap=y_idx[:, par:par + 1], axis=0),
                                        in_=y_sb[:, 1 + par, :], in_offset=None, compute_op=ALU.add).then_inc(y_added, 16)

            pow_h(0, 0)
            pow_h(1, 1)

            def step(j, par=None):
                par = j % 2 if par is None else par
                after = not (isinstance(j, int) and j == 0)
                shift_ht(j)
                gather_x(j + 4, par)
                if not (isinstance(j, int) and j < 2):
                    add_y(j - 2, par)
                if after:
                    pow_y(j - 1)
                pow_h(j + 2, par)
                if after:
                    scale_y(j - 1, 1 - par)

            tiles(pool, step)
            pow_y(SLOT_TILES - 1)
            add_y(SLOT_TILES - 2, 0)
            scale_y(SLOT_TILES - 1, 1)
            add_y(SLOT_TILES - 1, 1)

        hold_reg = {}

        def hold(eng, semaphore, count):
            if isinstance(count, int):
                eng.wait_ge(semaphore, count)
            else:
                if eng.engine not in hold_reg:
                    hold_reg[eng.engine] = eng.alloc_register(f"hold_{len(hold_reg)}")
                eng.reg_mov(hold_reg[eng.engine], count)
                eng.wait_ge(const_ready, CONSTS)
                eng.wait_ge(semaphore, hold_reg[eng.engine])

        def split3(eng, dst, src, tmp, step, at):
            none = zero[0:src.shape[0], 0:1].to_broadcast(src.shape)
            eng.tensor_tensor(dst[0], src, none, ALU.add).then_inc(step, 1)
            hold(eng, step, at + 1)
            eng.tensor_tensor(tmp, src, dst[0], ALU.subtract).then_inc(step, 1)
            hold(eng, step, at + 2)
            eng.tensor_tensor(dst[1], tmp, none, ALU.add).then_inc(step, 1)
            hold(eng, step, at + 3)
            eng.tensor_tensor(dst[2], tmp, dst[1], ALU.subtract).then_inc(step, 1)

        def bank(kind, b, i):
            if not (isinstance(b, int) and b == 0):
                return ps_m[:, :]
            return ps_s[:, i % 2, :] if kind == "V" else ps_t[:, i % 4, :]

        block = ctx.enter_context(nc.Block())

        @block.sync
        def _(sp):
            def load_x(b):
                sp.dma_start(x_in[:, :, :], x_v[b]).then_inc(x_loaded, 16)
                sp.dma_start(c_in[:, :, :], c_v[b]).then_inc(c_loaded, 16)

            def store_parts(b, i):
                sp.wait_ge(qk_split, 4 * (6 * b + i + 1))
                if i < 2:
                    dst = q_parts[b, :, i * P:(i + 1) * P, :]
                else:
                    c, h = divmod(i - 2, 2)
                    dst = k_parts[b, :, c * P:(c + 1) * P, h * S:(h + 1) * S]
                sp.dma_start(dst.rearrange("j p t -> p j t"), proj_parts[:, i % 2, :, :]).then_inc(parts_stored[i % 2], 16)

            def load_stack(b, g):
                for r in range(len(Q_PART)):
                    h0 = g * GH * HD
                    src = q_parts[b, Q_PART[r], h0:h0 + GH * HD, :].rearrange("(h d) t -> d h t", d=HD)
                    sp.dma_start(q_stack[r * HD:(r + 1) * HD, g, :, :], src).then_inc(stack_loaded[g], 16)
                    src = k_parts[b, K_PART[r], h0:h0 + GH * HD, :].rearrange("(h d) t -> d h t", d=HD)
                    sp.dma_start(k_stack[r * HD:(r + 1) * HD, g, :, :], src).then_inc(stack_loaded[g], 16)
                src = mask_parts[:, b, :].unsqueeze(1).to_broadcast((PARTS, GH, KEYS))
                sp.dma_start(k_stack[R_MASK:R_MAX, g, :, :], src).then_inc(stack_loaded[g], 16)

            def load_max(b, g):
                sp.wait_ge(m_split, 4 * (G * b + g + 1))
                for j in range(PARTS):
                    sp.dma_start(q_stack[R_MAX + j:R_MAX + j + 1, g, :, :].rearrange("o h (t q) -> o (h t) q", q=P),
                                 m_parts[:, j, :]).then_inc(max_loaded[g], 16)

            def batch(b, first=False, last=False):
                if not first:
                    sp.wait_ge(st_ready, 2 * KT * (G * b))
                    load_stack(b, 3)
                load_max(b, 1)
                if last:
                    sp.wait_ge(v_ready, 4 * B)
                    for half in range(2):
                        sp.wait_ge(parts_stored[half], 16 * 3 * B)
                    load_w2(3); load_w2(4)
                if not last:
                    sp.wait_ge(t_ready, 4 * (b + 2))
                    load_next(b + 2)
                    for i in range(5):
                        store_parts(b + 1, i)
                    sp.wait_ge(parts_stored[0], 16 * (3 * (b + 1) + 2))
                    sp.wait_ge(parts_stored[1], 16 * (3 * (b + 1) + 2))
                    sp.wait_ge(st_ready, 2 * KT * (G * b + 1))
                    load_stack(b + 1, 0)
                load_max(b, 2)
                if last:
                    load_w2(5); load_w2(6)
                if not last:
                    store_parts(b + 1, 5)
                if not first:
                    store_x1(b - 1)
                sp.dma_start(x_res[:, :, :], x_v[b]).then_inc(res_loaded, 16)
                if not last:
                    for half in range(2):
                        sp.wait_ge(parts_stored[half], 16 * 3 * (b + 2))
                if last:
                    sp.wait_ge(v_copied, G * B)
                    load_w2(2)
                    sp.wait_ge(st_ready, 2 * KT * (G * b + 1))
                    load_w1(2)
                load_max(b, 3)
                if last:
                    sp.wait_ge(st_ready, 2 * KT * (G * b + 2))
                    load_w1(3); load_w1(0)
                    sp.wait_ge(pv_done, KT * (G * b + 2))
                    load_w2(0)
                    sp.wait_ge(max_loaded[3], 16 * PARTS * B)
                    load_w2(7)
                    sp.wait_ge(st_ready, 2 * KT * (G * b + 3))
                    load_w1(4)
                if not last:
                    sp.wait_ge(st_ready, 2 * KT * (G * b + 2))
                    load_stack(b + 1, 1)
                    load_max(b + 1, 0)
                    sp.wait_ge(st_ready, 2 * KT * (G * b + 3))
                    load_stack(b + 1, 2)

            def store_x1(b):
                sp.wait_ge(x1_added, G * (b + 1))
                sp.dma_start(x1_v[b], x_res[:, :, :]).then_inc(x1_stored, 16)
                sp.wait_ge(x1_normed, QT * (b + 1))
                sp.dma_start(xn2_v[b], xn2[:, :, :]).then_inc(xn2_stored, 16)
                sp.wait_ge(x1_stored, 16 * (b + 1))

            def load_next(b):
                if isinstance(b, int) and b >= B:
                    return
                load_x(b)

            sp.dma_start(mk[:, :], mask.rearrange("b o n (k c) -> (b o n k) c", c=P)).then_inc(mask_loaded, 16)
            load_x(0)
            for w, t in ((Wq, wq), (Wk, wk), (Wv, wv)):
                sp.dma_start(t[:, :, :], w.rearrange("(c p) n -> p c n", p=P)).then_inc(w_loaded, 16)
            sp.dma_start(b_q[:, :], bq.rearrange("(c p) -> p c", p=P), allow_slow_non_contiguous=True).then_inc(w_loaded, 16)
            sp.dma_start(b_k[:, :], bk.rearrange("(c p) -> p c", p=P), allow_slow_non_contiguous=True).then_inc(w_loaded, 16)
            sp.dma_start(b_v[:, :], bv.partition_broadcast(P)).then_inc(w_loaded, 16)
            sp.dma_start(g_raw[:, :], g_xattn.partition_broadcast(P)).then_inc(w_loaded, 16)
            sp.dma_start(wr[:, :, :], Wr.rearrange("(c p) e -> p c e", p=P)).then_inc(w_loaded, 16)
            sp.dma_start(b_r[:, :], br.partition_broadcast(P)).then_inc(w_loaded, 16)
            sp.dma_start(gf_raw[:, :], g_ffn.partition_broadcast(P)).then_inc(w_loaded, 16)
            sp.dma_start(gb_rows[:, 0, :], g1.rearrange("e (c p) -> (e c) p", p=P)).then_inc(gb_loaded, 16)
            sp.dma_start(gb_rows[:, 1, :], be1.rearrange("e (c p) -> (e c) p", p=P)).then_inc(gb_loaded, 16)
            sp.wait_ge(mask_step, 4)
            sp.dma_start(mask_parts.rearrange("j b (k c) -> (b k) j c", c=P), mk_parts[:, :, :]).then_inc(mask_stored, 16)
            sp.wait_ge(t_ready, 4)
            load_x(1)
            for i in range(6):
                store_parts(0, i)
            for half in range(2):
                sp.wait_ge(parts_stored[half], 16 * 3)
            sp.wait_ge(mask_stored, 16)
            sp.wait_ge(ones_set, 3)
            for g in range(4):
                load_stack(0, g)
            load_max(0, 0)
            sp.dma_start(acc_d[TOKENS:TOKENS + P, :], x[0, 0:P, :]).then_inc(spare_stored, 16)
            sp.dma_start(b1_bc[:, :, :], b1.partition_broadcast(P)).then_inc(w1_loaded, 16)
            batch(0, first=True)
            with sp.Fori(1, B - 2) as b:
                batch(b)
            batch(B - 2)
            batch(B - 1, last=True)
            store_x1(B - 1)
            experts_sync(sp)

        @block.tensor
        def _(pe):
            EVAC = {"T": t_evac, "Q": qk_evac, "V": v_evac, "M": m_evac, "O": o_evac, "L": l_evac, "R": r_evac}
            prev = [None]

            def spare_free():
                if prev[0] is not None:
                    kind, n = prev[0]
                    pe.wait_ge(EVAC[kind], n + 1)

            def use_T(b, i):
                src = x_in if i < 2 else c_in
                if i == 0:
                    pe.wait_ge(x_normed, QT * (b + 1))
                if i == 2:
                    pe.wait_ge(c_loaded, 16 * (b + 1))
                for t in range(QT):
                    mm = pe.transpose(bank("T", b, i)[:, t * P:(t + 1) * P], src[:, t, (i % 2) * P:(i % 2 + 1) * P], ident[:, :])
                mm.then_inc(t_ready, 1)

            def use_Q(b, i):
                pe.wait_ge(t_evac, 4 * b + 4 if i > 1 else 4 * b + 2)
                c, h = (i, 0) if i < 2 else divmod(i - 2, 2)
                w = wq if i < 2 else wk
                if isinstance(b, int) and b == 0 and i >= 4:
                    pe.wait_ge(qk_evac, i - 3)
                for k in range(DC):
                    mm = pe.matmul(bank("Q", b, i), w[:, k, c * P:(c + 1) * P], all_t[:, k, h * S:(h + 1) * S],
                                   start=(k == 0), stop=(k == DC - 1))
                mm.then_inc(qk_ready, 1)

            def use_V(b, i):
                if isinstance(b, int) and b == 0 and i >= 2:
                    pe.wait_ge(v_evac, i - 1)
                for n in range(2):
                    for k in range(DC):
                        kt = 2 * i + n
                        mm = pe.matmul(bank("V", b, i)[:, n * D:(n + 1) * D], all_t[:, k, kt * P:(kt + 1) * P], wv[:, k, :],
                                       start=(k == 0), stop=(k == DC - 1))
                mm.then_inc(v_ready, 1)

            def use_M(u):
                pe.wait_ge(m_reduced, u + 1)
                pe.transpose(ps_m[0:GH * QT, 0:P], m_row[:, :], ident[:, :]).then_inc(m_ready, 1)

            def use_O(u):
                pe.wait_ge(o_copied, u + 1)
                for t in range(QT):
                    mm = pe.transpose(ps_m[:, t * P:(t + 1) * P], o_sb[:, t * P:(t + 1) * P], ident[:, :])
                mm.then_inc(o_ready, 1)

            def use_L(b, i):
                if i == 0:
                    pe.wait_ge(x1_normed, QT * (b + 1))
                for t in range(QT):
                    mm = pe.transpose(ps_m[:, t * P:(t + 1) * P], xn2[:, t, i * P:(i + 1) * P], ident[:, :])
                mm.then_inc(l_ready, 1)

            def use_R(b):
                for t in range(QT):
                    for k in range(DC):
                        mm = pe.matmul(ps_m[:, t * E:(t + 1) * E], xn2_t[:, k, t * P:(t + 1) * P], wr[:, k, :],
                                       start=(k == 0), stop=(k == DC - 1))
                mm.then_inc(r_ready, 1)

            def spare(use, b, u):
                spare_free()
                kind, i = use[0], int(use[1:] or 0)
                if kind == "T":
                    use_T(b + 1, i); n = 4 * (b + 1) + i
                elif kind == "Q":
                    use_Q(b + 1, i); n = 6 * (b + 1) + i
                elif kind == "V":
                    use_V(b + 1, i); n = 4 * (b + 1) + i
                elif kind == "M":
                    use_M(u + 1); n = u + 1
                elif kind == "L":
                    use_L(b - 1, i); n = 2 * (b - 1) + i
                elif kind == "R":
                    use_R(b - 1); n = b - 1
                else:
                    use_O(u - 1); n = u - 1
                prev[0] = (kind, n)

            def scores_max(w, g, i):
                h, t, half = i // 8, i // 2 % QT, i % 2
                n = 32 * w + i
                if not (isinstance(n, int) and n < 2):
                    pe.wait_ge(s_used, n - 1)
                pe.matmul(ps_s[:, i % 2, :], q_stack[0:R_MAX, g, h, t * P:(t + 1) * P],
                          k_stack[0:R_MAX, g, h, half * S:(half + 1) * S], start=True, stop=True).then_inc(s_ready, 1)

            def scores_t(b, g, k, pair):
                n = KT * (G * b + g) + k
                if k == 0 and pair == 0:
                    pe.wait_ge(max_loaded[g], 16 * PARTS * (b + 1))
                if not (isinstance(n, int) and n == 0):
                    pe.wait_ge(exp_done, 2 * n - 1 + pair)
                for h in (2 * pair, 2 * pair + 1):
                    mm = pe.matmul(ps_t[:, h, :], k_stack[0:ROWS, g, h, k * P:(k + 1) * P], q_stack[0:ROWS, g, h, :],
                                   start=True, stop=True)
                mm.then_inc(st_ready, 1)

            def probs_v(b, g, k):
                u = G * b + g
                pe.wait_ge(exp_done, 2 * (KT * u + k) + 2)
                if k == 0:
                    pe.wait_ge(v_copied, u + 1)
                    if not (isinstance(u, int) and u == 0):
                        pe.wait_ge(o_copied, u)
                for h in range(GH):
                    mm = pe.matmul(ps_o[32 * h:32 * h + 32, :], v_ring[:, g, k, h, :], probs[:, k % 2, h, :],
                                   start=(k == 0), stop=(k == KT - 1))
                mm.then_inc(pv_done, 1)

            def batch(b, first=False, last=False):
                for step in range(G * KT):
                    g, k = divmod(step, KT)
                    slot = (g + 2) % G

                    def ahead(i):
                        if last and g >= 2:
                            return
                        if k == 0 and i == 0:
                            pe.wait_ge(stack_loaded[slot], 16 * LOADS * (b + 1 + (g + 2) // G))
                        scores_max(G * b + g + 2, slot, 4 * k + i)

                    ahead(0)
                    scores_t(b, g, k, 0)
                    ahead(1)
                    scores_t(b, g, k, 1)
                    uses = list(plan(step, first, last))
                    for use in uses[0:1]:
                        spare(use, b, G * b + g)
                    ahead(2)
                    ahead(3)
                    if step:
                        probs_v(b, (step - 1) // KT, (step - 1) % KT)
                    elif not first:
                        probs_v(b - 1, G - 1, KT - 1)
                    for use in uses[1:]:
                        spare(use, b, G * b + g)

            pe.wait_ge(const_ready, CONSTS)
            pe.wait_ge(w_loaded, 16 * 10)
            for i in range(4):
                use_T(0, i)
            for i in range(6):
                use_Q(0, i)
            for i in range(4):
                use_V(0, i)
            pe.wait_ge(v_evac, 4)
            pe.wait_ge(gb_loaded, 32)
            for i in range(2):
                mm = pe.transpose(ps_o[:, i * 64:(i + 1) * 64], gb_rows[:, i, :], ident[0:64, 0:64])
            mm.then_inc(gb_ready, 1)
            for w in range(2):
                pe.wait_ge(stack_loaded[w], 16 * LOADS)
                for i in range(32):
                    scores_max(w, w, i)
                if w == 0:
                    spare("M", 0, -1)
            batch(0, first=True)
            with pe.Fori(1, B - 2) as b:
                prev[0] = ("O", G * b - 2)
                batch(b)
            prev[0] = ("O", G * (B - 2) - 2)
            batch(B - 2)
            batch(B - 1, last=True)
            probs_v(B - 1, G - 1, KT - 1)
            for use in ("O", "L0", "L1", "R"):
                spare(use, B, UNITS)
            experts_tensor(pe)

        @block.scalar
        def _(act):
            def evac_T(b, i):
                act.wait_ge(t_ready, 4 * b + i + 1)
                o = S * (i // 2)
                act.activation(all_t[:, i % 2, o:o + S], bank("T", b, i), ACT.Copy).then_inc(t_evac, 1)

            def evac_Q(b, i):
                act.wait_ge(qk_ready, 6 * b + i + 1)
                if not (isinstance(b, int) and b == 0 and i < 2):
                    act.wait_ge(qk_split, 4 * (6 * b + i - 1))
                bias = b_qs[:, i:i + 1] if i < 2 else b_k[:, (i - 2) // 2:(i - 2) // 2 + 1]
                act.activation(proj[:, i % 2, :], bank("Q", b, i), ACT.Identity, bias=bias,
                               scale=HD ** -0.5 if i < 2 else 1.0).then_inc(qk_evac, 1)

            def evac_V(b, i):
                act.wait_ge(v_ready, 4 * b + i + 1)
                if i == 0 and not (isinstance(b, int) and b == 0):
                    act.wait_ge(v_copied, G * b)
                act.activation(v_all[:, 2 * i:2 * i + 2, :], bank("V", b, i).rearrange("p (n d) -> p n d", d=D),
                               ACT.Copy).then_inc(v_evac, 1)

            def evac_L(b, i):
                act.wait_ge(l_ready, 2 * b + i + 1)
                if i == 0 and not (isinstance(b, int) and b == 0):
                    act.wait_ge(r_ready, b)
                act.activation(xn2_t[:, i, :], ps_m[:, :], ACT.Copy).then_inc(l_evac, 1)

            def copy_O(u):
                act.wait_ge(pv_done, KT * (u + 1))
                if not (isinstance(u, int) and u == 0):
                    act.wait_ge(o_ready, u)
                act.activation(o_sb[:, :], ps_o[:, :], ACT.Copy).then_inc(o_copied, 1)

            def exp(b, g, k, pair):
                n = KT * (G * b + g) + k
                act.wait_ge(st_ready, 2 * n + pair + 1)
                if pair == 0 and not (isinstance(n, int) and n < 2):
                    act.wait_ge(pv_done, n - 1)
                act.activation(probs[:, k % 2, 2 * pair:2 * pair + 2, :], ps_t[:, 2 * pair:2 * pair + 2, :],
                               ACT.Exp).then_inc(exp_done, 1)

            def batch(b, first=False, last=False):
                for step in range(G * KT):
                    g, k = divmod(step, KT)
                    exp(b, g, k, 0)
                    exp(b, g, k, 1)
                    for use in plan(step, first, last):
                        if use[0] == "T":
                            evac_T(b + 1, int(use[1]))
                        if use[0] == "Q":
                            evac_Q(b + 1, int(use[1]))
                        if use[0] == "V":
                            evac_V(b + 1, int(use[1]))
                        if use[0] == "L":
                            evac_L(b - 1, int(use[1]))
                    if k == 0 and not (first and g == 0):
                        copy_O(G * b + g - 1)

            act.wait_ge(w_loaded, 16 * 10)
            act.activation(b_qs[:, :], b_q[:, :], ACT.Copy, scale=HD ** -0.5).then_inc(bq_scaled, 1)
            act.activation(g_tanh[:, :], g_raw[:, :], ACT.Tanh).then_inc(g_ready, 1)
            act.activation(gf_tanh[:, :], gf_raw[:, :], ACT.Tanh).then_inc(g_ready, 1)
            act.wait_ge(bq_scaled, 1)
            for i in range(4):
                evac_T(0, i)
            for i in range(6):
                evac_Q(0, i)
            for i in range(4):
                evac_V(0, i)
            batch(0, first=True)
            with act.Fori(1, B - 2) as b:
                batch(b)
            batch(B - 2)
            batch(B - 1, last=True)
            copy_O(UNITS - 1)
            evac_L(B - 1, 0)
            evac_L(B - 1, 1)
            experts_scalar(act)

        @block.vector
        def _(dve):
            def stats_x(b, tiles=range(QT)):
                dve.wait_ge(x_loaded, 16 * (b + 1))
                for t in tiles:
                    dve.bn_stats(stat1[:, t, :], x_in[:, t, :]).then_inc(stats1, 1)

            def means_x(b):
                hold(dve, stats1, QT * (b + 1))
                if not (isinstance(b, int) and b == 0):
                    hold(dve, x_normed, QT * b)
                for t in range(QT):
                    dve.bn_aggr(mv1[:, t, :], stat1[:, t, :]).then_inc(agg1, 1)

            def norm_x(b, tiles=range(QT)):
                dve.wait_ge(rstd1_step, 2 * b + 2)
                for t in tiles:
                    dve.tensor_scalar(x_in[:, t, :], x_in[:, t, :], mv1[:, t, 0:1], rstd1[:, t:t + 1],
                                      ALU.subtract, ALU.mult).then_inc(x_normed, 1)

            def stats_x1(b, tiles=range(QT)):
                dve.wait_ge(x1_added, G * (b + 1))
                for t in tiles:
                    dve.bn_stats(stat2[:, t, :], x_res[:, t, :]).then_inc(stats2, 1)

            def means_x1(b):
                hold(dve, stats2, QT * (b + 1))
                if not (isinstance(b, int) and b == 0):
                    hold(dve, x1_normed, QT * b)
                for t in range(QT):
                    dve.bn_aggr(mv2[:, t, :], stat2[:, t, :]).then_inc(agg2, 1)

            def norm_x1(b, tiles=range(QT)):
                if tiles[0] == 0:
                    dve.wait_ge(rstd2_step, 2 * b + 2)
                if tiles[0] == 0 and not (isinstance(b, int) and b == 0):
                    hold(dve, xn2_stored, 16 * b)
                    hold(dve, l_ready, 2 * b)
                for t in tiles:
                    dve.tensor_scalar(xn2[:, t, :], x_res[:, t, :], mv2[:, t, 0:1], rstd2[:, t:t + 1],
                                      ALU.subtract, ALU.mult).then_inc(x1_normed, 1)

            def evac_R(b):
                dve.wait_ge(r_ready, b + 1)
                dve.tensor_copy(logits[:, bass.ds(b * QT, QT), :],
                                ps_m[:, 0:QT * E].rearrange("p (t e) -> p t e", e=E)).then_inc(r_evac, 1)

            def reduce_max(w, par, i):
                n = 32 * w + i
                if i == 0 and not (isinstance(w, int) and w < 2):
                    dve.wait_ge(m_reduced, w - 1)
                dve.wait_ge(s_ready, n + 1)
                dve.tensor_reduce(m_half[:, par, i:i + 1], ps_s[:, i % 2, :], AX.X, ALU.max).then_inc(s_used, 1)

            def join_max(u, par):
                dve.wait_ge(s_used, 32 * (u + 1))
                if not (isinstance(u, int) and u == 0):
                    dve.wait_ge(m_ready, u)
                dve.tensor_reduce(m_row[:, :], m_half[:, par, :].rearrange("p (n h) -> p n h", h=2), AX.X,
                                  ALU.max).then_inc(m_reduced, 1)

            def evac_M(u):
                dve.wait_ge(m_ready, u + 1)
                if not (isinstance(u, int) and u == 0):
                    dve.wait_ge(m_split, 4 * u)
                dve.tensor_scalar(m_neg[:, :], ps_m[0:GH * QT, 0:P], -1.0, None, ALU.mult).then_inc(m_evac, 1)

            def evac_O(u):
                dve.wait_ge(o_ready, u + 1)
                o = ps_m[:, :].rearrange("p (t h d) -> p t h d", t=QT, h=GH)
                dve.reciprocal(r_sum[:, :, :], o[:, :, :, HD]).then_inc(o_recip, 1)
                dve.wait_ge(o_recip, u + 1)
                dve.tensor_scalar(r_scl[:, :, :], r_sum[:, :, :], g_tanh[:, 0:1], None, ALU.mult).then_inc(o_scaled, 1)
                dve.wait_ge(o_scaled, u + 1)
                if not (isinstance(u, int) and u == 0):
                    dve.wait_ge(x1_added, u)
                dve.tensor_tensor(ctx_n[:, :, :].rearrange("p t (h d) -> p t h d", d=HD), o[:, :, :, 0:HD],
                                  r_scl[:, :, :].unsqueeze(3).to_broadcast((P, QT, GH, HD)),
                                  ALU.mult).then_inc(o_evac, 1)

            def ahead(u, g, k, i, last):
                if not (last and g >= 2):
                    reduce_max(u + 2, g % 2, 4 * k + i)
                    reduce_max(u + 2, g % 2, 4 * k + i + 1)

            HALF = (range(0, QT // 2), range(QT // 2, QT))

            def batch(b, first=False, last=False, stats=True):
                for step in range(G * KT):
                    g, k = divmod(step, KT)
                    u = G * b + g
                    if k == 0 and not (last and g == 3):
                        join_max(u + 1, (g + 1) % 2)
                    ahead(u, g, k, 0, last)
                    for use in plan(step, first, last):
                        if use == "M":
                            evac_M(u + 1)
                        if use == "O":
                            evac_O(u - 1)
                        if use == "R":
                            evac_R(b - 1)
                    ahead(u, g, k, 2, last)
                    if not first:
                        if step in (5, 6):
                            stats_x1(b - 1, HALF[step - 5])
                        if step == 7:
                            means_x1(b - 1)
                        if step in (11, 12):
                            norm_x1(b - 1, HALF[step - 11])
                    if stats and not last:
                        if step in (20, 21):
                            stats_x(b + 2, HALF[step - 20])
                        if step == 22:
                            means_x(b + 2)
                        if step in (23, 24):
                            norm_x(b + 2, HALF[step - 23])

            stats_x(0)
            means_x(0)
            norm_x(0)
            two_ones = 1 + 0x3F80 / 2.0 ** 23
            for stack in (q_stack, k_stack):
                dve.memset(stack[R_MASK:P, :, :, :].bitcast(F32), two_ones).then_inc(ones_set, 1)
            dve.memset(v_ring[:, :, :, :, HD:32], 1.0).then_inc(ones_set, 1)
            dve.wait_ge(w_loaded, 16 * 10)
            dve.wait_ge(g_ready, 2)
            dve.tensor_scalar(b_v[:, :], b_v[:, :], g_tanh[:, 0:1], None, ALU.mult).then_inc(bv_scaled, 1)
            for i in range(6):
                dve.wait_ge(qk_evac, i + 1)
                if i >= 2:
                    dve.wait_ge(parts_stored[i % 2], 16 * (i // 2))
                split3(dve, [proj_parts[:, i % 2, j, :] for j in range(PARTS)], proj[:, i % 2, :], rest[:, i % 2, :],
                       qk_split, 4 * i)
            dve.wait_ge(gb_ready, 1)
            dve.tensor_copy(g1_t[:, :, :], ps_o[:, 0:P].rearrange("p (i n) -> p i n", i=2)).then_inc(gb_evac, 1)
            for w in range(2):
                for i in range(32):
                    reduce_max(w, w, i)
                if w == 0:
                    join_max(0, 0)
                    evac_M(0)
                    stats_x(1)
                    means_x(1)
                    norm_x(1)
            batch(0, first=True)
            with dve.Fori(1, B - 2) as b:
                batch(b)
            batch(B - 2, stats=False)
            batch(B - 1, last=True)
            evac_O(UNITS - 1)
            stats_x1(B - 1)
            means_x1(B - 1)
            norm_x1(B - 1)
            evac_R(B - 1)
            experts_vector(dve)

        @block.gpsimd
        def _(pool):
            def rstd_x(b):
                hold(pool, agg1, QT * (b + 1))
                pool.tensor_scalar(rstd1[:, :], mv1[:, :, 1], EPS, None, ALU.add).then_inc(rstd1_step, 1)
                hold(pool, rstd1_step, 2 * b + 1)
                pool.tensor_tensor(rstd1[:, :], rstd1[:, :], minus_half[:, :], ALU.pow).then_inc(rstd1_step, 1)

            def split_Q(b, i):
                n = 6 * b + i
                hold(pool, qk_evac, n + 1)
                if not (isinstance(n, int) and n < 2):
                    hold(pool, parts_stored[i % 2], 16 * (3 * b + i // 2))
                split3(pool, [proj_parts[:, i % 2, j, :] for j in range(PARTS)], proj[:, i % 2, :], rest[:, i % 2, :],
                       qk_split, 4 * n)

            def split_M(u, g):
                hold(pool, m_evac, u + 1)
                if not (isinstance(u, int) and u == 0):
                    hold(pool, max_loaded[(g - 1) % G], 16 * PARTS * ((u - 1 - (g - 1) % G) // G + 1) if isinstance(u, int)
                                 else 16 * PARTS * mload[0])
                split3(pool, [m_parts[:, j, :] for j in range(PARTS)], m_neg[:, :], m_rest[:, :], m_split, 4 * u)

            mload = [None]

            def copy_V(b, g):
                hold(pool, v_evac, 4 * (b + 1))
                if not (isinstance(b, int) and b == 0):
                    hold(pool, pv_done, KT * (G * (b - 1) + g + 1))
                v = v_all[:, :, g * GH * HD:(g + 1) * GH * HD].rearrange("p k (h d) -> p k h d", d=HD)
                pool.tensor_tensor(v_ring[:, g, :, :, 0:HD], v,
                                   zero[:, 0:1].unsqueeze(2).unsqueeze(3).to_broadcast((P, KT, GH, HD)), ALU.add).then_inc(v_copied, 1)

            def add_x(b, g):
                if g == 0:
                    pool.wait_ge(res_loaded, 16 * (b + 1))
                    pool.tensor_tensor(x_res[:, :, :], x_res[:, :, :], b_v[:, :].unsqueeze(1).to_broadcast((P, QT, D)),
                                       ALU.add).then_inc(res_biased, 1)
                    pool.wait_ge(res_biased, b + 1)
                pool.wait_ge(o_evac, G * b + g + 1)
                o = g * GH * HD
                pool.tensor_tensor(x_res[:, :, o:o + GH * HD], x_res[:, :, o:o + GH * HD], ctx_n[:, :, :],
                                   ALU.add).then_inc(x1_added, 1)

            def rstd_x1(b):
                hold(pool, agg2, QT * (b + 1))
                pool.tensor_scalar(rstd2[:, :], mv2[:, :, 1], EPS, None, ALU.add).then_inc(rstd2_step, 1)
                pool.wait_ge(rstd2_step, 2 * b + 1)
                pool.tensor_tensor(rstd2[:, :], rstd2[:, :], minus_half[:, :], ALU.pow).then_inc(rstd2_step, 1)

            def batch(b, first=False, last=False, norm=True):
                for step in range(G * KT):
                    g, k = divmod(step, KT)
                    u = G * b + g
                    if step == 4 and not first:
                        copy_V(b, 3)
                    if step == 20 and not last:
                        copy_V(b + 1, 0)
                        copy_V(b + 1, 1)
                    if step == 28 and not last:
                        copy_V(b + 1, 2)
                    for use in plan(step, first, last):
                        if use == "M":
                            mload[0] = b + 1
                            split_M(u + 1, (g + 1) % G)
                        if use == "O":
                            if g == 0:
                                add_x(b - 1, 3)
                            else:
                                add_x(b, g - 1)
                        if use[0] == "Q":
                            split_Q(b + 1, int(use[1]))
                    if step == 7 and not first:
                        rstd_x1(b - 1)
                    if step == 22 and norm and not last:
                        rstd_x(b + 2)

            pool.memset(ones[:, :], 1.0).then_inc(ones_ready, 1)
            pool.wait_ge(ones_ready, 1)
            pool.affine_select(out=tri[:, :], in_=ones[:, :], compare_op=ALU.is_gt, fill=0.0, base=0,
                               pattern=[[1, P]], channel_multiplier=-1).then_inc(const_ready, 1)
            pool.memset(minus_half[:, :], -0.5).then_inc(const_ready, 1)
            pool.memset(zero[:, :], 0.0).then_inc(const_ready, 1)
            pool.memset(ident[:, :], 0.0).then_inc(ident_zero, 1)
            hold(pool, ident_zero, 1)
            pool.affine_select(out=ident[:, :], in_=ident[:, :], compare_op=ALU.not_equal, fill=1.0, base=0,
                               pattern=[[-1, P]], channel_multiplier=1).then_inc(const_ready, 1)
            pool.wait_ge(const_ready, CONSTS)
            hold(pool, mask_loaded, 16)
            pool.tensor_copy(mk_parts[:, 0, :], mk[:, :]).then_inc(mask_step, 1)
            hold(pool, mask_step, 1)
            pool.tensor_tensor(mk_rest[:, :], mk[:, :], mk_parts[:, 0, :], ALU.subtract).then_inc(mask_step, 1)
            hold(pool, mask_step, 2)
            pool.tensor_copy(mk_parts[:, 1, :], mk_rest[:, :]).then_inc(mask_step, 1)
            pool.wait_ge(mask_step, 3)
            pool.tensor_tensor(mk_parts[:, 2, :], mk_rest[:, :], mk_parts[:, 1, :], ALU.subtract).then_inc(mask_step, 1)
            rstd_x(0)
            pool.wait_ge(bv_scaled, 1)
            for g in range(4):
                copy_V(0, g)
            split_M(0, 0)
            rstd_x(1)
            batch(0, first=True)
            with pool.Fori(1, B - 2) as b:
                batch(b)
            batch(B - 2, norm=False)
            batch(B - 1, last=True)
            add_x(B - 1, 3)
            rstd_x1(B - 1)
            experts_gpsimd(pool)


_INS = ['x', 'ctx_1024', 'mask_Bx1x1x4096_ff0', 'g_xattn', 'g_ffn', 'L0_xattn_Wq', 'L0_xattn_bq', 'L0_xattn_Wk',
        'L0_xattn_bk', 'L0_xattn_Wv', 'L0_xattn_bv', 'L0_ffn_Wr', 'L0_ffn_br', 'L0_ffn_W1', 'L0_ffn_b1', 'L0_ffn_g1',
        'L0_ffn_be1', 'L0_ffn_W2', 'L0_ffn_b2', 'L0_ffn_g2', 'L0_ffn_be2']
_OUTS = [((8, 512, 256), 'float32')]


def kernel(**inputs):
    import numpy as _np
    import concourse.bacc as _bacc
    from concourse import mybir as _mybir
    from concourse.bass_utils import run_bass_kernel_spmd as _run

    nc = _bacc.Bacc("TRN2", target_bir_lowering=False, num_devices=1)
    arrays, args = {}, []
    for name in _INS:
        a = _np.ascontiguousarray(inputs[name])
        arrays[f"in_{name}_dram"] = a
        args.append(nc.dram_tensor(f"in_{name}_dram", a.shape, _mybir.dt.from_np(a.dtype), kind="ExternalInput").ap())
    for i, (shape, dtype) in enumerate(_OUTS):
        dt = _mybir.dt.from_np(_np.dtype(dtype))
        args.append(nc.dram_tensor(f"out_{i}_dram", shape, dt, kind="ExternalOutput").ap())
    flamingo_kernel(nc, *args)
    r = _run(nc, [arrays], core_ids=[0])
    return r.results[0]["out_0_dram"]
```

```python
from contextlib import ExitStack

import concourse.bass as bass
from concourse import mybir

F32 = mybir.dt.float32
BF16 = mybir.dt.bfloat16
I32 = mybir.dt.int32
U32 = mybir.dt.uint32
ALU = mybir.AluOpType
ACT = mybir.ActivationFunctionType
AX = mybir.AxisListType

P = 128
B, S, D = 8, 512, 256
NH, HD = 16, 16
KEYS = 2 * S
GH = 4
G = NH // GH
KT = KEYS // P
QT = S // P
DC = D // P
UNITS = B * G
EPS = 1e-5
Q_PART = (0, 0, 1, 1, 0, 2)
K_PART = (0, 1, 0, 1, 2, 0)
PARTS = 3
PROD = len(Q_PART) * HD
R_MASK = PROD
R_MAX = R_MASK + PARTS
ROWS = R_MAX + PARTS
TWO_ONES = 1 + 0x3F80 / 2.0 ** 23
LOADS = 2 * len(Q_PART) + 1

E, F = 8, 1024
FC = F // P
HC = FC // 2
TOP = 2
TOKENS = B * S
TT = TOKENS // P
CONSTS = 4
SLOT_TILES = TOP * TOKENS // P + E - 1
LOOP_END = (SLOT_TILES - 4) // 2


def before(n, limit):
    return isinstance(n, int) and n < limit


def beyond(j):
    return isinstance(j, int) and j >= SLOT_TILES


def carve(region, at, shape, dt=F32):
    n = 1
    for d in shape[1:]:
        n *= d
    cols = n * (2 if dt == BF16 else 4) // 4
    v = region[0:shape[0], at:at + cols]
    if dt != F32:
        v = v.bitcast(dt)
    if len(shape) == 2:
        return v
    names = "abcdefgh"[:len(shape) - 1]
    return v.rearrange(f"p ({' '.join(names)}) -> p {' '.join(names)}", **dict(zip(names, shape[1:])))


def flamingo_kernel(nc, x, ctx_in, mask, g_xattn, g_ffn, Wq, bq, Wk, bk, Wv, bv,
                    Wr, br, W1, b1, g1, be1, W2, b2, g2, be2, out):
    with ExitStack() as ctx:
        def sb(name, shape, dt=F32):
            return ctx.enter_context(nc.sbuf_tensor(name, shape, dt))

        def sem(name):
            return ctx.enter_context(nc.semaphore(name))

        def dram(name, shape, dt=F32):
            return nc.dram_tensor(name, shape, dt, kind="Internal").ap()

        q_parts = dram("q_parts", (B, PARTS, D, S), BF16)
        k_parts = dram("k_parts", (B, PARTS, D, KEYS), BF16)
        mask_parts = dram("mask_parts", (PARTS, B, KEYS), BF16)

        acc_d = dram("acc_d", (TOKENS + P, D))
        xn2_d = dram("xn2_d", (TOKENS, D))

        big = sb("big", [P, E * (DC * F + FC * D)])
        mid = sb("mid", [P, E * F])
        small = sb("small", [P, 4864])
        q_stack = carve(big, 0, [P, G, GH, S], BF16)
        k_stack = carve(big, 4096, [P, G, GH, KEYS], BF16)
        probs = carve(big, 12288, [P, 2, GH, S])
        v_ring = carve(big, 16384, [P, G, KT, GH, 32])
        v_all = carve(big, 20480, [P, KT, D])
        all_t = carve(big, 22528, [P, DC, KEYS])
        x_in = carve(big, 24576, [P, QT, D])
        c_in = carve(big, 25600, [P, QT, D])
        proj = carve(big, 26624, [P, 2, S])
        rest = carve(big, 27648, [P, 2, S])
        proj_parts = carve(big, 28672, [P, 2, PARTS, S], BF16)
        x_res = carve(small, 0, [P, QT, D])
        o_sb = carve(small, 1024, [P, S])
        ctx_n = carve(small, 1536, [P, QT, GH * HD])
        xn2 = carve(small, 1792, [P, QT, D])
        xn2_t = carve(small, 2816, [P, DC, S])
        wq, wk, wv = (carve(big, 30208 + 512 * i, [P, DC, D]) for i in range(3))
        wr = sb("wr", [P, DC, E]); b_r = sb("b_r", [P, E])
        logits = carve(small, 4352, [P, TT, E])
        gf_raw = sb("gf_raw", [P, 1]); gf_tanh = sb("gf_tanh", [P, 1])
        b_q = sb("b_q", [P, DC]); b_qs = sb("b_qs", [P, DC]); b_k = sb("b_k", [P, DC])
        b_v = carve(small, 4096, [P, D])
        ident = sb("ident", [P, P])
        g_raw = sb("g_raw", [P, 1]); g_tanh = sb("g_tanh", [P, 1])
        stat1 = sb("stat1", [P, QT, 6]); mv1 = sb("mv1", [P, QT, 2]); rstd1 = sb("rstd1", [P, QT])
        minus_half = sb("minus_half", [P, QT]); zero = sb("zero", [P, 1])
        stat2 = sb("stat2", [P, QT, 6]); mv2 = sb("mv2", [P, QT, 2]); rstd2 = sb("rstd2", [P, QT])
        m_half = carve(big, 31744, [P, 2, GH * QT * 2]); m_row = carve(big, 31808, [P, GH * QT])
        m_neg = carve(big, 31824, [GH * QT, P]); m_rest = carve(big, 31952, [GH * QT, P])
        m_parts = carve(big, 32080, [GH * QT, PARTS, P], BF16)
        r_sum = sb("r_sum", [P, QT, GH]);
        mk = carve(big, 32272, [64, P]); mk_rest = carve(big, 32400, [64, P]); mk_parts = carve(big, 32528, [64, PARTS, P], BF16)

        ps_t = ctx.enter_context(nc.psum_tensor("ps_t", [P, GH, S], F32))
        ps_s = ctx.enter_context(nc.psum_tensor("ps_s", [P, 2, S], F32))
        ps_o = ctx.enter_context(nc.psum_tensor("ps_o", [P, S], F32))
        ps_m = ctx.enter_context(nc.psum_tensor("ps_m", [P, S], F32))

        x_loaded = sem("x_loaded"); c_loaded = sem("c_loaded"); w_loaded = sem("w_loaded")
        const_ready = sem("const_ready"); ident_zero = sem("ident_zero"); bq_scaled = sem("bq_scaled"); bv_scaled = sem("bv_scaled"); res_biased = sem("res_biased"); g_ready = sem("g_ready")
        mask_loaded = sem("mask_loaded"); mask_step = sem("mask_step"); mask_stored = sem("mask_stored")
        stats1 = sem("stats1"); agg1 = sem("agg1"); rstd1_step = sem("rstd1_step"); x_normed = sem("x_normed")
        t_ready = sem("t_ready"); t_evac = sem("t_evac")
        qk_ready = sem("qk_ready"); qk_evac = sem("qk_evac"); qk_split = sem("qk_split"); parts_stored = [sem(f"parts_stored{h}") for h in range(2)]
        v_ready = sem("v_ready"); v_evac = sem("v_evac"); v_copied = sem("v_copied")
        stack_loaded = [sem(f"stack_loaded{g}") for g in range(G)]
        s_ready = sem("s_ready"); s_used = sem("s_used"); m_reduced = sem("m_reduced")
        m_ready = sem("m_ready"); m_evac = sem("m_evac"); m_split = sem("m_split")
        max_loaded = [sem(f"max_loaded{g}") for g in range(G)]
        st_ready = sem("st_ready"); exp_done = sem("exp_done"); pv_done = sem("pv_done")
        o_copied = sem("o_copied"); o_ready = sem("o_ready"); o_recip = sem("o_recip"); o_evac = sem("o_evac")
        res_loaded = sem("res_loaded"); x1_added = sem("x1_added")
        stats2 = sem("stats2"); agg2 = sem("agg2"); rstd2_step = sem("rstd2_step"); x1_normed = sem("x1_normed")
        x1_stored = sem("x1_stored"); xn2_stored = sem("xn2_stored")
        l_ready = sem("l_ready"); l_evac = sem("l_evac"); r_ready = sem("r_ready"); r_evac = sem("r_evac")
        ones_ready = sem("ones_ready"); q_ones_set = sem("q_ones_set"); k_ones_set = sem("k_ones_set"); v_ones_set = sem("v_ones_set");

        x_v = x.rearrange("b (t p) d -> b p t d", p=P)
        c_v = ctx_in.rearrange("b (t p) d -> b p t d", p=P)
        xn2_v = xn2_d.rearrange("(b t p) d -> b p t d", t=QT, p=P)
        x1_v = acc_d[0:TOKENS, :].rearrange("(b t p) d -> b p t d", t=QT, p=P)

        PLAN = {0: ["T0"], 1: ["M", "T1"], 2: ["O", "T2"], 3: ["T3"], 4: ["Q0"], 5: ["Q1"], 6: ["Q2"],
                7: ["Q3"], 8: ["Q4"], 9: ["M", "Q5"], 10: ["O"], 11: ["V0"], 12: ["V1"], 13: ["V2"], 14: ["V3"],
                17: ["M"], 18: ["O"], 19: ["L0"], 20: ["L1"], 22: ["R"], 25: ["M"], 26: ["O"]}

        def plan(step, first, last):
            for use in PLAN.get(step, []):
                if use[0] in "TQV" and last:
                    continue
                if use == "M" and last and step >= 24:
                    continue
                if first and (use == "O" and step < 8 or use[0] in "LR"):
                    continue
                yield use

        def third_bank(step, first, last):
            return not list(plan(step, first, last)) and not (last and step >= 16)

        w1_sb = carve(big, 0, [P, E, DC, F])
        w2_sb = carve(big, E * DC * F, [P, E, FC, D])
        b1_bc = carve(mid, 0, [P, E, F])
        h_sb = carve(small, 0, [P, 2, F])
        ht_sb = carve(small, 2048, [P, FC, P])
        x_sb = carve(small, 3072, [P, 2, D])
        xt_sb = carve(small, 3584, [P, 2, DC, P])
        y_sb = carve(small, 4096, [P, 3, D])
        late = sb("late", [P, 3 * E * D])
        g2_bc, be2_bc, b2_bc = (carve(late, i * E * D, [P, E, D]) for i in range(3))
        is_lane = carve(late, 0, [P, 2, TOP, QT, P])
        in_tile = carve(late, 2048, [P, 2, TOP, QT, SLOT_TILES])
        slot_of = carve(late, 3200, [P, 2, TOP, QT, 2, SLOT_TILES])
        gb_rows = carve(small, 3840, [E * FC, 2, P])
        g1_t = sb("g1_t", [P, 2, E * FC])
        h_stat = sb("h_stat", [P, 2, 6]); h_mv = sb("h_mv", [P, 2, 2]); h_rstd = sb("h_rstd", [P, 2])
        y_stat = sb("y_stat", [P, 6]); y_mv = sb("y_mv", [P, 2]); y_rstd = sb("y_rstd", [P, 1])
        ra, rb, rc, one1, one2, base_a, base_b = (carve(small, 256 * i, [P, TT, E]) for i in range(7))
        rank = carve(small, 1792, [P, E]); rank_i = carve(small, 1800, [P, E], I32)
        step_f = carve(small, 1808, [P, TT]); step_i = carve(small, 1840, [P, TT], I32)
        slot_f = carve(small, 1872, [P, SLOT_TILES]); slot_i = carve(small, 1952, [P, SLOT_TILES], I32)
        top1, top2, den, best = (carve(small, 2048 + 32 * i, [P, TT]) for i in range(4))
        tiles_e, start_a, start_b, count_e = (carve(small, 2176 + 8 * i, [P, E]) for i in range(4))
        more = carve(small, 2304, [P, E, TT])
        owner = carve(small, 2560, [P, SLOT_TILES, E])
        pos_f = carve(small, 3200, [P, TOP, TT]); owner_f = carve(small, 3264, [P, SLOT_TILES])
        lane_i = carve(small, 3336, [P, P], I32); lane_f = carve(small, 3464, [P, P])
        low_i, high_i = (carve(small, 3592 + 64 * i, [P, TOP, TT], U32) for i in range(2))
        low_f, high_f = (carve(small, 3720 + 64 * i, [P, TOP, TT]) for i in range(2))
        token_i = carve(small, 3848, [P, TT], I32); token_f = carve(small, 3880, [P, TT])
        slot_tok = sb("slot_tok", [P, SLOT_TILES]); slot_gate = sb("slot_gate", [P, SLOT_TILES])
        x_idx = sb("x_idx", [P, 2], U32); y_idx = sb("y_idx", [P, 2], U32); slot_dst = sb("slot_dst", [P, SLOT_TILES])
        no_token = carve(small, 3912, [P, SLOT_TILES]); spare_i = carve(small, 3984, [P, 1], I32); spare_f = carve(small, 3985, [P, 1])
        oh = sb("oh", [P, TT, E], BF16); tri = sb("tri", [P, P], BF16); ones = sb("ones", [P, P], BF16)
        pos = sb("pos", [P, TOP, TT], U32)
        owner_i = sb("owner_i", [1, SLOT_TILES], I32)
        w_top = sb("w_top", [P, TOP, TT])

        bc_loaded = sem("bc_loaded"); experts_loaded = sem("experts_loaded"); gb_loaded = sem("gb_loaded")
        gb_ready = sem("gb_ready"); gb_evac = sem("gb_evac")
        iota_step = sem("iota_step"); found = sem("found"); valued = sem("valued"); weighed = sem("weighed"); turned = sem("turned"); slots_ready = sem("slots_ready"); idx_ready = sem("idx_ready"); route = sem("route"); route_exp = sem("route_exp")
        counted = sem("counted"); oh_ready = sem("oh_ready"); routed = sem("routed")
        x_got = [sem(f"x_got{h}") for h in range(2)]
        xt_ready = sem("xt_ready"); xt_evac = sem("xt_evac")
        h_ready = sem("h_ready"); h_biased = sem("h_biased"); h_relu = sem("h_relu"); h_stats = sem("h_stats")
        h_agg = sem("h_agg"); h_pow = sem("h_pow"); h_normed = sem("h_normed")
        ht_ready = sem("ht_ready"); ht_scaled = sem("ht_scaled"); ht_done = sem("ht_done")
        y_ready = sem("y_ready"); y_biased = sem("y_biased"); y_relu = sem("y_relu"); y_stats = sem("y_stats")
        y_agg = sem("y_agg"); y_pow = sem("y_pow"); y_normed = sem("y_normed"); y_scaled = sem("y_scaled"); y_done = sem("y_done")
        y_gated = sem("y_gated"); y_added = sem("y_added")
        spare_stored = sem("spare_stored"); out_stored = sem("out_stored")
        ps_h = [ps_t[:, 0:2, :], ps_t[:, 2:4, :]]
        ps_ht = ps_s
        ps_y = ps_o[:, 0:D]
        ps_x = ps_m[:, 0:D]

        def tiles(eng, step):
            for j in range(4):
                step(j)
            with eng.Fori(2, LOOP_END) as i:
                step(2 * i, 0)
                step(2 * i + 1, 1)
            for j in range(2 * LOOP_END, SLOT_TILES):
                step(j)

        def experts_sync(sp):
            sp.wait_ge(pv_done, KT * UNITS)
            load_w1(1); load_w2(1); load_w1(5); load_w1(6); load_w1(7)
            sp.wait_ge(turned, B)
            sp.wait_ge(x_got[1], 16)
            for i, (t, v) in enumerate(((b2_bc, b2), (g2_bc, g2), (be2_bc, be2))):
                sp.dma_start(t[:, :, :], v.partition_broadcast(P)).then_inc(bc_loaded, 16)
                sp.wait_ge(bc_loaded, 16 * (i + 1))
            sp.wait_ge(y_added, 16 * SLOT_TILES)
            sp.dma_start(out.rearrange("b s d -> (b s) d"), acc_d[0:TOKENS, :]).then_inc(out_stored, 16)
            sp.wait_ge(out_stored, 16)

        def load_w1(e):
            nc.sync.dma_start(w1_sb[:, e, :, :], W1[e].rearrange("(c p) f -> p c f", p=P)).then_inc(experts_loaded, 16)

        def load_w2(e):
            nc.sync.dma_start(w2_sb[:, e, :, :], W2[e].rearrange("(c p) d -> p c d", p=P)).then_inc(experts_loaded, 16)

        def expert_of(eng, j):
            return eng.value_load(owner_i[0:1, bass.ds(j, 1)], min_val=0, max_val=E - 1)

        def experts_tensor(pe):
            pe.wait_ge(oh_ready, 1)
            pe.wait_ge(r_evac, B)
            pe.matmul(ps_o[:, 0:TT * E], tri[:, :], oh[:, :, :], start=True, stop=True).then_inc(counted, 1)
            pe.matmul(ps_m[:, 0:TT * E], ones[:, :], oh[:, :, :], start=True, stop=True).then_inc(counted, 1)
            for b in range(B):
                pe.wait_ge(found, 2 * (b + 1))
                pe.wait_ge(valued, 2 * (b + 1))
                pe.wait_ge(weighed, QT * (b + 1))
                for k in range(TOP):
                    for t in range(QT):
                        mm = pe.matmul(ps_t[:, 0, 0:2 * SLOT_TILES], is_lane[:, b % 2, k, t, :], slot_of[:, b % 2, k, t, :, :],
                                       start=(b + k + t == 0), stop=(b == B - 1 and k == TOP - 1 and t == QT - 1))
                mm.then_inc(turned, 1)

            def turn_x(j, par, nth):
                if beyond(j):
                    return
                pe.wait_ge(x_got[par], 16 * nth)
                if not before(j, 1):
                    pe.wait_ge(xt_evac, j)
                for k in range(DC):
                    mm = pe.transpose(ps_x[:, k * P:(k + 1) * P], x_sb[:, par, k * P:(k + 1) * P], ident[:, :])
                mm.then_inc(xt_ready, 1)

            def up(j, par):
                if beyond(j):
                    return
                e = expert_of(pe, j)
                pe.wait_ge(xt_evac, j + 1)
                if not before(j, 2):
                    pe.wait_ge(h_biased, j - 1)
                for n in range(2):
                    for k in range(DC):
                        mm = pe.matmul(ps_h[par][:, n, :], xt_sb[:, par, k, :], w1_sb[:, e, k, n * 512:(n + 1) * 512],
                                       start=(k == 0), stop=(k == DC - 1))
                mm.then_inc(h_ready, 1)

            def turn_h(j, par):
                pe.wait_ge(h_normed, j + 1)
                if not before(j, 1):
                    pe.wait_ge(ht_scaled, 2 * j)
                for c in range(FC):
                    mm = pe.transpose(ps_ht[:, c // 4, c % 4 * P:(c % 4 + 1) * P], h_sb[:, par, c * P:(c + 1) * P], ident[:, :])
                mm.then_inc(ht_ready, 1)

            def down(j):
                e = expert_of(pe, j)
                if not before(j, 1):
                    pe.wait_ge(y_biased, j)
                for c in range(FC):
                    if c % HC == 0:
                        pe.wait_ge(ht_done, 2 * j + c // HC + 1)
                    mm = pe.matmul(ps_y, ht_sb[:, c, :], w2_sb[:, e, c, :], start=(c == 0), stop=(c == FC - 1))
                mm.then_inc(y_ready, 1)

            turn_x(0, 0, 1)
            turn_x(1, 1, 1)
            pe.wait_ge(experts_loaded, 16 * (2 * E + 1))
            pe.wait_ge(slots_ready, 3)
            up(0, 0)
            turn_x(2, 0, 2)
            up(1, 1)

            def step(j, par, nth):
                turn_h(j, par)
                up(j + 2, par)
                turn_x(j + 3, 1 - par, nth)
                down(j)

            for j in range(2):
                step(j, j, (j + 3) // 2 + 1)
            with pe.Fori(1, LOOP_END) as i:
                step(2 * i, 0, i + 2)
                step(2 * i + 1, 1, i + 3)
            for j in range(2 * LOOP_END, SLOT_TILES):
                step(j, j % 2, (j + 3) // 2 + 1)

        def experts_scalar(act):
            act.wait_ge(route, 3)
            act.activation(rb[:, :, :], ra[:, :, :], ACT.Exp).then_inc(route_exp, 1)
            for b in range(B):
                act.wait_ge(found, 2 * b + 1)
                if b >= 2:
                    act.wait_ge(turned, b - 1)
                for t in range(QT):
                    act.activation(slot_of[:, b % 2, 0, t, 1, :], in_tile[:, b % 2, 0, t, :], ACT.Copy,
                                   scale=w_top[:, 0, b * QT + t:b * QT + t + 1]).then_inc(weighed, 1)

            def evac_x(j, par):
                if beyond(j):
                    return
                act.wait_ge(xt_ready, j + 1)
                if not before(j, 2):
                    act.wait_ge(h_ready, j - 1)
                act.activation(xt_sb[:, par, :, :], ps_x.rearrange("p (k t) -> p k t", k=DC), ACT.Copy).then_inc(xt_evac, 1)

            def relu_h(j, par):
                if beyond(j):
                    return
                act.wait_ge(h_biased, j + 1)
                act.activation(h_sb[:, par, :], h_sb[:, par, :], ACT.Relu).then_inc(h_relu, 1)

            def relu_y(j):
                act.wait_ge(y_biased, j + 1)
                act.activation(y_sb[:, 0, :], y_sb[:, 0, :], ACT.Relu).then_inc(y_relu, 1)

            def pick_x(j, par):
                if beyond(j):
                    return
                if not before(j, 2):
                    act.wait_ge(xt_ready, j - 1)
                act.activation(x_idx[:, par:par + 1], slot_tok[:, bass.ds(j, 1)], ACT.Copy).then_inc(idx_ready, 1)

            def gate_y(j, par):
                act.wait_ge(y_done, j + 1)
                act.activation(y_sb[:, 1 + par, :], y_sb[:, 1 + par, :], ACT.Copy,
                               scale=slot_gate[:, bass.ds(j, 1)]).then_inc(y_gated, 1)
                if not before(j, 2):
                    act.wait_ge(y_added, 16 * (j - 1))
                act.activation(y_idx[:, par:par + 1], slot_dst[:, bass.ds(j, 1)], ACT.Copy).then_inc(y_gated, 1)

            act.wait_ge(slots_ready, 3)
            pick_x(0, 0)
            pick_x(1, 1)
            evac_x(0, 0)
            pick_x(2, 0)
            evac_x(1, 1)
            pick_x(3, 1)
            evac_x(2, 0)
            relu_h(0, 0)
            relu_h(1, 1)

            def step(j, par=None):
                par = j % 2 if par is None else par
                if not before(j, 2):
                    gate_y(j - 2, par)
                pick_x(j + 4, par)
                if not before(j, 1):
                    relu_y(j - 1)
                evac_x(j + 3, 1 - par)
                relu_h(j + 2, par)

            tiles(act, step)
            gate_y(SLOT_TILES - 2, (SLOT_TILES - 2) % 2)
            relu_y(SLOT_TILES - 1)
            gate_y(SLOT_TILES - 1, (SLOT_TILES - 1) % 2)

        def experts_vector(dve):
            n = [0]

            def chain(ins):
                n[0] += 1
                ins.then_inc(route, 1)
                dve.wait_ge(route, n[0])

            def over_e(t):
                return t.unsqueeze(2).to_broadcast((P, TT, E))

            def over_t(t):
                return t.unsqueeze(1).to_broadcast((P, TT, E))

            dve.wait_ge(r_evac, B)
            dve.wait_ge(xn2_stored, 16 * B)
            dve.wait_ge(x1_stored, 16 * B)
            dve.wait_ge(iota_step, 6)
            chain(dve.tensor_tensor(ra[:, :, :], logits[:, :, :], over_t(b_r[:, :]), ALU.add))
            chain(dve.tensor_reduce(best[:, :], ra[:, :, :], AX.X, ALU.max))
            chain(dve.tensor_tensor(ra[:, :, :], ra[:, :, :], over_e(best[:, :]), ALU.subtract))
            dve.tensor_copy(rank[:, :], rank_i[:, :]).then_inc(route, 1)
            dve.tensor_copy(step_f[:, :], step_i[:, :]).then_inc(route, 1)
            dve.tensor_copy(lane_f[:, :], lane_i[:, :]).then_inc(route, 1)
            dve.tensor_copy(token_f[:, :], token_i[:, :]).then_inc(route, 1)
            dve.tensor_copy(spare_f[:, :], spare_i[:, :]).then_inc(route, 1)
            n[0] += 5
            chain(dve.tensor_copy(slot_f[:, :], slot_i[:, :]))
            dve.wait_ge(route_exp, 1)
            chain(dve.tensor_reduce(den[:, :], rb[:, :, :], AX.X, ALU.add))
            chain(dve.reciprocal(den[:, :], den[:, :]))
            chain(dve.tensor_tensor(rb[:, :, :], rb[:, :, :], over_e(den[:, :]), ALU.mult))
            for top, one in ((top1, one1), (top2, one2)):
                chain(dve.tensor_reduce(top[:, :], rb[:, :, :], AX.X, ALU.max))
                chain(dve.tensor_tensor(rc[:, :, :], rb[:, :, :], over_e(top[:, :]), ALU.is_equal))
                chain(dve.tensor_tensor(rc[:, :, :], rc[:, :, :], over_t(rank[:, :]), ALU.mult))
                chain(dve.tensor_reduce(best[:, :], rc[:, :, :], AX.X, ALU.max))
                chain(dve.tensor_tensor(one[:, :, :], rc[:, :, :], over_e(best[:, :]), ALU.is_equal))
                if one is one1:
                    chain(dve.scalar_tensor_tensor(rb[:, :, :], one1[:, :, :], -2.0, rb[:, :, :], ALU.mult, ALU.add))
            dve.tensor_tensor(oh[:, :, :], one1[:, :, :], one2[:, :, :], ALU.add).then_inc(oh_ready, 1)
            chain(dve.tensor_tensor(den[:, :], top1[:, :], top2[:, :], ALU.add))
            chain(dve.reciprocal(den[:, :], den[:, :]))
            for k, top in enumerate((top1, top2)):
                chain(dve.tensor_tensor(top[:, :], top[:, :], den[:, :], ALU.mult))
                chain(dve.tensor_scalar(w_top[:, k, :], top[:, :], gf_tanh[:, 0:1], None, ALU.mult))
            dve.wait_ge(counted, 2)
            chain(dve.tensor_copy(base_a[:, :, :], ps_m[:, 0:TT * E].rearrange("p (t e) -> p t e", e=E)))
            chain(dve.tensor_copy(rc[:, :, :], base_a[:, :, :]))
            a, b_, reach = base_a, base_b, 1
            while reach < TT:
                dve.tensor_copy(b_[:, 0:reach, :], a[:, 0:reach, :]).then_inc(route, 1)
                n[0] += 1
                chain(dve.tensor_tensor(b_[:, reach:TT, :], a[:, reach:TT, :], a[:, 0:TT - reach, :], ALU.add))
                a, b_, reach = b_, a, 2 * reach
            chain(dve.tensor_copy(count_e[:, :], a[:, TT - 1, :]))
            chain(dve.tensor_tensor(b_[:, :, :], a[:, :, :], rc[:, :, :], ALU.subtract))
            chain(dve.tensor_tensor(more[:, :, :], count_e[:, :].unsqueeze(2).to_broadcast((P, E, TT)),
                                    step_f[:, :].unsqueeze(1).to_broadcast((P, E, TT)), ALU.is_gt))
            chain(dve.tensor_reduce(tiles_e[:, :], more[:, :, :], AX.X, ALU.add))
            chain(dve.memset(start_a[:, 0:1], 0.0))
            chain(dve.tensor_copy(start_a[:, 1:E], tiles_e[:, 0:E - 1]))
            c, d, reach = start_a, start_b, 1
            while reach < E:
                dve.tensor_copy(d[:, 0:reach], c[:, 0:reach]).then_inc(route, 1)
                n[0] += 1
                chain(dve.tensor_tensor(d[:, reach:E], c[:, reach:E], c[:, 0:E - reach], ALU.add))
                c, d, reach = d, c, 2 * reach
            chain(dve.scalar_tensor_tensor(b_[:, :, :], over_t(c[:, :]), float(P), b_[:, :, :], ALU.mult, ALU.add))
            chain(dve.tensor_tensor(b_[:, :, :], b_[:, :, :], ps_o[:, 0:TT * E].rearrange("p (t e) -> p t e", e=E), ALU.add))
            for k, one in enumerate((one1, one2)):
                chain(dve.tensor_tensor(rc[:, :, :], one[:, :, :], b_[:, :, :], ALU.mult))
                chain(dve.tensor_reduce(pos_f[:, k, :], rc[:, :, :], AX.X, ALU.add))
            chain(dve.tensor_copy(pos[:, :, :], pos_f[:, :, :]))
            dve.tensor_scalar(low_i[:, :, :], pos[:, :, :], P - 1, None, ALU.bitwise_and).then_inc(route, 1)
            dve.tensor_scalar(high_i[:, :, :], pos[:, :, :], 7, None, ALU.logical_shift_right).then_inc(route, 1)
            n[0] += 2
            dve.wait_ge(route, n[0])
            dve.tensor_copy(low_f[:, :, :], low_i[:, :, :]).then_inc(route, 1)
            dve.tensor_copy(high_f[:, :, :], high_i[:, :, :]).then_inc(route, 1)
            n[0] += 2
            dve.wait_ge(route, n[0])
            for b in range(B):
                t0, par = b * QT, b % 2
                if b >= 2:
                    dve.wait_ge(valued, 2 * (b - 1))
                    dve.wait_ge(weighed, QT * (b - 1))
                dve.tensor_tensor(in_tile[:, par], slot_f[:, :].unsqueeze(1).unsqueeze(2).to_broadcast((P, TOP, QT, SLOT_TILES)),
                                  high_f[:, :, t0:t0 + QT].unsqueeze(3).to_broadcast((P, TOP, QT, SLOT_TILES)),
                                  ALU.is_equal).then_inc(found, 1)
                if b >= 2:
                    dve.wait_ge(turned, b - 1)
                dve.tensor_tensor(is_lane[:, par], lane_f[:, :].unsqueeze(1).unsqueeze(2).to_broadcast((P, TOP, QT, P)),
                                  low_f[:, :, t0:t0 + QT].unsqueeze(3).to_broadcast((P, TOP, QT, P)),
                                  ALU.is_equal).then_inc(found, 1)
            chain(dve.tensor_tensor(owner[0:1, :, 1:E], slot_f[0:1, :].unsqueeze(2).to_broadcast((1, SLOT_TILES, E - 1)),
                                    c[0:1, 1:E].unsqueeze(1).to_broadcast((1, SLOT_TILES, E - 1)), ALU.is_ge))
            chain(dve.tensor_reduce(owner_f[0:1, :], owner[0:1, :, 1:E], AX.X, ALU.add))
            dve.tensor_copy(owner_i[:, :], owner_f[0:1, :]).then_inc(routed, 1)
            dve.wait_ge(turned, B)
            dve.tensor_scalar(slot_tok[:, :], ps_t[:, 0, 0:SLOT_TILES], 1.0, 0.0, ALU.subtract, ALU.max).then_inc(slots_ready, 1)
            dve.tensor_copy(slot_gate[:, :], ps_t[:, 0, SLOT_TILES:2 * SLOT_TILES]).then_inc(slots_ready, 1)
            chain(dve.tensor_scalar(no_token[:, :], ps_t[:, 0, 0:SLOT_TILES], 0.0, spare_f[:, 0:1], ALU.is_equal, ALU.mult))
            dve.scalar_tensor_tensor(slot_dst[:, :], ps_t[:, 0, 0:SLOT_TILES], -1.0, no_token[:, :],
                                     ALU.add, ALU.add).then_inc(slots_ready, 1)
            dve.wait_ge(routed, 1)
            dve.wait_ge(experts_loaded, 16 * (2 * E + 1))

            def bias_h(j, par):
                if beyond(j):
                    return
                e = expert_of(dve, j)
                dve.wait_ge(h_ready, j + 1)
                if not before(j, 2):
                    dve.wait_ge(ht_ready, j - 1)
                dve.tensor_tensor(h_sb[:, par, :].rearrange("p (n f) -> p n f", n=2), ps_h[par],
                                  b1_bc[:, e, :].rearrange("p (n f) -> p n f", n=2), ALU.add).then_inc(h_biased, 1)

            def stats_h(j, par):
                if beyond(j):
                    return
                hold(dve, h_relu, j + 1)
                for i in range(2):
                    dve.bn_stats(h_stat[:, i, :], h_sb[:, par, i * 512:(i + 1) * 512]).then_inc(h_stats, 1)
                hold(dve, h_stats, 2 * (j + 1))
                dve.bn_aggr(h_mv[:, par, :], h_stat[:, :, :]).then_inc(h_agg, 1)

            def norm_h(j, par):
                if beyond(j):
                    return
                dve.wait_ge(h_pow, 2 * (j + 1))
                dve.tensor_scalar(h_sb[:, par, :], h_sb[:, par, :], h_mv[:, par, 0:1], h_rstd[:, par:par + 1],
                                  ALU.subtract, ALU.mult).then_inc(h_normed, 1)

            def scale_ht(j):
                e = expert_of(dve, j)
                dve.wait_ge(ht_ready, j + 1)
                if not before(j, 1):
                    dve.wait_ge(y_ready, j)
                for i in range(2):
                    dve.tensor_tensor(ht_sb[:, i * HC:(i + 1) * HC, :], ps_ht[:, i, :].rearrange("p (c t) -> p c t", t=P),
                                      g1_t[:, 0, bass.ds(e * FC + i * HC, HC)].unsqueeze(2).to_broadcast((P, HC, P)),
                                      ALU.mult).then_inc(ht_scaled, 1)

            def bias_y(j):
                e = expert_of(dve, j)
                dve.wait_ge(y_ready, j + 1)
                if before(j, 1):
                    dve.wait_ge(bc_loaded, 16)
                else:
                    dve.wait_ge(y_scaled, j)
                dve.tensor_tensor(y_sb[:, 0, :], ps_y, b2_bc[:, e, :], ALU.add).then_inc(y_biased, 1)

            def stats_y(j):
                hold(dve, y_relu, j + 1)
                dve.bn_stats(y_stat[:, :], y_sb[:, 0, :]).then_inc(y_stats, 1)
                hold(dve, y_stats, j + 1)
                dve.bn_aggr(y_mv[:, :], y_stat[:, :]).then_inc(y_agg, 1)

            def norm_y(j):
                dve.wait_ge(y_pow, 2 * (j + 1))
                dve.tensor_scalar(y_sb[:, 0, :], y_sb[:, 0, :], y_mv[:, 0:1], y_rstd[:, 0:1],
                                  ALU.subtract, ALU.mult).then_inc(y_normed, 1)

            bias_h(0, 0)
            stats_h(0, 0)
            bias_h(1, 1)
            norm_h(0, 0)
            stats_h(1, 1)

            def step(j, par=None):
                par = j % 2 if par is None else par
                after = not (before(j, 1))
                scale_ht(j)
                if after:
                    bias_y(j - 1)
                norm_h(j + 1, 1 - par)
                bias_h(j + 2, par)
                if after:
                    stats_y(j - 1)
                stats_h(j + 2, par)
                if after:
                    norm_y(j - 1)

            tiles(dve, step)
            bias_y(SLOT_TILES - 1)
            stats_y(SLOT_TILES - 1)
            norm_y(SLOT_TILES - 1)

        def experts_gpsimd(pool):
            pool.wait_ge(xn2_stored, 16 * B)
            pool.wait_ge(x1_stored, 16 * B)
            pool.wait_ge(spare_stored, 16)
            pool.wait_ge(r_ready, B)
            pool.iota(rank_i[:, :], pattern=[[-1, E]], base=E, channel_multiplier=0).then_inc(iota_step, 1)
            pool.iota(step_i[:, :], pattern=[[P, TT]], base=0, channel_multiplier=0).then_inc(iota_step, 1)
            pool.iota(slot_i[:, :], pattern=[[1, SLOT_TILES]], base=0, channel_multiplier=0).then_inc(iota_step, 1)
            pool.iota(lane_i[:, :], pattern=[[1, P]], base=0, channel_multiplier=0).then_inc(iota_step, 1)
            pool.iota(spare_i[:, :], pattern=[[1, 1]], base=TOKENS + 1, channel_multiplier=1).then_inc(iota_step, 1)
            pool.iota(token_i[:, :], pattern=[[P, TT]], base=1, channel_multiplier=1).then_inc(iota_step, 1)
            for b in range(B):
                pool.wait_ge(found, 2 * b + 1)
                if b >= 2:
                    pool.wait_ge(turned, b - 1)
                t0, par = b * QT, b % 2
                pool.tensor_tensor(slot_of[:, par, :, :, 0, :], in_tile[:, par],
                                   token_f[:, t0:t0 + QT].unsqueeze(1).unsqueeze(3).to_broadcast((P, TOP, QT, SLOT_TILES)),
                                   ALU.mult).then_inc(valued, 1)
                pool.tensor_tensor(slot_of[:, par, 1, :, 1, :], in_tile[:, par, 1],
                                   w_top[:, 1, t0:t0 + QT].unsqueeze(2).to_broadcast((P, QT, SLOT_TILES)),
                                   ALU.mult).then_inc(valued, 1)

            def gather_x(j, par):
                if beyond(j):
                    return
                hold(pool, idx_ready, j + 1)
                pool.indirect_dma_start(out=x_sb[:, par, :], out_offset=None, in_=xn2_d,
                                        in_offset=bass.IndirectOffsetOnAxis(ap=x_idx[:, par:par + 1], axis=0)
                                        ).then_inc(x_got[par], 16)

            for j in range(4):
                gather_x(j, j % 2)

            def pow_h(j, par):
                if beyond(j):
                    return
                hold(pool, h_agg, j + 1)
                pool.tensor_scalar(h_rstd[:, par:par + 1], h_mv[:, par, 1:2], EPS, None, ALU.add).then_inc(h_pow, 1)
                pool.wait_ge(h_pow, 2 * j + 1)
                pool.tensor_tensor(h_rstd[:, par:par + 1], h_rstd[:, par:par + 1], minus_half[:, 0:1], ALU.pow).then_inc(h_pow, 1)

            def shift_ht(j):
                e = expert_of(pool, j)
                for i in range(2):
                    pool.wait_ge(ht_scaled, 2 * j + i + 1)
                    h = ht_sb[:, i * HC:(i + 1) * HC, :]
                    pool.tensor_tensor(h, h, g1_t[:, 1, bass.ds(e * FC + i * HC, HC)].unsqueeze(2).to_broadcast((P, HC, P)),
                                       ALU.add).then_inc(ht_done, 1)

            def pow_y(j):
                hold(pool, y_agg, j + 1)
                pool.tensor_scalar(y_rstd[:, :], y_mv[:, 1:2], EPS, None, ALU.add).then_inc(y_pow, 1)
                pool.wait_ge(y_pow, 2 * j + 1)
                pool.tensor_tensor(y_rstd[:, :], y_rstd[:, :], minus_half[:, 0:1], ALU.pow).then_inc(y_pow, 1)

            def scale_y(j, par):
                e = expert_of(pool, j)
                if before(j, 1):
                    pool.wait_ge(bc_loaded, 48)
                pool.wait_ge(y_normed, j + 1)
                if not before(j, 2):
                    pool.wait_ge(y_added, 16 * (j - 1))
                y = y_sb[:, 1 + par, :]
                pool.tensor_tensor(y, y_sb[:, 0, :], g2_bc[:, e, :], ALU.mult).then_inc(y_scaled, 1)
                pool.wait_ge(y_scaled, j + 1)
                pool.tensor_tensor(y, y, be2_bc[:, e, :], ALU.add).then_inc(y_done, 1)

            def add_y(j, par):
                hold(pool, y_gated, 2 * (j + 1))
                if not before(j, 1):
                    hold(pool, y_added, 16 * j)
                pool.indirect_dma_start(out=acc_d, out_offset=bass.IndirectOffsetOnAxis(ap=y_idx[:, par:par + 1], axis=0),
                                        in_=y_sb[:, 1 + par, :], in_offset=None, compute_op=ALU.add).then_inc(y_added, 16)

            pow_h(0, 0)
            pow_h(1, 1)

            def step(j, par=None):
                par = j % 2 if par is None else par
                after = not (before(j, 1))
                shift_ht(j)
                gather_x(j + 4, par)
                if not before(j, 2):
                    add_y(j - 2, par)
                if after:
                    pow_y(j - 1)
                pow_h(j + 2, par)
                if after:
                    scale_y(j - 1, 1 - par)

            tiles(pool, step)
            pow_y(SLOT_TILES - 1)
            add_y(SLOT_TILES - 2, (SLOT_TILES - 2) % 2)
            scale_y(SLOT_TILES - 1, (SLOT_TILES - 1) % 2)
            add_y(SLOT_TILES - 1, (SLOT_TILES - 1) % 2)

        hold_reg = {}

        def hold(eng, semaphore, count):
            if isinstance(count, int):
                eng.wait_ge(semaphore, count)
            else:
                if eng.engine not in hold_reg:
                    hold_reg[eng.engine] = eng.alloc_register(f"hold_{len(hold_reg)}")
                eng.reg_mov(hold_reg[eng.engine], count)
                eng.wait_ge(const_ready, CONSTS)
                eng.wait_ge(semaphore, hold_reg[eng.engine])

        def split3(eng, dst, src, tmp, step, at):
            none = zero[0:src.shape[0], 0:1].to_broadcast(src.shape)

            def rounded(out, x):
                return eng.tensor_copy(out, x) if eng is nc.vector else eng.tensor_tensor(out, x, none, ALU.add)

            rounded(dst[0], src).then_inc(step, 1)
            hold(eng, step, at + 1)
            eng.tensor_tensor(tmp, src, dst[0], ALU.subtract).then_inc(step, 1)
            hold(eng, step, at + 2)
            rounded(dst[1], tmp).then_inc(step, 1)
            hold(eng, step, at + 3)
            eng.tensor_tensor(dst[2], tmp, dst[1], ALU.subtract).then_inc(step, 1)

        def bank(kind, b, i):
            if not before(b, 1):
                return ps_m[:, :]
            return ps_s[:, i % 2, :] if kind == "V" else ps_t[:, i % 4, :]

        block = ctx.enter_context(nc.Block())

        @block.sync
        def _(sp):
            def load_x(b):
                sp.dma_start(x_in[:, :, :], x_v[b]).then_inc(x_loaded, 16)
                sp.dma_start(c_in[:, :, :], c_v[b]).then_inc(c_loaded, 16)

            def store_parts(b, i):
                sp.wait_ge(qk_split, 4 * (6 * b + i + 1))
                if i < 2:
                    dst = q_parts[b, :, i * P:(i + 1) * P, :]
                else:
                    c, h = divmod(i - 2, 2)
                    dst = k_parts[b, :, c * P:(c + 1) * P, h * S:(h + 1) * S]
                sp.dma_start(dst.rearrange("j p t -> p j t"), proj_parts[:, i % 2, :, :]).then_inc(parts_stored[i % 2], 16)

            def load_stack(b, g):
                for r in range(len(Q_PART)):
                    h0 = g * GH * HD
                    src = q_parts[b, Q_PART[r], h0:h0 + GH * HD, :].rearrange("(h d) t -> d h t", d=HD)
                    sp.dma_start(q_stack[r * HD:(r + 1) * HD, g, :, :], src).then_inc(stack_loaded[g], 16)
                    src = k_parts[b, K_PART[r], h0:h0 + GH * HD, :].rearrange("(h d) t -> d h t", d=HD)
                    sp.dma_start(k_stack[r * HD:(r + 1) * HD, g, :, :], src).then_inc(stack_loaded[g], 16)
                src = mask_parts[:, b, :].unsqueeze(1).to_broadcast((PARTS, GH, KEYS))
                sp.dma_start(k_stack[R_MASK:R_MAX, g, :, :], src).then_inc(stack_loaded[g], 16)

            def load_max(b, g):
                sp.wait_ge(m_split, 4 * (G * b + g + 1))
                for j in range(PARTS):
                    sp.dma_start(q_stack[R_MAX + j:R_MAX + j + 1, g, :, :].rearrange("o h (t q) -> o (h t) q", q=P),
                                 m_parts[:, j, :]).then_inc(max_loaded[g], 16)

            def batch(b, first=False, last=False):
                if not first:
                    sp.wait_ge(st_ready, 2 * KT * (G * b))
                    load_stack(b, 3)
                load_max(b, 1)
                if last:
                    sp.wait_ge(v_ready, 4 * B)
                    for half in range(2):
                        sp.wait_ge(parts_stored[half], 16 * 3 * B)
                    load_w2(3); load_w2(4)
                if not last:
                    sp.wait_ge(t_ready, 4 * (b + 2))
                    load_next(b + 2)
                    for i in range(5):
                        store_parts(b + 1, i)
                    sp.wait_ge(parts_stored[0], 16 * (3 * (b + 1) + 2))
                    sp.wait_ge(parts_stored[1], 16 * (3 * (b + 1) + 2))
                    sp.wait_ge(st_ready, 2 * KT * (G * b + 1))
                    load_stack(b + 1, 0)
                load_max(b, 2)
                if last:
                    load_w2(5); load_w2(6)
                if not last:
                    store_parts(b + 1, 5)
                if not first:
                    store_x1(b - 1)
                sp.dma_start(x_res[:, :, :], x_v[b]).then_inc(res_loaded, 16)
                if not last:
                    for half in range(2):
                        sp.wait_ge(parts_stored[half], 16 * 3 * (b + 2))
                if last:
                    sp.wait_ge(v_copied, G * B)
                    load_w2(2)
                    sp.wait_ge(st_ready, 2 * KT * (G * b + 1))
                    load_w1(2)
                load_max(b, 3)
                if last:
                    sp.wait_ge(st_ready, 2 * KT * (G * b + 2))
                    load_w1(3); load_w1(0)
                    sp.wait_ge(pv_done, KT * (G * b + 2))
                    load_w2(0)
                    sp.wait_ge(max_loaded[3], 16 * PARTS * B)
                    load_w2(7)
                    sp.wait_ge(st_ready, 2 * KT * (G * b + 3))
                    load_w1(4)
                if not last:
                    sp.wait_ge(st_ready, 2 * KT * (G * b + 2))
                    load_stack(b + 1, 1)
                    load_max(b + 1, 0)
                    sp.wait_ge(st_ready, 2 * KT * (G * b + 3))
                    load_stack(b + 1, 2)

            def store_x1(b):
                sp.wait_ge(x1_added, G * (b + 1))
                sp.dma_start(x1_v[b], x_res[:, :, :]).then_inc(x1_stored, 16)
                sp.wait_ge(x1_normed, QT * (b + 1))
                sp.dma_start(xn2_v[b], xn2[:, :, :]).then_inc(xn2_stored, 16)
                sp.wait_ge(x1_stored, 16 * (b + 1))

            def load_next(b):
                if isinstance(b, int) and b >= B:
                    return
                load_x(b)

            sp.dma_start(mk[:, :], mask.rearrange("b o n (k c) -> (b o n k) c", c=P)).then_inc(mask_loaded, 16)
            load_x(0)
            for w, t in ((Wq, wq), (Wk, wk), (Wv, wv)):
                sp.dma_start(t[:, :, :], w.rearrange("(c p) n -> p c n", p=P)).then_inc(w_loaded, 16)
            sp.dma_start(b_q[:, :], bq.rearrange("(c p) -> p c", p=P), allow_slow_non_contiguous=True).then_inc(w_loaded, 16)
            sp.dma_start(b_k[:, :], bk.rearrange("(c p) -> p c", p=P), allow_slow_non_contiguous=True).then_inc(w_loaded, 16)
            sp.dma_start(b_v[:, :], bv.partition_broadcast(P)).then_inc(w_loaded, 16)
            sp.dma_start(g_raw[:, :], g_xattn.partition_broadcast(P)).then_inc(w_loaded, 16)
            sp.dma_start(wr[:, :, :], Wr.rearrange("(c p) e -> p c e", p=P)).then_inc(w_loaded, 16)
            sp.dma_start(b_r[:, :], br.partition_broadcast(P)).then_inc(w_loaded, 16)
            sp.dma_start(gf_raw[:, :], g_ffn.partition_broadcast(P)).then_inc(w_loaded, 16)
            sp.dma_start(gb_rows[:, 0, :], g1.rearrange("e (c p) -> (e c) p", p=P)).then_inc(gb_loaded, 16)
            sp.dma_start(gb_rows[:, 1, :], be1.rearrange("e (c p) -> (e c) p", p=P)).then_inc(gb_loaded, 16)
            sp.wait_ge(mask_step, 4)
            sp.dma_start(mask_parts.rearrange("j b (k c) -> (b k) j c", c=P), mk_parts[:, :, :]).then_inc(mask_stored, 16)
            sp.wait_ge(t_ready, 4)
            load_x(1)
            for i in range(5):
                store_parts(0, i)
            for half in range(2):
                sp.wait_ge(parts_stored[half], 16 * 2)
            sp.wait_ge(mask_stored, 16)
            sp.wait_ge(q_ones_set, 1)
            sp.wait_ge(k_ones_set, 1)
            load_stack(0, 0)
            store_parts(0, 5)
            for half in range(2):
                sp.wait_ge(parts_stored[half], 16 * 3)
            for g in range(1, G):
                load_stack(0, g)
            load_max(0, 0)
            sp.dma_start(acc_d[TOKENS:TOKENS + P, :], x[0, 0:P, :]).then_inc(spare_stored, 16)
            sp.dma_start(b1_bc[:, :, :], b1.partition_broadcast(P)).then_inc(experts_loaded, 16)
            batch(0, first=True)
            with sp.Fori(1, B - 2) as b:
                batch(b)
            batch(B - 2)
            batch(B - 1, last=True)
            store_x1(B - 1)
            experts_sync(sp)

        @block.tensor
        def _(pe):
            EVAC = {"T": t_evac, "Q": qk_evac, "V": v_evac, "M": m_evac, "O": o_evac, "L": l_evac, "R": r_evac, "S": s_used}
            prev = [None]

            def spare_free():
                if prev[0] is not None:
                    kind, n = prev[0]
                    pe.wait_ge(EVAC[kind], n + 1)

            def use_T(b, i):
                src = x_in if i < 2 else c_in
                if i == 0:
                    pe.wait_ge(x_normed, QT * (b + 1))
                if i == 2:
                    pe.wait_ge(c_loaded, 16 * (b + 1))
                for t in range(QT):
                    mm = pe.transpose(bank("T", b, i)[:, t * P:(t + 1) * P], src[:, t, (i % 2) * P:(i % 2 + 1) * P], ident[:, :])
                mm.then_inc(t_ready, 1)

            def use_Q(b, i):
                pe.wait_ge(t_evac, 4 * b + 4 if i > 1 else 4 * b + 2)
                c, h = (i, 0) if i < 2 else divmod(i - 2, 2)
                w = wq if i < 2 else wk
                if isinstance(b, int) and b == 0 and i >= 4:
                    pe.wait_ge(qk_evac, i - 3)
                for k in range(DC):
                    mm = pe.matmul(bank("Q", b, i), w[:, k, c * P:(c + 1) * P], all_t[:, k, h * S:(h + 1) * S],
                                   start=(k == 0), stop=(k == DC - 1))
                mm.then_inc(qk_ready, 1)

            def use_V(b, i):
                if isinstance(b, int) and b == 0 and i >= 2:
                    pe.wait_ge(v_evac, i - 1)
                for n in range(2):
                    for k in range(DC):
                        kt = 2 * i + n
                        mm = pe.matmul(bank("V", b, i)[:, n * D:(n + 1) * D], all_t[:, k, kt * P:(kt + 1) * P], wv[:, k, :],
                                       start=(k == 0), stop=(k == DC - 1))
                mm.then_inc(v_ready, 1)

            def use_M(u):
                pe.wait_ge(m_reduced, u + 1)
                pe.transpose(ps_m[0:GH * QT, 0:P], m_row[:, :], ident[:, :]).then_inc(m_ready, 1)

            def use_O(u):
                pe.wait_ge(o_copied, u + 1)
                for t in range(QT):
                    mm = pe.transpose(ps_m[:, t * P:(t + 1) * P], o_sb[:, t * P:(t + 1) * P], ident[:, :])
                mm.then_inc(o_ready, 1)

            def use_L(b, i):
                if i == 0:
                    pe.wait_ge(x1_normed, QT * (b + 1))
                for t in range(QT):
                    mm = pe.transpose(ps_m[:, t * P:(t + 1) * P], xn2[:, t, i * P:(i + 1) * P], ident[:, :])
                mm.then_inc(l_ready, 1)

            def use_R(b):
                for t in range(QT):
                    for k in range(DC):
                        mm = pe.matmul(ps_m[:, t * E:(t + 1) * E], xn2_t[:, k, t * P:(t + 1) * P], wr[:, k, :],
                                       start=(k == 0), stop=(k == DC - 1))
                mm.then_inc(r_ready, 1)

            def spare(use, b, u):
                spare_free()
                kind, i = use[0], int(use[1:] or 0)
                if kind == "T":
                    use_T(b + 1, i); n = 4 * (b + 1) + i
                elif kind == "Q":
                    use_Q(b + 1, i); n = 6 * (b + 1) + i
                elif kind == "V":
                    use_V(b + 1, i); n = 4 * (b + 1) + i
                elif kind == "M":
                    use_M(u + 1); n = u + 1
                elif kind == "L":
                    use_L(b - 1, i); n = 2 * (b - 1) + i
                elif kind == "R":
                    use_R(b - 1); n = b - 1
                else:
                    use_O(u - 1); n = u - 1
                prev[0] = (kind, n)

            def scores_max(w, g, i, bank=None, back=2):
                h, t, half = i // 8, i // 2 % QT, i % 2
                n = 32 * w + i
                if bank is None and not before(n, 2):
                    pe.wait_ge(s_used, n + 1 - back)
                pe.matmul(ps_s[:, i % 2, :] if bank is None else bank, q_stack[0:R_MAX, g, h, t * P:(t + 1) * P],
                          k_stack[0:R_MAX, g, h, half * S:(half + 1) * S], start=True, stop=True).then_inc(s_ready, 1)

            def scores_t(b, g, k, pair):
                n = KT * (G * b + g) + k
                if k == 0 and pair == 0:
                    pe.wait_ge(max_loaded[g], 16 * PARTS * (b + 1))
                if not before(n, 1):
                    pe.wait_ge(exp_done, 2 * n - 1 + pair)
                for h in (2 * pair, 2 * pair + 1):
                    mm = pe.matmul(ps_t[:, h, :], k_stack[0:ROWS, g, h, k * P:(k + 1) * P], q_stack[0:ROWS, g, h, :],
                                   start=True, stop=True)
                mm.then_inc(st_ready, 1)

            def probs_v(b, g, k):
                u = G * b + g
                pe.wait_ge(exp_done, 2 * (KT * u + k) + 2)
                if k == 0:
                    pe.wait_ge(v_copied, u + 1)
                    if not before(u, 1):
                        pe.wait_ge(o_copied, u)
                for h in range(GH):
                    mm = pe.matmul(ps_o[32 * h:32 * h + 32, :], v_ring[:, g, k, h, :], probs[:, k % 2, h, :],
                                   start=(k == 0), stop=(k == KT - 1))
                mm.then_inc(pv_done, 1)

            def batch(b, first=False, last=False):
                for step in range(G * KT):
                    g, k = divmod(step, KT)
                    slot = (g + 2) % G

                    def ahead(i):
                        if last and g >= 2:
                            return
                        if k == 0 and i == 0:
                            pe.wait_ge(stack_loaded[slot], 16 * LOADS * (b + 1 + (g + 2) // G))
                        w = G * b + g + 2
                        if i == 3 and third_bank(step, first, last):
                            spare_free()
                            scores_max(w, slot, 4 * k + i, bank=ps_m[:, :])
                            prev[0] = ("S", 32 * w + 4 * k + i)
                        else:
                            skip = i == 1 and not (first and step == 0) and third_bank((step - 1) % 32, first, last)
                            scores_max(w, slot, 4 * k + i, back=4 if skip else 2)

                    ahead(0)
                    scores_t(b, g, k, 0)
                    ahead(1)
                    uses = list(plan(step, first, last))
                    scores_t(b, g, k, 1)
                    for use in uses[0:1]:
                        spare(use, b, G * b + g)
                    ahead(2)
                    ahead(3)
                    if step:
                        probs_v(b, (step - 1) // KT, (step - 1) % KT)
                    elif not first:
                        probs_v(b - 1, G - 1, KT - 1)
                    for use in uses[1:]:
                        spare(use, b, G * b + g)

            pe.wait_ge(const_ready, CONSTS)
            pe.wait_ge(w_loaded, 16 * 10)
            for i in range(4):
                use_T(0, i)
            for i in range(6):
                use_Q(0, i)
            for i in range(4):
                use_V(0, i)
            pe.wait_ge(v_evac, 4)
            pe.wait_ge(gb_loaded, 32)
            for i in range(2):
                mm = pe.transpose(ps_o[:, i * 64:(i + 1) * 64], gb_rows[:, i, :], ident[0:64, 0:64])
            mm.then_inc(gb_ready, 1)
            for w in range(2):
                pe.wait_ge(stack_loaded[w], 16 * LOADS)
                for i in range(32):
                    scores_max(w, w, i)
                if w == 0:
                    spare("M", 0, -1)
            pe.wait_ge(v_ones_set, 1)
            batch(0, first=True)
            with pe.Fori(1, B - 2) as b:
                prev[0] = ("S", 32 * (G * b + 1) + 31)
                batch(b)
            prev[0] = ("S", 32 * (G * (B - 2) + 1) + 31)
            batch(B - 2)
            batch(B - 1, last=True)
            probs_v(B - 1, G - 1, KT - 1)
            for use in ("O", "L0", "L1", "R"):
                spare(use, B, UNITS)
            experts_tensor(pe)

        @block.scalar
        def _(act):
            def evac_T(b, i):
                act.wait_ge(t_ready, 4 * b + i + 1)
                o = S * (i // 2)
                act.activation(all_t[:, i % 2, o:o + S], bank("T", b, i), ACT.Copy).then_inc(t_evac, 1)

            def evac_Q(b, i):
                act.wait_ge(qk_ready, 6 * b + i + 1)
                if not (isinstance(b, int) and b == 0 and i < 2):
                    act.wait_ge(qk_split, 4 * (6 * b + i - 1))
                bias = b_qs[:, i:i + 1] if i < 2 else b_k[:, (i - 2) // 2:(i - 2) // 2 + 1]
                act.activation(proj[:, i % 2, :], bank("Q", b, i), ACT.Identity, bias=bias,
                               scale=HD ** -0.5 if i < 2 else 1.0).then_inc(qk_evac, 1)

            def evac_V(b, i):
                act.wait_ge(v_ready, 4 * b + i + 1)
                if i == 0 and not before(b, 1):
                    act.wait_ge(v_copied, G * b)
                act.activation(v_all[:, 2 * i:2 * i + 2, :], bank("V", b, i).rearrange("p (n d) -> p n d", d=D),
                               ACT.Copy, scale=g_tanh[:, 0:1]).then_inc(v_evac, 1)

            def evac_L(b, i):
                act.wait_ge(l_ready, 2 * b + i + 1)
                if i == 0 and not before(b, 1):
                    act.wait_ge(r_ready, b)
                act.activation(xn2_t[:, i, :], ps_m[:, :], ACT.Copy).then_inc(l_evac, 1)

            def copy_O(u):
                act.wait_ge(pv_done, KT * (u + 1))
                if not before(u, 1):
                    act.wait_ge(o_ready, u)
                act.activation(o_sb[:, :], ps_o[:, :], ACT.Copy).then_inc(o_copied, 1)

            def exp(b, g, k, pair):
                n = KT * (G * b + g) + k
                act.wait_ge(st_ready, 2 * n + pair + 1)
                if pair == 0 and not before(n, 2):
                    act.wait_ge(pv_done, n - 1)
                act.activation(probs[:, k % 2, 2 * pair:2 * pair + 2, :], ps_t[:, 2 * pair:2 * pair + 2, :],
                               ACT.Exp).then_inc(exp_done, 1)

            def batch(b, first=False, last=False):
                for step in range(G * KT):
                    g, k = divmod(step, KT)
                    exp(b, g, k, 0)
                    exp(b, g, k, 1)
                    for use in plan(step, first, last):
                        if use[0] == "T":
                            evac_T(b + 1, int(use[1]))
                        if use[0] == "Q":
                            evac_Q(b + 1, int(use[1]))
                        if use[0] == "V":
                            evac_V(b + 1, int(use[1]))
                        if use[0] == "L":
                            evac_L(b - 1, int(use[1]))
                    if k == 0 and not (first and g == 0):
                        copy_O(G * b + g - 1)

            act.wait_ge(w_loaded, 16 * 10)
            act.activation(b_qs[:, :], b_q[:, :], ACT.Copy, scale=HD ** -0.5).then_inc(bq_scaled, 1)
            act.activation(g_tanh[:, :], g_raw[:, :], ACT.Tanh).then_inc(g_ready, 1)
            act.activation(gf_tanh[:, :], gf_raw[:, :], ACT.Tanh).then_inc(g_ready, 1)
            act.wait_ge(bq_scaled, 1)
            act.wait_ge(g_ready, 2)
            for i in range(4):
                evac_T(0, i)
            for i in range(6):
                evac_Q(0, i)
            for i in range(4):
                evac_V(0, i)
            batch(0, first=True)
            with act.Fori(1, B - 2) as b:
                batch(b)
            batch(B - 2)
            batch(B - 1, last=True)
            copy_O(UNITS - 1)
            evac_L(B - 1, 0)
            evac_L(B - 1, 1)
            experts_scalar(act)

        @block.vector
        def _(dve):
            def stats_x(b, tiles=range(QT)):
                dve.wait_ge(x_loaded, 16 * (b + 1))
                for t in tiles:
                    dve.bn_stats(stat1[:, t, :], x_in[:, t, :]).then_inc(stats1, 1)

            def means_x(b):
                hold(dve, stats1, QT * (b + 1))
                if not before(b, 1):
                    hold(dve, x_normed, QT * b)
                for t in range(QT):
                    dve.bn_aggr(mv1[:, t, :], stat1[:, t, :]).then_inc(agg1, 1)

            def norm_x(b, tiles=range(QT)):
                dve.wait_ge(rstd1_step, 2 * b + 2)
                for t in tiles:
                    dve.tensor_scalar(x_in[:, t, :], x_in[:, t, :], mv1[:, t, 0:1], rstd1[:, t:t + 1],
                                      ALU.subtract, ALU.mult).then_inc(x_normed, 1)

            def stats_x1(b, tiles=range(QT)):
                dve.wait_ge(x1_added, G * (b + 1))
                for t in tiles:
                    dve.bn_stats(stat2[:, t, :], x_res[:, t, :]).then_inc(stats2, 1)

            def means_x1(b):
                hold(dve, stats2, QT * (b + 1))
                if not before(b, 1):
                    hold(dve, x1_normed, QT * b)
                for t in range(QT):
                    dve.bn_aggr(mv2[:, t, :], stat2[:, t, :]).then_inc(agg2, 1)

            def norm_x1(b, tiles=range(QT)):
                if tiles[0] == 0:
                    dve.wait_ge(rstd2_step, 2 * b + 2)
                if tiles[0] == 0 and not before(b, 1):
                    hold(dve, xn2_stored, 16 * b)
                    hold(dve, l_ready, 2 * b)
                for t in tiles:
                    dve.tensor_scalar(xn2[:, t, :], x_res[:, t, :], mv2[:, t, 0:1], rstd2[:, t:t + 1],
                                      ALU.subtract, ALU.mult).then_inc(x1_normed, 1)

            def evac_R(b):
                dve.wait_ge(r_ready, b + 1)
                dve.tensor_copy(logits[:, bass.ds(b * QT, QT), :],
                                ps_m[:, 0:QT * E].rearrange("p (t e) -> p t e", e=E)).then_inc(r_evac, 1)

            def reduce_max(w, par, i, bank=None):
                n = 32 * w + i
                if i == 0 and not before(w, 2):
                    dve.wait_ge(m_reduced, w - 1)
                dve.wait_ge(s_ready, n + 1)
                dve.tensor_reduce(m_half[:, par, i:i + 1], ps_s[:, i % 2, :] if bank is None else bank, AX.X, ALU.max).then_inc(s_used, 1)

            def join_max(u, par):
                dve.wait_ge(s_used, 32 * (u + 1))
                if not before(u, 1):
                    dve.wait_ge(m_ready, u)
                dve.tensor_reduce(m_row[:, :], m_half[:, par, :].rearrange("p (n h) -> p n h", h=2), AX.X,
                                  ALU.max).then_inc(m_reduced, 1)

            def evac_M(u):
                dve.wait_ge(m_ready, u + 1)
                if not before(u, 1):
                    dve.wait_ge(m_split, 4 * u)
                dve.tensor_scalar(m_neg[:, :], ps_m[0:GH * QT, 0:P], -1.0, None, ALU.mult).then_inc(m_evac, 1)

            def evac_O(u):
                dve.wait_ge(o_ready, u + 1)
                o = ps_m[:, :].rearrange("p (t h d) -> p t h d", t=QT, h=GH)
                dve.reciprocal(r_sum[:, :, :], o[:, :, :, HD]).then_inc(o_recip, 1)
                dve.wait_ge(o_recip, u + 1)
                if not before(u, 1):
                    dve.wait_ge(x1_added, u)
                dve.tensor_tensor(ctx_n[:, :, :].rearrange("p t (h d) -> p t h d", d=HD), o[:, :, :, 0:HD],
                                  r_sum[:, :, :].unsqueeze(3).to_broadcast((P, QT, GH, HD)),
                                  ALU.mult).then_inc(o_evac, 1)

            def ahead(u, g, k, i, first, last):
                if not (last and g >= 2):
                    third = i == 2 and third_bank(g * KT + k, first, last)
                    reduce_max(u + 2, g % 2, 4 * k + i)
                    reduce_max(u + 2, g % 2, 4 * k + i + 1, bank=ps_m[:, :] if third else None)

            HALF = (range(0, QT // 2), range(QT // 2, QT))

            def batch(b, first=False, last=False, stats=True):
                for step in range(G * KT):
                    g, k = divmod(step, KT)
                    u = G * b + g
                    if k == 0 and not (last and g == 3):
                        join_max(u + 1, (g + 1) % 2)
                    ahead(u, g, k, 0, first, last)
                    for use in plan(step, first, last):
                        if use == "M":
                            evac_M(u + 1)
                        if use == "O":
                            evac_O(u - 1)
                        if use == "R":
                            evac_R(b - 1)
                    ahead(u, g, k, 2, first, last)
                    if not first:
                        if step in (5, 6):
                            stats_x1(b - 1, HALF[step - 5])
                        if step == 7:
                            means_x1(b - 1)
                        if step in (11, 12):
                            norm_x1(b - 1, HALF[step - 11])
                    if stats and not last:
                        if step in (11, 12):
                            stats_x(b + 2, HALF[step - 11])
                        if step == 13:
                            means_x(b + 2)
                        if step in (19, 20):
                            norm_x(b + 2, HALF[step - 19])

            dve.memset(q_stack[R_MASK:P, :, :, :].bitcast(F32), TWO_ONES).then_inc(q_ones_set, 1)
            stats_x(0)
            means_x(0)
            norm_x(0)
            dve.wait_ge(w_loaded, 16 * 10)
            dve.wait_ge(g_ready, 2)
            dve.tensor_scalar(b_v[:, :], b_v[:, :], g_tanh[:, 0:1], None, ALU.mult).then_inc(bv_scaled, 1)
            for i in range(6):
                dve.wait_ge(qk_evac, i + 1)
                if i >= 2:
                    dve.wait_ge(parts_stored[i % 2], 16 * (i // 2))
                split3(nc.vector, [proj_parts[:, i % 2, j, :] for j in range(PARTS)], proj[:, i % 2, :], rest[:, i % 2, :],
                       qk_split, 4 * i)
            dve.memset(v_ring[:, :, :, :, HD:32], 1.0).then_inc(v_ones_set, 1)
            dve.wait_ge(gb_ready, 1)
            dve.tensor_copy(g1_t[:, :, :], ps_o[:, 0:P].rearrange("p (i n) -> p i n", i=2)).then_inc(gb_evac, 1)
            stats_x(1)
            means_x(1)
            norm_x(1)
            for w in range(2):
                for i in range(32):
                    reduce_max(w, w, i)
                if w == 0:
                    join_max(0, 0)
                    evac_M(0)
            batch(0, first=True)
            with dve.Fori(1, B - 2) as b:
                batch(b)
            batch(B - 2, stats=False)
            batch(B - 1, last=True)
            evac_O(UNITS - 1)
            stats_x1(B - 1)
            means_x1(B - 1)
            norm_x1(B - 1)
            evac_R(B - 1)
            experts_vector(dve)

        @block.gpsimd
        def _(pool):
            def rstd_x(b):
                hold(pool, agg1, QT * (b + 1))
                pool.tensor_scalar(rstd1[:, :], mv1[:, :, 1], EPS, None, ALU.add).then_inc(rstd1_step, 1)
                hold(pool, rstd1_step, 2 * b + 1)
                pool.tensor_tensor(rstd1[:, :], rstd1[:, :], minus_half[:, :], ALU.pow).then_inc(rstd1_step, 1)

            def split_Q(b, i):
                n = 6 * b + i
                hold(pool, qk_evac, n + 1)
                if not before(n, 2):
                    hold(pool, parts_stored[i % 2], 16 * (3 * b + i // 2))
                split3(pool, [proj_parts[:, i % 2, j, :] for j in range(PARTS)], proj[:, i % 2, :], rest[:, i % 2, :],
                       qk_split, 4 * n)

            def split_M(u, last_slot, loads):
                hold(pool, m_evac, u + 1)
                if not before(u, 1):
                    hold(pool, max_loaded[last_slot], 16 * PARTS * loads)
                split3(pool, [m_parts[:, j, :] for j in range(PARTS)], m_neg[:, :], m_rest[:, :], m_split, 4 * u)

            def copy_V(b, g):
                hold(pool, v_evac, 4 * (b + 1))
                if not before(b, 1):
                    hold(pool, pv_done, KT * (G * (b - 1) + g + 1))
                v = v_all[:, :, g * GH * HD:(g + 1) * GH * HD].rearrange("p k (h d) -> p k h d", d=HD)
                pool.tensor_tensor(v_ring[:, g, :, :, 0:HD], v,
                                   zero[:, 0:1].unsqueeze(2).unsqueeze(3).to_broadcast((P, KT, GH, HD)), ALU.add).then_inc(v_copied, 1)

            def add_x(b, g):
                if g == 0:
                    pool.wait_ge(res_loaded, 16 * (b + 1))
                    pool.tensor_tensor(x_res[:, :, :], x_res[:, :, :], b_v[:, :].unsqueeze(1).to_broadcast((P, QT, D)),
                                       ALU.add).then_inc(res_biased, 1)
                    pool.wait_ge(res_biased, b + 1)
                pool.wait_ge(o_evac, G * b + g + 1)
                o = g * GH * HD
                pool.tensor_tensor(x_res[:, :, o:o + GH * HD], x_res[:, :, o:o + GH * HD], ctx_n[:, :, :],
                                   ALU.add).then_inc(x1_added, 1)

            def rstd_x1(b):
                hold(pool, agg2, QT * (b + 1))
                pool.tensor_scalar(rstd2[:, :], mv2[:, :, 1], EPS, None, ALU.add).then_inc(rstd2_step, 1)
                pool.wait_ge(rstd2_step, 2 * b + 1)
                pool.tensor_tensor(rstd2[:, :], rstd2[:, :], minus_half[:, :], ALU.pow).then_inc(rstd2_step, 1)

            def batch(b, first=False, last=False, norm=True):
                for step in range(G * KT):
                    g, k = divmod(step, KT)
                    u = G * b + g
                    if step == 4 and not first:
                        copy_V(b, 3)
                    if step == 20 and not last:
                        copy_V(b + 1, 0)
                        copy_V(b + 1, 1)
                    if step == 28 and not last:
                        copy_V(b + 1, 2)
                    for use in plan(step, first, last):
                        if use == "M":
                            split_M(u + 1, g, b + 1)
                        if use == "O":
                            if g == 0:
                                add_x(b - 1, 3)
                            else:
                                add_x(b, g - 1)
                        if use[0] == "Q":
                            split_Q(b + 1, int(use[1]))
                    if step == 7 and not first:
                        rstd_x1(b - 1)
                    if step == 15 and norm and not last:
                        rstd_x(b + 2)

            pool.memset(ones[:, :], 1.0).then_inc(ones_ready, 1)
            pool.wait_ge(ones_ready, 1)
            pool.affine_select(out=tri[:, :], in_=ones[:, :], compare_op=ALU.is_gt, fill=0.0, base=0,
                               pattern=[[1, P]], channel_multiplier=-1).then_inc(const_ready, 1)
            pool.memset(minus_half[:, :], -0.5).then_inc(const_ready, 1)
            pool.memset(zero[:, :], 0.0).then_inc(const_ready, 1)
            pool.memset(ident[:, :], 0.0).then_inc(ident_zero, 1)
            hold(pool, ident_zero, 1)
            pool.affine_select(out=ident[:, :], in_=ident[:, :], compare_op=ALU.not_equal, fill=1.0, base=0,
                               pattern=[[-1, P]], channel_multiplier=1).then_inc(const_ready, 1)
            pool.wait_ge(const_ready, CONSTS)
            hold(pool, mask_loaded, 16)
            pool.tensor_copy(mk_parts[:, 0, :], mk[:, :]).then_inc(mask_step, 1)
            hold(pool, mask_step, 1)
            pool.tensor_tensor(mk_rest[:, :], mk[:, :], mk_parts[:, 0, :], ALU.subtract).then_inc(mask_step, 1)
            hold(pool, mask_step, 2)
            pool.tensor_copy(mk_parts[:, 1, :], mk_rest[:, :]).then_inc(mask_step, 1)
            pool.wait_ge(mask_step, 3)
            pool.tensor_tensor(mk_parts[:, 2, :], mk_rest[:, :], mk_parts[:, 1, :], ALU.subtract).then_inc(mask_step, 1)
            rstd_x(0)
            pool.wait_ge(rstd1_step, 2)
            pool.memset(k_stack[R_MASK:P, :, :, :].bitcast(F32), TWO_ONES).then_inc(k_ones_set, 1)
            pool.wait_ge(k_ones_set, 1)
            rstd_x(1)
            pool.wait_ge(bv_scaled, 1)
            for g in range(4):
                copy_V(0, g)
            split_M(0, None, None)
            batch(0, first=True)
            with pool.Fori(1, B - 2) as b:
                batch(b)
            batch(B - 2, norm=False)
            batch(B - 1, last=True)
            add_x(B - 1, 3)
            rstd_x1(B - 1)
            experts_gpsimd(pool)


_INS = ['x', 'ctx_1024', 'mask_Bx1x1x4096_ff0', 'g_xattn', 'g_ffn', 'L0_xattn_Wq', 'L0_xattn_bq', 'L0_xattn_Wk',
        'L0_xattn_bk', 'L0_xattn_Wv', 'L0_xattn_bv', 'L0_ffn_Wr', 'L0_ffn_br', 'L0_ffn_W1', 'L0_ffn_b1', 'L0_ffn_g1',
        'L0_ffn_be1', 'L0_ffn_W2', 'L0_ffn_b2', 'L0_ffn_g2', 'L0_ffn_be2']
_OUTS = [((8, 512, 256), 'float32')]


def kernel(**inputs):
    import numpy as _np
    import concourse.bacc as _bacc
    from concourse import mybir as _mybir
    from concourse.bass_utils import run_bass_kernel_spmd as _run

    nc = _bacc.Bacc("TRN2", target_bir_lowering=False, num_devices=1)
    arrays, args = {}, []
    for name in _INS:
        a = _np.ascontiguousarray(inputs[name])
        arrays[f"in_{name}_dram"] = a
        args.append(nc.dram_tensor(f"in_{name}_dram", a.shape, _mybir.dt.from_np(a.dtype), kind="ExternalInput").ap())
    for i, (shape, dtype) in enumerate(_OUTS):
        dt = _mybir.dt.from_np(_np.dtype(dtype))
        args.append(nc.dram_tensor(f"out_{i}_dram", shape, dt, kind="ExternalOutput").ap())
    flamingo_kernel(nc, *args)
    r = _run(nc, [arrays], core_ids=[0])
    return r.results[0]["out_0_dram"]
```
